# Optimizing a Trainium2 kernel written in Bass

```python
import numpy as np
import jax
import jax.numpy as jnp

def _softmax(x, axis=-1):
    return jax.nn.softmax(x, axis=axis)

def _gelu(x):
    return jax.nn.gelu(x, approximate=True)

def _silu(x):
    return jax.nn.silu(x)

def _sigmoid(x):
    return jax.nn.sigmoid(x)

def _layernorm(x, axis=-1, eps=1e-05):
    m = jnp.mean(x, axis=axis, keepdims=True)
    v = jnp.var(x, axis=axis, keepdims=True)
    return (x - m) / jnp.sqrt(v + eps)

def _scatter_add(tgt, idx, src, axis=0):
    return tgt.at[idx].add(src)

def _segment_sum(src, seg, n):
    return jax.ops.segment_sum(src, seg, n)
kernel_name = 'mk_decoder_preln_d2_seqx_r4_d7efea'

def setup_inputs(seed: int=0):
    np.random.seed(seed)
    _w = jnp.asarray

    def _rec_inputs():
        import jax
        import jax.numpy as jnp
        _rk = jax.random.key(seed)
        x = -1.394e-06 + 0.9999 * jax.random.normal(jax.random.fold_in(_rk, 1), (16, 128, 256), jnp.float32)
        _lenS = 128 - jax.random.randint(jax.random.fold_in(_rk, 7), (16,), 0, max(1, 128 // 4) + 1, jnp.int32)
        _lenS2 = 128 - jax.random.randint(jax.random.fold_in(_rk, 8), (16,), 0, max(1, 128 // 4) + 1, jnp.int32)
        _ctx_1024P = jax.random.normal(jax.random.fold_in(_rk, 11), (16, 16, 256), jnp.float32)
        _ctx_1024c = jax.random.dirichlet(jax.random.fold_in(_rk, 511), 0.3 * jnp.ones((16,), jnp.float32), (16, 128))
        _ctx_1024t = jnp.einsum('bsk,bkd->bsd', _ctx_1024c, _ctx_1024P)
        _ctx_1024t = _ctx_1024t * jax.lax.rsqrt(jnp.mean(jnp.square(_ctx_1024t)) + 1e-12) * 0.953939
        ctx_1024 = -0.000292821 + 1.00034 * (_ctx_1024t + 0.3 * jax.random.normal(jax.random.fold_in(_rk, 611), (16, 128, 256), jnp.float32))
        fside_BxSxS2_0 = -1.47943e-05 + 1.00017 * jax.random.normal(jax.random.fold_in(_rk, 12), (16, 128, 128), jnp.float32)
        return (x, ctx_1024, fside_BxSxS2_0)
    x, ctx_1024, fside_BxSxS2_0 = _rec_inputs()

    def _L0_attn_setup():
        import jax, jax.numpy as jnp
        import numpy as np
        D_STATE = 16

        def _silu(v):
            return v * jax.nn.sigmoid(v)
        key = jax.random.key(seed)
        ks = jax.random.split(key, 7)
        B, L, d_model = (2, 1024, 256)
        d_inner, d_conv, d_state = (512, 4, D_STATE)
        s = 0.02
        return {'x': jax.random.normal(ks[0], (B, L, d_model), jnp.float32), 'W_in': jax.random.normal(ks[1], (2 * d_inner, d_model), jnp.float32) * s, 'conv_w': jax.random.normal(ks[2], (d_inner, d_conv), jnp.float32) * 0.3, 'conv_b': jax.random.normal(ks[3], (d_inner,), jnp.float32) * 0.1, 'W_xproj': jax.random.normal(ks[4], (2 * d_state + d_inner, d_inner), jnp.float32) * s, 'D': jnp.ones((d_inner,), jnp.float32), 'W_out': jax.random.normal(ks[5], (d_model, d_inner), jnp.float32) * s}
    _L0_attn_all = _L0_attn_setup()
    _L0_attn_in = {k: v for k, v in _L0_attn_all.items() if k in ('W_in', 'conv_w', 'conv_b', 'W_xproj', 'D', 'W_out')}
    del _L0_attn_all

    def _L0_xattn_setup():
        import jax, jax.numpy as jnp
        import numpy as np
        N_HEADS = 16
        D_EMBED = 256
        D_HEAD = D_EMBED // N_HEADS
        B, S = (2, 512)
        key = jax.random.key(seed)
        ks = jax.random.split(key, 6)
        k = jax.random.normal(ks[0], (B, S, D_EMBED), dtype=jnp.float32)
        q = jax.random.normal(ks[1], (B, S, D_EMBED), dtype=jnp.float32)
        v = jax.random.normal(ks[2], (B, S, D_EMBED), dtype=jnp.float32)
        scale = 1.0 / np.sqrt(D_HEAD)
        Wk = jax.random.normal(ks[3], (D_HEAD, D_HEAD), dtype=jnp.float32) * scale
        Wq = jax.random.normal(ks[4], (D_HEAD, D_HEAD), dtype=jnp.float32) * scale
        Wv = jax.random.normal(ks[5], (D_HEAD, D_HEAD), dtype=jnp.float32) * scale
        return {'k': k, 'q': q, 'v': v, 'Wk': Wk, 'Wq': Wq, 'Wv': Wv}
    _L0_xattn_all = _L0_xattn_setup()
    _L0_xattn_in = {k: v for k, v in _L0_xattn_all.items() if k in ('Wk', 'Wq', 'Wv')}
    del _L0_xattn_all

    def _L0_ffn_setup():
        import jax, jax.numpy as jnp
        import numpy as np
        import math
        E = 32
        K = 2
        CF = 1.2
        D = 256
        F = 1024
        key = jax.random.key(seed)
        ks = jax.random.split(key, 7)
        s = 0.02
        return {'x': jax.random.normal(ks[0], (4, 512, D), jnp.float32), 'gate_w': jax.random.normal(ks[1], (D, E), jnp.float32) * s, 'gate_b': jnp.zeros((E,), jnp.float32), 'w1': jax.random.normal(ks[2], (E, D, F), jnp.float32) * s, 'b1': jnp.zeros((E, F), jnp.float32), 'w2': jax.random.normal(ks[3], (E, F, D), jnp.float32) * s, 'b2': jnp.zeros((E, D), jnp.float32)}
    _L0_ffn_all = _L0_ffn_setup()
    _L0_ffn_in = {k: v for k, v in _L0_ffn_all.items() if k in ('gate_w', 'gate_b', 'w1', 'b1', 'w2', 'b2')}
    del _L0_ffn_all

    def _L1_attn_setup():
        import jax, jax.numpy as jnp
        import numpy as np
        import math
        DIM = 256
        HEADS = 16
        B, N = (2, 512)
        POLY = jnp.array([-0.037, 0.481, -2.3, 4.917, -1.791], dtype=jnp.float32)

        def adaptive_temperature_softmax(logits):
            original_probs = jax.nn.softmax(logits, axis=-1)
            entropy = jnp.sum(-original_probs * jnp.log(original_probs + 1e-09), axis=-1, keepdims=True)
            e2 = entropy * entropy
            poly_result = POLY[0] * e2 * e2 + POLY[1] * e2 * entropy + POLY[2] * e2 + POLY[3] * entropy + POLY[4]
            beta = jnp.where(entropy > 0.5, jnp.maximum(poly_result, 1.0), 1.0)
            return jax.nn.softmax(logits * beta, axis=-1)
        key = jax.random.key(seed)
        ks = jax.random.split(key, 5)
        s = 1.0 / math.sqrt(DIM)
        return {'x': jax.random.normal(ks[0], (B, N, DIM), dtype=jnp.float32), 'Wq': jax.random.normal(ks[1], (DIM, DIM), dtype=jnp.float32) * s, 'Wk': jax.random.normal(ks[2], (DIM, DIM), dtype=jnp.float32) * s, 'Wv': jax.random.normal(ks[3], (DIM, DIM), dtype=jnp.float32) * s, 'Wo': jax.random.normal(ks[4], (DIM, DIM), dtype=jnp.float32) * s, 'bo': jnp.zeros((DIM,), dtype=jnp.float32)}
    _L1_attn_all = _L1_attn_setup()
    _L1_attn_in = {k: v for k, v in _L1_attn_all.items() if k in ('Wq', 'Wk', 'Wv', 'Wo', 'bo')}
    del _L1_attn_all

    def _L1_xattn_setup():
        import jax, jax.numpy as jnp
        import numpy as np
        D = 256
        key = jax.random.key(seed)
        ks = jax.random.split(key, 13)
        B, S, d = (4, 512, D)
        inp = {'q_in': jax.random.normal(ks[0], (B, S, d), jnp.float32), 'k_in': jax.random.normal(ks[1], (B, S, d), jnp.float32), 'v_in': jax.random.normal(ks[2], (B, S, d), jnp.float32), 'phi_risk': jax.random.normal(ks[3], (B, S, S), jnp.float32), 'phi_prio': jax.random.normal(ks[4], (B, S, S), jnp.float32), 'phi_impl': jax.random.normal(ks[5], (B, S, S), jnp.float32), 'Wq': jax.random.normal(ks[6], (d, d), jnp.float32) / np.sqrt(d), 'bq': jax.random.normal(ks[7], (d,), jnp.float32) * 0.01, 'Wk': jax.random.normal(ks[8], (d, d), jnp.float32) / np.sqrt(d), 'bk': jax.random.normal(ks[9], (d,), jnp.float32) * 0.01, 'Wv': jax.random.normal(ks[10], (d, d), jnp.float32) / np.sqrt(d), 'bv': jax.random.normal(ks[11], (d,), jnp.float32) * 0.01, 'beta_risk': jnp.float32(0.1), 'beta_prio': jnp.float32(0.1), 'beta_impl': jnp.float32(0.1)}
        return inp
    _L1_xattn_all = _L1_xattn_setup()
    _L1_xattn_in = {k: v for k, v in _L1_xattn_all.items() if k in ('Wq', 'bq', 'Wk', 'bk', 'Wv', 'bv', 'beta_risk', 'beta_prio', 'beta_impl')}
    del _L1_xattn_all

    def _L1_ffn_setup():
        import jax, jax.numpy as jnp
        import numpy as np
        HID = 256
        NH = 16
        NKV = 4
        HD = HID // NH
        E = 8
        TOPK = 2
        FFN = 512
        EPS = 1e-05
        THETA = 10000.0

        def _rmsnorm(x, w):
            var = jnp.mean(x * x, axis=-1, keepdims=True)
            return x * jax.lax.rsqrt(var + EPS) * w

        def _rope_tables(S):
            inv_freq = 1.0 / THETA ** (jnp.arange(0, HD, 2, dtype=jnp.float32) / HD)
            freqs = jnp.arange(S, dtype=jnp.float32)[:, None] * inv_freq[None, :]
            emb = jnp.concatenate([freqs, freqs], axis=-1)
            return (jnp.cos(emb), jnp.sin(emb))

        def _apply_rope(t, cos, sin):
            t1, t2 = jnp.split(t, 2, axis=-1)
            rot = jnp.concatenate([-t2, t1], axis=-1)
            return t * cos[None, :, None, :] + rot * sin[None, :, None, :]
        key = jax.random.key(seed)
        ks = jax.random.split(key, 6)
        B, S = (1, 512)
        x = jax.random.normal(ks[0], (B, S, HID), dtype=jnp.float32)
        wqkv = jax.random.normal(ks[1], ((NH + 2 * NKV) * HD, HID), dtype=jnp.float32) * 0.02
        wo = jax.random.normal(ks[2], (HID, NH * HD), dtype=jnp.float32) * 0.02
        gate_w = jax.random.normal(ks[3], (E, HID), dtype=jnp.float32) * 0.02
        w13 = jax.random.normal(ks[4], (E, 2 * FFN, HID), dtype=jnp.float32) * 0.02
        w2 = jax.random.normal(ks[5], (E, HID, FFN), dtype=jnp.float32) * 0.02
        return {'x': x, 'ln1_w': jnp.ones((HID,), jnp.float32), 'ln2_w': jnp.ones((HID,), jnp.float32), 'wqkv': wqkv, 'wo': wo, 'gate_w': gate_w, 'w13': w13, 'w2': w2}
    _L1_ffn_all = _L1_ffn_setup()
    _L1_ffn_in = {k: v for k, v in _L1_ffn_all.items() if k in ('ln1_w', 'ln2_w', 'wqkv', 'wo', 'gate_w', 'w13', 'w2')}
    del _L1_ffn_all
    return {'x': x, 'ctx_1024': ctx_1024, 'fside_BxSxS2_0': fside_BxSxS2_0, 'L0_attn_W_in': _L0_attn_in['W_in'], 'L0_attn_conv_w': _L0_attn_in['conv_w'], 'L0_attn_conv_b': _L0_attn_in['conv_b'], 'L0_attn_W_xproj': _L0_attn_in['W_xproj'], 'L0_attn_D': _L0_attn_in['D'], 'L0_attn_W_out': _L0_attn_in['W_out'], 'L0_xattn_Wk': _L0_xattn_in['Wk'], 'L0_xattn_Wq': _L0_xattn_in['Wq'], 'L0_xattn_Wv': _L0_xattn_in['Wv'], 'L0_ffn_gate_w': _L0_ffn_in['gate_w'], 'L0_ffn_gate_b': _L0_ffn_in['gate_b'], 'L0_ffn_w1': _L0_ffn_in['w1'], 'L0_ffn_b1': _L0_ffn_in['b1'], 'L0_ffn_w2': _L0_ffn_in['w2'], 'L0_ffn_b2': _L0_ffn_in['b2'], 'L1_attn_Wq': _L1_attn_in['Wq'], 'L1_attn_Wk': _L1_attn_in['Wk'], 'L1_attn_Wv': _L1_attn_in['Wv'], 'L1_attn_Wo': _L1_attn_in['Wo'], 'L1_attn_bo': _L1_attn_in['bo'], 'L1_xattn_Wq': _L1_xattn_in['Wq'], 'L1_xattn_bq': _L1_xattn_in['bq'], 'L1_xattn_Wk': _L1_xattn_in['Wk'], 'L1_xattn_bk': _L1_xattn_in['bk'], 'L1_xattn_Wv': _L1_xattn_in['Wv'], 'L1_xattn_bv': _L1_xattn_in['bv'], 'L1_xattn_beta_risk': _L1_xattn_in['beta_risk'], 'L1_xattn_beta_prio': _L1_xattn_in['beta_prio'], 'L1_xattn_beta_impl': _L1_xattn_in['beta_impl'], 'L1_ffn_ln1_w': _L1_ffn_in['ln1_w'], 'L1_ffn_ln2_w': _L1_ffn_in['ln2_w'], 'L1_ffn_wqkv': _L1_ffn_in['wqkv'], 'L1_ffn_wo': _L1_ffn_in['wo'], 'L1_ffn_gate_w': _L1_ffn_in['gate_w'], 'L1_ffn_w13': _L1_ffn_in['w13'], 'L1_ffn_w2': _L1_ffn_in['w2']}

def reference(x, ctx_1024, fside_BxSxS2_0, L0_attn_W_in, L0_attn_conv_w, L0_attn_conv_b, L0_attn_W_xproj, L0_attn_D, L0_attn_W_out, L0_xattn_Wk, L0_xattn_Wq, L0_xattn_Wv, L0_ffn_gate_w, L0_ffn_gate_b, L0_ffn_w1, L0_ffn_b1, L0_ffn_w2, L0_ffn_b2, L1_attn_Wq, L1_attn_Wk, L1_attn_Wv, L1_attn_Wo, L1_attn_bo, L1_xattn_Wq, L1_xattn_bq, L1_xattn_Wk, L1_xattn_bk, L1_xattn_Wv, L1_xattn_bv, L1_xattn_beta_risk, L1_xattn_beta_prio, L1_xattn_beta_impl, L1_ffn_ln1_w, L1_ffn_ln2_w, L1_ffn_wqkv, L1_ffn_wo, L1_ffn_gate_w, L1_ffn_w13, L1_ffn_w2):
    import jax
    import jax.numpy as jnp

    def _L0_attn_ref(x, W_in, conv_w, conv_b, W_xproj, D, W_out):
        import jax, jax.numpy as jnp
        import numpy as np
        D_STATE = 16

        def _silu(v):
            return v * jax.nn.sigmoid(v)
        Bsz, L, _ = x.shape
        d_inner, d_conv = conv_w.shape
        d_state = D_STATE
        xz = jnp.einsum('bld,ed->ble', x, W_in)
        xb, z = (xz[..., :d_inner], xz[..., d_inner:])
        xpad = jnp.pad(xb, ((0, 0), (d_conv - 1, 0), (0, 0)))
        xc = conv_b
        for k in range(d_conv):
            xc = xc + conv_w[:, k] * xpad[:, k:k + L, :]
        xc = _silu(xc)
        proj = jnp.einsum('bld,ed->ble', xc, W_xproj)
        Bm = proj[..., :d_state]
        Cm = proj[..., d_state:2 * d_state]
        delta = jax.nn.softplus(proj[..., 2 * d_state:])
        bc = jnp.einsum('bls,bls->bl', Bm, Cm)
        y = delta * xc * bc[..., None] + D * xc
        y = y * _silu(z)
        return jnp.einsum('bld,ed->ble', y, W_out)

    def _L0_xattn_ref(k, q, v, Wk, Wq, Wv):
        import jax, jax.numpy as jnp
        import numpy as np
        N_HEADS = 16
        D_EMBED = 256
        D_HEAD = D_EMBED // N_HEADS
        B, S = (2, 512)
        b, s, _ = k.shape
        kh = k.reshape(b, s, N_HEADS, D_HEAD)
        qh = q.reshape(b, s, N_HEADS, D_HEAD)
        vh = v.reshape(b, s, N_HEADS, D_HEAD)
        kh = jnp.einsum('bshd,ed->bshe', kh, Wk)
        qh = jnp.einsum('bshd,ed->bshe', qh, Wq)
        vh = jnp.einsum('bshd,ed->bshe', vh, Wv)
        scores = jnp.einsum('bqhd,bkhd->bhqk', qh, kh) / np.sqrt(D_HEAD).astype(np.float32)
        attn = jax.nn.softmax(scores, axis=-1)
        out = jnp.einsum('bhqk,bkhd->bqhd', attn, vh)
        return out.reshape(b, s, D_EMBED)

    def _L0_ffn_ref(x, gate_w, gate_b, w1, b1, w2, b2):
        import jax, jax.numpy as jnp
        import numpy as np
        import math
        E = 32
        K = 2
        CF = 1.2
        D = 256
        F = 1024
        orig_shape = x.shape
        xt = x.reshape(-1, D)
        T = xt.shape[0]
        C = int(math.ceil(T * K / E * CF))
        logits = xt @ gate_w + gate_b
        probs = jax.nn.softmax(logits, axis=-1)
        top_w, top_i = jax.lax.top_k(probs, K)
        w = top_w / jnp.sum(top_w, axis=-1, keepdims=True)
        flat_e = top_i.reshape(-1)
        oh = jax.nn.one_hot(flat_e, E, dtype=jnp.int32)
        pos_all = jnp.cumsum(oh, axis=0) - 1
        pos = jnp.take_along_axis(pos_all, flat_e[:, None], axis=1)[:, 0]
        valid = pos < C
        pos_d = jnp.where(valid, pos, C)
        x_rep = jnp.repeat(xt, K, axis=0)
        xe = jnp.zeros((E, C, D), x.dtype).at[flat_e, pos_d].add(x_rep, mode='drop')
        he = jax.nn.gelu(jnp.einsum('ecd,edf->ecf', xe, w1) + b1[:, None, :], approximate=False)
        ye = jnp.einsum('ecf,efd->ecd', he, w2) + b2[:, None, :]
        y_flat = ye[flat_e, jnp.minimum(pos, C - 1)] * valid[:, None].astype(x.dtype)
        y = (y_flat.reshape(T, K, D) * w[..., None]).sum(axis=1)
        return y.reshape(orig_shape)

    def _L1_attn_ref(x, Wq, Wk, Wv, Wo, bo):
        import jax, jax.numpy as jnp
        import numpy as np
        import math
        DIM = 256
        HEADS = 16
        B, N = (2, 512)
        POLY = jnp.array([-0.037, 0.481, -2.3, 4.917, -1.791], dtype=jnp.float32)

        def adaptive_temperature_softmax(logits):
            original_probs = jax.nn.softmax(logits, axis=-1)
            entropy = jnp.sum(-original_probs * jnp.log(original_probs + 1e-09), axis=-1, keepdims=True)
            e2 = entropy * entropy
            poly_result = POLY[0] * e2 * e2 + POLY[1] * e2 * entropy + POLY[2] * e2 + POLY[3] * entropy + POLY[4]
            beta = jnp.where(entropy > 0.5, jnp.maximum(poly_result, 1.0), 1.0)
            return jax.nn.softmax(logits * beta, axis=-1)
        b, n, d = x.shape
        h = HEADS
        hd = d // h

        def proj(W):
            t = x @ W.T
            return t.reshape(b, n, h, hd).transpose(0, 2, 1, 3)
        q, k, v = (proj(Wq), proj(Wk), proj(Wv))
        sim = jnp.einsum('bhid,bhjd->bhij', q, k) / math.sqrt(hd)
        neg = -jnp.finfo(sim.dtype).max
        causal = jnp.triu(jnp.ones((n, n), dtype=bool), k=1)
        sim = jnp.where(causal, neg, sim)
        attn = adaptive_temperature_softmax(sim)
        out = jnp.einsum('bhij,bhjd->bhid', attn, v)
        out = out.transpose(0, 2, 1, 3).reshape(b, n, d)
        return out @ Wo.T + bo

    def _L1_xattn_ref(q_in, k_in, v_in, phi_risk, phi_prio, phi_impl, Wq, bq, Wk, bk, Wv, bv, beta_risk, beta_prio, beta_impl):
        import jax, jax.numpy as jnp
        import numpy as np
        D = 256
        d = q_in.shape[-1]
        scale = jnp.asarray(d, q_in.dtype) ** (-0.5)
        Q = q_in @ Wq.T + bq
        K = k_in @ Wk.T + bk
        V = v_in @ Wv.T + bv
        att = jnp.einsum('bsd,btd->bst', Q, K) * scale
        att = att + beta_risk * phi_risk + beta_prio * phi_prio - beta_impl * phi_impl
        w = jax.nn.softmax(att, axis=-1)
        return jnp.einsum('bst,btd->bsd', w, V)

    def _L1_ffn_ref(x, ln1_w, ln2_w, wqkv, wo, gate_w, w13, w2):
        import jax, jax.numpy as jnp
        import numpy as np
        HID = 256
        NH = 16
        NKV = 4
        HD = HID // NH
        E = 8
        TOPK = 2
        FFN = 512
        EPS = 1e-05
        THETA = 10000.0

        def _rmsnorm(x, w):
            var = jnp.mean(x * x, axis=-1, keepdims=True)
            return x * jax.lax.rsqrt(var + EPS) * w

        def _rope_tables(S):
            inv_freq = 1.0 / THETA ** (jnp.arange(0, HD, 2, dtype=jnp.float32) / HD)
            freqs = jnp.arange(S, dtype=jnp.float32)[:, None] * inv_freq[None, :]
            emb = jnp.concatenate([freqs, freqs], axis=-1)
            return (jnp.cos(emb), jnp.sin(emb))

        def _apply_rope(t, cos, sin):
            t1, t2 = jnp.split(t, 2, axis=-1)
            rot = jnp.concatenate([-t2, t1], axis=-1)
            return t * cos[None, :, None, :] + rot * sin[None, :, None, :]
        B, S, _ = x.shape
        h = _rmsnorm(x, ln1_w)
        qkv = jnp.einsum('bsh,oh->bso', h, wqkv)
        q = qkv[..., :NH * HD].reshape(B, S, NH, HD)
        k = qkv[..., NH * HD:(NH + NKV) * HD].reshape(B, S, NKV, HD)
        v = qkv[..., (NH + NKV) * HD:].reshape(B, S, NKV, HD)
        cos, sin = _rope_tables(S)
        q = _apply_rope(q, cos, sin)
        k = _apply_rope(k, cos, sin)
        groups = NH // NKV
        k = jnp.repeat(k, groups, axis=2)
        v = jnp.repeat(v, groups, axis=2)
        scale = HD ** (-0.5)
        scores = jnp.einsum('bqhd,bkhd->bhqk', q, k) * scale
        causal = jnp.tril(jnp.ones((S, S), dtype=bool))
        scores = jnp.where(causal[None, None], scores, jnp.finfo(scores.dtype).min)
        probs = jax.nn.softmax(scores, axis=-1)
        attn = jnp.einsum('bhqk,bkhd->bqhd', probs, v).reshape(B, S, NH * HD)
        x = x + jnp.einsum('bso,ho->bsh', attn, wo)
        h = _rmsnorm(x, ln2_w).reshape(-1, HID)
        T = h.shape[0]
        logits = jnp.einsum('th,eh->te', h, gate_w)
        rprobs = jax.nn.softmax(logits.astype(jnp.float32), axis=-1)
        topw, topi = jax.lax.top_k(rprobs, TOPK)
        topw = topw / jnp.sum(topw, axis=-1, keepdims=True)
        wfull = jnp.zeros((T, E), jnp.float32).at[jnp.arange(T)[:, None], topi].set(topw)
        wfull = wfull.astype(h.dtype)
        out = jnp.zeros((T, HID), h.dtype)
        for e in range(E):
            w1 = w13[e, :FFN]
            w3 = w13[e, FFN:]
            g = jax.nn.silu(h @ w1.T) * (h @ w3.T)
            out = out + jnp.einsum('tf,hf->th', g, w2[e]) * wfull[:, e:e + 1]
        return x + out.reshape(B, S, HID)
    x = x + _L0_attn_ref(_layernorm(x, axis=-1), L0_attn_W_in, L0_attn_conv_w, L0_attn_conv_b, L0_attn_W_xproj, L0_attn_D, L0_attn_W_out)
    x = x + _L0_xattn_ref(ctx_1024, _layernorm(x, axis=-1), ctx_1024, L0_xattn_Wk, L0_xattn_Wq, L0_xattn_Wv)
    x = x + _L0_ffn_ref(_layernorm(x, axis=-1), L0_ffn_gate_w, L0_ffn_gate_b, L0_ffn_w1, L0_ffn_b1, L0_ffn_w2, L0_ffn_b2)
    x = x + _L1_attn_ref(_layernorm(x, axis=-1), L1_attn_Wq, L1_attn_Wk, L1_attn_Wv, L1_attn_Wo, L1_attn_bo)
    x = x + _L1_xattn_ref(_layernorm(x, axis=-1), ctx_1024, ctx_1024, fside_BxSxS2_0, fside_BxSxS2_0, fside_BxSxS2_0, L1_xattn_Wq, L1_xattn_bq, L1_xattn_Wk, L1_xattn_bk, L1_xattn_Wv, L1_xattn_bv, L1_xattn_beta_risk, L1_xattn_beta_prio, L1_xattn_beta_impl)
    x = x + _L1_ffn_ref(_layernorm(x, axis=-1), L1_ffn_ln1_w, L1_ffn_ln2_w, L1_ffn_wqkv, L1_ffn_wo, L1_ffn_gate_w, L1_ffn_w13, L1_ffn_w2)
    return x

_drawn_inputs = setup_inputs


def setup_inputs(seed=0):
    import zlib

    import numpy as np

    out = dict(_drawn_inputs(seed))
    spreads = {'L0_attn_D': (1.0, 0.2),
     'L0_ffn_gate_b': (0.0, 0.1),
     'L0_ffn_b1': (0.0, 0.1),
     'L0_ffn_b2': (0.0, 0.1),
     'L1_attn_bo': (0.0, 0.1),
     'L1_ffn_ln1_w': (1.0, 0.2),
     'L1_ffn_ln2_w': (1.0, 0.2)}
    factors = {}
    for name, (base, spread) in spreads.items():
        noise = np.random.default_rng([zlib.crc32(name.encode()), seed]).standard_normal(out[name].shape)
        drawn = base * np.exp(spread * noise) if base else spread * noise
        out[name] = jnp.asarray(drawn.astype(out[name].dtype))
    for name, factor in factors.items():
        out[name] = (out[name] * factor).astype(out[name].dtype)
    return out
```

```python
from contextlib import ExitStack

import numpy as np
import concourse.bass as bass
from concourse import mybir

F32 = mybir.dt.float32
BF16 = mybir.dt.bfloat16
I32 = mybir.dt.int32
U32 = mybir.dt.uint32
ALU = mybir.AluOpType
ACT = mybir.ActivationFunctionType
AX = mybir.AxisListType.X

P = 128
NSEQ = 16
D = 256
KD = D // P
GS = 4
NG = NSEQ // GS
GT = GS * P
NH, HD = 16, 16
DI = 512
KI = DI // P
DSTATE = 16
E0, F0 = 32, 1024
CAP = 154
E1, F1 = 8, 512
R1 = NSEQ * P + P
NT1 = NSEQ * P * 2 // P + E1
NEG = -1.0e30
POLY = [-0.037, 0.481, -2.3, 4.917, -1.791]
RING = 4
NB = 8
ND = 8
DCONST = [(0, 8), (8, 24), (24, 88), (88, 88 + NT1), (88 + NT1, 88 + 2 * NT1)]
STOP = None


class Lane:

    def __init__(self, eng, sem, step=1):
        self.eng, self.sem, self.step, self.count, self.seen = eng, sem, step, 0, {}

    def mark(self, ins):
        self.count += self.step
        ins.then_inc(self.sem, self.step)
        return (self, self.count)

    def need(self, *marks):
        for m in marks:
            if m is not None and self.seen.get(m[0], 0) < m[1]:
                self.eng.wait_ge(m[0].sem, m[1])
                self.seen[m[0]] = m[1]


class Core:

    def __init__(self, nc, ctx):
        self.nc, self.ctx = nc, ctx
        self.pe = Lane(nc.tensor, self.sem("pe"))
        self.dve = Lane(nc.vector, self.sem("dve"))
        self.act = Lane(nc.scalar, self.sem("act"))
        self.pool = Lane(nc.gpsimd, self.sem("pool"))
        self.sp = Lane(nc.sync, self.sem("sp"))
        self.lanes = [self.pe, self.dve, self.act, self.pool, self.sp]
        self.streams = []
        self.ps = ctx.enter_context(nc.psum_tensor("ps", [P, 8, 512], F32))
        self.bank_read = [None] * 8

    def sem(self, name):
        return self.ctx.enter_context(self.nc.semaphore("s_" + name))

    def stream(self, name, reset=True):
        s = Lane(None, self.sem(name), 16)
        if reset:
            self.streams.append(s)
        return s

    def new_epoch(self):
        for lane in self.lanes:
            lane.need((lane, lane.count))
        for s in self.streams:
            self.sp.need((s, s.count))
        self.nc.all_engine_barrier()
        for x in self.lanes + self.streams:
            if x.count:
                self.nc.sync.sem_clear(x.sem)
            x.count = 0
        for x in self.lanes:
            x.seen = {}
        self.bank_read = [None] * 8
        self.nc.all_engine_barrier()

    def transposes(self, bank, pairs, ident, *marks):
        self.pe.need(self.bank_read[bank], *marks)
        for col, src in pairs:
            n = src.shape[0]
            ins = self.nc.tensor.transpose(self.ps[0:src.shape[1], bank, col:col + n], src, ident[0:n, 0:n])
        return self.pe.mark(ins)


def layernorm(c, buf, xg, xn, xt, ident, x_ready, xn_free=None, banks=(0, 1)):
    nc, pe, dve, act, pool = c.nc, c.pe, c.dve, c.act, c.pool
    dve.need(x_ready, xn_free)
    for s in range(GS):
        st = dve.mark(nc.vector.bn_stats(buf["st"][:, s, :], xg[:, s, :]))
    dve.need(st)
    for s in range(GS):
        mv = dve.mark(nc.vector.bn_aggr(buf["mv"][:, s, :], buf["st"][:, s, :]))
    dve.need(mv)
    ve = dve.mark(nc.vector.tensor_scalar(buf["ve"][:, :], buf["mv"][:, :, 1], 1e-5, None, ALU.add))
    pool.need(ve)
    rs = pool.mark(nc.gpsimd.tensor_tensor(buf["rs"][:, :], buf["ve"][:, :], buf["mhalf"][:, :], ALU.pow))
    dve.need(rs)
    for s in range(GS):
        n = dve.mark(nc.vector.tensor_scalar(xn[:, s, :], xg[:, s, :], buf["mv"][:, s, 0:1],
                                             buf["rs"][:, s:s + 1], ALU.subtract, ALU.mult))
    return n, transpose_group(c, xn, xt, ident, n, banks)


def transpose_group(c, xn, xt, ident, ready, banks=(0, 1), scale=None):
    nc, act = c.nc, c.act
    for k in range(KD):
        b = banks[k % 2]
        t = c.transposes(b, [(P * s, xn[:, s, P * k:P * k + P]) for s in range(GS)], ident, ready)
        act.need(t)
        if scale is None:
            m = act.mark(nc.scalar.activation(xt[:, k, :], c.ps[:, b, :], ACT.Copy))
        else:
            m = act.mark(nc.scalar.activation(xt[:, k, :], c.ps[:, b, :], ACT.Identity, scale=scale[:, k:k + 1]))
        c.bank_read[b] = m
    return m


def project(c, bank, w, x, ready, rows=P, last=True):
    nc, pe = c.nc, c.pe
    pe.need(c.bank_read[bank], *ready)
    for k in range(len(w)):
        ins = nc.tensor.matmul(c.ps[0:rows, bank, 0:x[k].shape[-1]], w[k], x[k], start=(k == 0), stop=(k == len(w) - 1))
    return pe.mark(ins)


def attention(c, buf, con, qt, kp, make_v, consume, ready, mask=None, adaptive=None):
    nc, pe, dve, act, pool = c.nc, c.pe, c.dve, c.act, c.pool
    S = c.ps[:, 0:4, :]
    heads = [(g, ch, j) for g in range(4) for ch in range(KD) for j in range(2)]
    soft_read = [None]
    pt_free = [None]
    os_free = [None]

    def scores(s):
        tok = slice(P * s, P * s + P)
        pe.need(*ready, *[c.bank_read[b] for b in range(4)])
        for g in range(4):
            if mask is not None:
                nc.tensor.matmul(c.ps[:, g, :], con["ident_bf"], mask, start=True, stop=True, skip_group_check=True)
            for ch in range(KD):
                ins = nc.tensor.matmul(c.ps[:, g, 256 * ch:256 * ch + 256], qt[32 * g:32 * g + 32, ch, tok],
                                       kp[32 * g:32 * g + 32, ch, :, tok], start=(mask is None), stop=True,
                                       tile_position=(32 * g, 0), skip_group_check=True)
        return pe.mark(ins)

    def softmax(s, m_scores, d_free):
        dve.need(m_scores, d_free)
        view = S.rearrange("p b (h k) -> p (b h) k", k=P)
        mx = dve.mark(nc.vector.tensor_reduce(buf["mx"][:, :], view, AX, ALU.max))
        dve.need(mx)
        sub = dve.mark(nc.vector.tensor_tensor(buf["D"][:, :, :], view,
                                               buf["mx"][:, :, None].to_broadcast([P, NH, P]), ALU.subtract))
        for b in range(4):
            c.bank_read[b] = sub
        if adaptive is not None:
            return adaptive(s, sub)
        act.need(sub)
        return act.mark(nc.scalar.activation(buf["D"][:, :, :], buf["D"][:, :, :], ACT.Exp))

    def weigh(s, e, v):
        d_read = []
        for q in range(4):
            b = 4 + q % 2
            t = c.transposes(b, [(P * n, buf["D"][:, 4 * q + n, :]) for n in range(4)], con["ident"], e)
            d_read = t
            act.need(t, pt_free[0])
            cp = act.mark(nc.scalar.activation(buf["PT"][:, 4 * q:4 * q + 4, :].rearrange("p h k -> p (h k)"),
                                               c.ps[:, b, :], ACT.Copy))
            c.bank_read[b] = cp
        pe.need(cp, v, c.bank_read[6])
        for n, (g, ch, j) in enumerate(heads):
            h = 8 * ch + 2 * g + j
            u, at = h % 4, h // 4
            ins = nc.tensor.matmul(c.ps[32 * u:32 * u + 32, 6, P * at:P * at + P], buf["V"][:, s % 2, h, :],
                                   buf["PT"][:, n, :], start=True, stop=True, tile_position=(0, 32 * u),
                                   skip_group_check=True)
        pv = pe.mark(ins)
        pt_free[0] = pv
        act.need(pv, os_free[0])
        os = act.mark(nc.scalar.activation(buf["OS"][:, :], c.ps[:, 6, :], ACT.Copy))
        c.bank_read[6] = os
        ot = c.transposes(7, [(P * at, buf["OS"][:, P * at:P * at + P]) for at in range(4)], con["ident"], os)
        os_free[0] = ot
        c.bank_read[7] = consume(s, c.ps[:, 7, :].rearrange("p (h e) -> p h e", e=32), ot)
        return d_read, pv

    v_free = [None, None]
    m = scores(0)
    v = make_v(0, 0, v_free[0])
    e = softmax(0, m, None)
    for s in range(GS):
        if s + 1 < GS:
            m = scores(s + 1)
            v_next = make_v(s + 1, (s + 1) % 2, v_free[(s + 1) % 2])
        d_read, pv = weigh(s, e, v)
        v_free[s % 2] = pv
        if s + 1 < GS:
            e = softmax(s + 1, m, d_read)
            v = v_next


def normalized(c, buf, out, ot, mark, free=None):
    nc, dve = c.nc, c.dve
    dve.need(mark, free)
    r = dve.mark(nc.vector.reciprocal(buf["rz"][:, :], ot[:, :, HD]))
    dve.need(r)
    return dve.mark(nc.vector.tensor_tensor(out.rearrange("p (h e) -> p h e", e=HD), ot[:, :, 0:HD],
                                            buf["rz"][:, :, None].to_broadcast([P, NH, HD]), ALU.mult))


def head_keys(c, bank, kp, ch, par, mark):
    nc, act = c.nc, c.act
    act.need(mark)
    for j in range(2):
        m = act.mark(nc.scalar.activation(kp[:, ch, j, :], c.ps[:, bank, :], ACT.Copy, scale=par[:, j:j + 1]))
    c.bank_read[bank] = m
    return m


def top2(c, buf, con, n_exp, logits, ready, base_bank, n_slot):
    nc, pe, dve, act, pool = c.nc, c.pe, c.dve, c.act, c.pool
    iota = con["iota"][:, 0:n_exp]
    dve.need(ready)
    a = dve.mark(nc.vector.max(out=buf["m8"][:, :], in_=logits))
    dve.need(a)
    a = dve.mark(nc.vector.max_index(out=buf["i8"][:, :], in_max=buf["m8"][:, :], in_values=logits))
    d = dve.mark(nc.vector.tensor_tensor(buf["gap"][:, :], buf["m8"][:, 1:2], buf["m8"][:, 0:1], ALU.subtract))
    act.need(d)
    ex = act.mark(nc.scalar.activation(buf["gap"][:, :], buf["gap"][:, :], ACT.Exp))
    dve.need(a)
    f = dve.mark(nc.vector.tensor_copy(buf["idx"][:, :], buf["i8"][:, 0:2]))
    dve.need(f, ex)
    for k in range(2):
        oh = dve.mark(nc.vector.tensor_scalar(buf["oh"][:, k, 0:n_exp], iota, buf["idx"][:, k:k + 1], None, ALU.is_equal))
    dn = dve.mark(nc.vector.tensor_scalar(buf["den"][:, :], buf["gap"][:, :], 1.0, None, ALU.add))
    dve.need(oh, dn)
    mm = dve.mark(nc.vector.tensor_tensor(buf["ohs"][:, 0:n_exp], buf["oh"][:, 0, 0:n_exp], buf["oh"][:, 1, 0:n_exp], ALU.add))
    w = dve.mark(nc.vector.reciprocal(buf["w"][:, 0:1], buf["den"][:, :]))
    dve.need(w)
    w = dve.mark(nc.vector.tensor_tensor(buf["w"][:, 1:2], buf["gap"][:, :], buf["w"][:, 0:1], ALU.mult))
    pe.need(mm, c.bank_read[base_bank])
    pb = c.ps[:, base_bank, 0:n_exp]
    nc.tensor.matmul(pb, con["before_bf"], buf["ohs"][:, 0:n_exp], start=True, stop=False)
    q = pe.mark(nc.tensor.matmul(pb, con["ones_bf"], buf["total"][:, 0:n_exp], start=False, stop=True))
    dve.need(q)
    for k in range(2):
        pr = dve.mark(nc.vector.tensor_tensor(buf["pr"][:, k, 0:n_exp], buf["oh"][:, k, 0:n_exp], pb, ALU.mult))
    t = dve.mark(nc.vector.tensor_tensor(buf["total"][:, 0:n_exp], buf["total"][:, 0:n_exp], buf["ohs"][:, 0:n_exp], ALU.add))
    dve.need(pr, t)
    c.bank_read[base_bank] = pr
    pos = dve.mark(nc.vector.tensor_reduce(buf["pos"][:, :], buf["pr"][:, :, 0:n_exp], AX, ALU.add))
    return pos, w


def phase_a(c, con, dram, persist):
    nc, pe, dve, act, pool, sp = c.nc, c.pe, c.dve, c.act, c.pool, c.sp
    with ExitStack() as ctx:
        def sb(name, shape, dt=F32):
            return ctx.enter_context(nc.sbuf_tensor("a_" + name, shape, dt))

        ident = con["ident"]
        win = sb("win", [P, KD, 2 * DI])
        wx = sb("wx", [P, KI, 64 + DI])
        wo = sb("wo", [P, KI, D])
        conv = sb("conv", [P, KI, 5])
        dvec = sb("dvec", [P, KI])
        bd = sb("bd", [P, 3, P])
        gw = sb("gw", [P, KD, E0])
        gb = sb("gb", [P, E0])
        xg = sb("xg", [P, GS, D])
        xn = sb("xn", [P, GS, D])
        xt = sb("xt", [P, KD, GT])
        ct = sb("ct", [P, KD, GT])
        buf = {"mhalf": con["mhalf"]}
        for name, shape, dt in (("st", [P, GS, 6], F32), ("mv", [P, GS, 2], F32), ("ve", [P, GS], F32),
                                ("rs", [P, GS], F32), ("mx", [P, NH], F32), ("rz", [P, NH], F32),
                                ("m8", [P, 8], F32), ("i8", [P, 8], U32), ("gap", [P, 1], F32), ("idx", [P, 2], F32),
                                ("oh", [P, 2, E0], F32), ("den", [P, 1], F32), ("ohs", [P, E0], BF16),
                                ("w", [P, 2], F32), ("total", [P, E0], BF16), ("pr", [P, 2, E0], F32),
                                ("pos", [P, 2], F32), ("lg", [P, E0], F32), ("over", [P, 2], F32),
                                ("clip", [P, 2], F32), ("sidx", [P, 2], F32), ("slot", [P, GS, 2], U32),
                                ("gidx", [P, GS, 2], U32), ("gwt", [P, GS, 2], F32)):
            buf[name] = sb(name, shape, dt)

        w_load = c.stream("a_w")
        for dst, src in ((win, "win"), (wx, "wx"), (wo, "wo"), (conv, "conv"), (dvec, "dvec"), (gw, "gw")):
            m = w_load.mark(nc.sync.dma_start(dst[:], dram[src]))
        m = w_load.mark(nc.sync.dma_start(gb[:, :], dram["gb"].partition_broadcast(P)))
        m = w_load.mark(nc.sync.dma_start(bd[:, :, :], dram["bd"]))
        z = dve.mark(nc.vector.memset(buf["total"][:, :], 0.0))
        for lane in (pe, dve, act, pool):
            lane.need(m, z)
        c.new_epoch()

        x_all = persist["x"]
        s_ct, s_disp = c.stream("a_ct"), c.stream("a_disp", reset=False)
        with nc.Fori(0, NG) as i:
            ct_in = s_ct.mark(nc.sync.dma_start(ct[:, :, :], dram["ctx_t"][:, :, bass.ds(i * GT, GT)]))
            x_in = act.mark(nc.scalar.activation(xg[:, :, :], x_all[:, bass.ds(i * GS, GS), :], ACT.Copy))
            _, xt_ok = layernorm(c, buf, xg, xn, xt, ident, x_in)

            with ExitStack() as inner:
                def sb2(name, shape, dt=F32):
                    return inner.enter_context(nc.sbuf_tensor("a_" + name, shape, dt))

                xb = sb2("xb", [P, KI, GS, P + 3])
                xc = sb2("xc", [P, KI, GT])
                sz = sb2("sz", [P, KI, GT])
                t1 = sb2("t1", [P, KI, GT])
                cs = sb2("cs", [DSTATE, GT])
                bc = sb2("bc", [DSTATE, GT])
                pad = pool.mark(nc.gpsimd.memset(xb[:, :, :, 0:3], 0.0))
                z_ok = []
                xb_ok = []
                for m in range(2 * KI):
                    r = project(c, m, [win[:, k, P * m:P * m + P] for k in range(KD)], [xt[:, k, :] for k in range(KD)], (xt_ok,))
                    act.need(r)
                    if m < KI:
                        a = act.mark(nc.scalar.activation(xb[:, m, :, 3:P + 3], c.ps[:, m, :].rearrange("p (s l) -> p s l", l=P), ACT.Copy))
                        xb_ok.append(a)
                    else:
                        a = act.mark(nc.scalar.activation(sz[:, m - KI, :], c.ps[:, m, :], ACT.Silu))
                        z_ok.append(a)
                    c.bank_read[m] = a
                dve.need(pad)
                for m in range(KI):
                    tv = t1[:, m, :].rearrange("p (s l) -> p s l", l=P)
                    dve.need(xb_ok[m])
                    a = dve.mark(nc.vector.tensor_scalar(tv, xb[:, m, :, 0:P], conv[:, m, 0:1], conv[:, m, 4:5], ALU.mult, ALU.add))
                    for k in range(1, 4):
                        dve.need(a)
                        a = dve.mark(nc.vector.scalar_tensor_tensor(out=tv, in0=xb[:, m, :, k:k + P], scalar=conv[:, m, k:k + 1],
                                                                    in1=tv, op0=ALU.mult, op1=ALU.add))
                    act.need(a)
                    xc_ok = act.mark(nc.scalar.activation(xc[:, m, :], t1[:, m, :], ACT.Silu))
                xcs = [xc[:, k, :] for k in range(KI)]
                r = project(c, 4, [wx[:, k, 0:64] for k in range(KI)], xcs, (xc_ok,), rows=64)
                act.need(r)
                a = act.mark(nc.scalar.activation(cs[:, :], c.ps[32:32 + DSTATE, 4, :], ACT.Copy))
                dve.need(a)
                b_ok = dve.mark(nc.vector.tensor_tensor(bc[:, :], c.ps[0:DSTATE, 4, :], cs[:, :], ALU.mult))
                c.bank_read[4] = b_ok
                dl = []
                for m in range(KI):
                    r = project(c, m, [wx[:, k, 64 + P * m:64 + P * m + P] for k in range(KI)], xcs, (xc_ok,))
                    act.need(r)
                    a = act.mark(nc.scalar.activation(t1[:, m, :], c.ps[:, m, :], ACT.Abs))
                    act.need(a)
                    dl.append((r, act.mark(nc.scalar.activation(t1[:, m, :], t1[:, m, :], ACT.Exp, scale=-1.0))))
                bc_ok = project(c, 5, [con["ones"][0:DSTATE, :]], [bc[:, :]], (b_ok,))
                act.need(dl[-1][1])
                y_ok = []
                for m in range(KI):
                    a = act.mark(nc.scalar.activation(t1[:, m, :], t1[:, m, :], ACT.Ln, bias=1.0))
                    dve.need(a, dl[m][0], bc_ok)
                    a = dve.mark(nc.vector.scalar_tensor_tensor(out=t1[:, m, :], in0=c.ps[:, m, :], scalar=0.0, in1=t1[:, m, :], op0=ALU.max, op1=ALU.add))
                    c.bank_read[m] = a
                    dve.need(a)
                    a = dve.mark(nc.vector.tensor_tensor(t1[:, m, :], t1[:, m, :], c.ps[:, 5, :], ALU.mult))
                    dve.need(a)
                    a = dve.mark(nc.vector.scalar_tensor_tensor(out=t1[:, m, :], in0=t1[:, m, :], scalar=dvec[:, m:m + 1], in1=xc[:, m, :], op0=ALU.add, op1=ALU.mult))
                    dve.need(a, z_ok[m])
                    a = dve.mark(nc.vector.tensor_tensor(t1[:, m, :], t1[:, m, :], sz[:, m, :], ALU.mult))
                    y_ok.append(a)
                c.bank_read[5] = a
                for s in range(GS):
                    b = 6 + s % 2
                    r = project(c, b, [t1[:, k, P * s:P * s + P] for k in range(KI)], [wo[:, k, :] for k in range(KI)], (y_ok[-1],))
                    dve.need(r)
                    x_in = dve.mark(nc.vector.tensor_tensor(xg[:, s, :], xg[:, s, :], c.ps[:, b, 0:D], ALU.add))
                    c.bank_read[b] = x_in
                mamba_done = r

            with ExitStack() as inner:
                qt, kp = attention_buffers(nc, inner, "a_", buf)
                _, xt_ok = layernorm(c, buf, xg, xn, xt, ident, x_in)
                pool.need(mamba_done)
                vz = v_constants(c, buf)
                act.need(ct_in, mamba_done)
                dve.need(mamba_done)
                for ch in range(KD):
                    r = project(c, 2 + ch, [bd[:, 0, :]], [xt[:, ch, :]], (xt_ok,))
                    act.need(r)
                    q_ok = act.mark(nc.scalar.activation(qt[:, ch, :], c.ps[:, 2 + ch, :], ACT.Copy, scale=HD ** -0.5))
                    c.bank_read[2 + ch] = q_ok
                    r = project(c, 4 + ch, [bd[:, 1, :]], [ct[:, ch, :]], (ct_in,))
                    k_ok = head_keys(c, 4 + ch, kp, ch, con["par"], r)

                def make_v(s, slot, free):
                    pe.need(c.bank_read[5], ct_in)
                    for ch in range(KD):
                        ins = nc.tensor.matmul(c.ps[:, 5, P * ch:P * ch + P], ct[:, ch, P * s:P * s + P], bd[:, 2, :], start=True, stop=True)
                    r = pe.mark(ins)
                    act.need(r, free, vz)
                    a = act.mark(nc.scalar.activation(buf["V"][:, slot, :, 0:HD], c.ps[:, 5, 0:D].rearrange("p (h e) -> p h e", e=HD), ACT.Copy))
                    c.bank_read[5] = a
                    return a

                res = [None]

                def consume(s, ot, mark):
                    a = normalized(c, buf, buf["AO"][:, :], ot, mark)
                    dve.need(a)
                    res[0] = dve.mark(nc.vector.tensor_tensor(xg[:, s, :], xg[:, s, :], buf["AO"][:, :], ALU.add))
                    return a

                attention(c, buf, con, qt, kp, make_v, consume, (q_ok, k_ok))
                x_in = res[0]

            xn_ok, xt_ok = layernorm(c, buf, xg, xn, xt, ident, x_in)
            act.need(x_in)
            x_out = act.mark(nc.scalar.activation(x_all[:, bass.ds(i * GS, GS), :], xg[:, :, :], ACT.Copy))
            for s in range(GS):
                b = 2 + s % 2
                r = project(c, b, [xt[:, k, P * s:P * s + P] for k in range(KD)], [gw[:, k, :] for k in range(KD)], (xt_ok,))
                dve.need(r)
                lg = dve.mark(nc.vector.tensor_tensor(buf["lg"][:, :], c.ps[:, b, 0:E0], gb[:, :], ALU.add))
                c.bank_read[b] = lg
                pos, w = top2(c, buf, con, E0, buf["lg"][:, :], lg, 4 + s % 2, s)
                dve.need(pos)
                a = dve.mark(nc.vector.tensor_scalar(buf["over"][:, :], buf["pos"][:, :], float(CAP) - 0.5, None, ALU.is_gt))
                a2 = dve.mark(nc.vector.tensor_scalar(buf["clip"][:, :], buf["pos"][:, :], float(CAP - 1), None, ALU.min))
                dve.need(a, a2)
                a = dve.mark(nc.vector.scalar_tensor_tensor(out=buf["sidx"][:, :], in0=buf["idx"][:, :], scalar=float(CAP), in1=buf["clip"][:, :], op0=ALU.mult, op1=ALU.add))
                dve.need(a)
                gi = dve.mark(nc.vector.tensor_copy(buf["gidx"][:, s, :], buf["sidx"][:, :]))
                a = dve.mark(nc.vector.scalar_tensor_tensor(out=buf["slot"][:, s, :], in0=buf["over"][:, :], scalar=float(E0 * CAP), in1=buf["sidx"][:, :], op0=ALU.mult, op1=ALU.add))
                keep = dve.mark(nc.vector.tensor_scalar(buf["over"][:, :], buf["over"][:, :], -1.0, 1.0, ALU.mult, ALU.add))
                dve.need(keep, w)
                wt = dve.mark(nc.vector.tensor_tensor(buf["gwt"][:, s, :], buf["w"][:, :], buf["over"][:, :], ALU.mult))
                pool.need(a, xn_ok)
                for k in range(2):
                    s_disp.mark(nc.gpsimd.indirect_dma_start(
                        out=dram["xe"], out_offset=bass.IndirectOffsetOnAxis(ap=buf["slot"][:, s, k:k + 1], axis=0),
                        in_=xn[:, s, :], in_offset=None, bounds_check=E0 * CAP - 1, oob_is_err=False))
            act.need(wt, gi)
            act.mark(nc.scalar.activation(persist["gwt"][:, bass.ds(i * GS, GS), :], buf["gwt"][:, :, :], ACT.Copy))
            dve.need(wt, gi)
            dve.mark(nc.vector.tensor_copy(persist["gidx"][:, bass.ds(i * GS, GS), :], buf["gidx"][:, :, :]))
            nc.sync.wait_ge(s_disp.sem, (i + 1) * s_disp.count)
            c.new_epoch()


def attention_buffers(nc, inner, prefix, buf):
    def sb(name, shape, dt=F32):
        return inner.enter_context(nc.sbuf_tensor(prefix + name, shape, dt))

    buf["D"] = sb("D", [P, NH, P])
    buf["PT"] = sb("PT", [P, NH, P])
    buf["V"] = sb("V", [P, 2, NH, 32])
    buf["OS"] = sb("OS", [P, GT])
    buf["AO"] = sb("AO", [P, D])
    return sb("qt", [P, KD, GT]), sb("kp", [P, KD, 2, GT])


def v_constants(c, buf):
    c.pool.mark(c.nc.gpsimd.memset(buf["V"][:, :, :, HD + 1:32], 0.0))
    return c.pool.mark(c.nc.gpsimd.memset(buf["V"][:, :, :, HD:HD + 1], 1.0))


def phase_b(c, con, dram, ring, s_ring):
    nc, pe, dve, act, pool, sp = c.nc, c.pe, c.dve, c.act, c.pool, c.sp
    w1r, w2r = ring
    MF = F0 // P
    TAIL = CAP - P
    with ExitStack() as ctx:
        def sb(name, shape, dt=F32):
            return ctx.enter_context(nc.sbuf_tensor("b_" + name, shape, dt))

        b1 = sb("b1", [P, E0, MF])
        b2 = sb("b2", [P, E0, KD])
        b1l = sb("b1l", [P, NB, MF])
        b2l = sb("b2l", [P, NB, KD])
        xe = sb("xe", [P, NB, D])
        xe2 = sb("xe2", [TAIL, NB, D])
        xet = sb("xet", [P, 2, KD, CAP])
        ht = sb("ht", [P, 2, MF, CAP])
        yt = sb("yt", [P, 2, KD, CAP])
        ye = sb("ye", [P, 2, D])
        ye2 = sb("ye2", [TAIL, 2, D])
        s_b = c.stream("b_bias")
        s_x, s_y = c.stream("b_x"), [c.stream("b_y0"), c.stream("b_y1")]
        s_b.mark(nc.sync.dma_start(b1[:, :, :], dram["b1"]))
        m = s_b.mark(nc.sync.dma_start(b2[:, :, :], dram["b2"]))
        act.need(m)
        xe_rows = dram["xe"].rearrange("(e r) d -> r e d", r=CAP)
        ye_rows = dram["ye"].rearrange("(e r) d -> r e d", r=CAP)

        def experts(first, it, refill):
            s_x.mark(nc.sync.dma_start(xe[:, :, :], xe_rows[0:P, bass.ds(first, NB), :]))
            x_in = s_x.mark(nc.sync.dma_start(xe2[:, :, :], xe_rows[P:CAP, bass.ds(first, NB), :]))
            b_in = act.mark(nc.scalar.activation(b1l[:, :, :], b1[:, bass.ds(first, NB), :], ACT.Copy))
            b_in = act.mark(nc.scalar.activation(b2l[:, :, :], b2[:, bass.ds(first, NB), :], ACT.Copy))
            act.need(b_in)
            dve.need(b_in)
            h_ok, down_ok, yt_ok, xt_read, xt_ok = [None] * NB, [None] * NB, [None] * NB, [None] * NB, [None] * NB
            turned = [None] * NB
            y_out = [None] * NB

            def turn_in(e):
                pe.need(x_in, c.bank_read[4])
                for k in range(KD):
                    nc.tensor.transpose(c.ps[:, 4, CAP * k:CAP * k + P], xe[:, e, k:D:KD], con["ident"])
                    t = nc.tensor.transpose(c.ps[:, 4, CAP * k + P:CAP * k + CAP], xe2[:, e, k:D:KD], con["ident"][0:TAIL, 0:TAIL])
                t = pe.mark(t)
                dve.need(t, xt_read[e - 2] if e >= 2 else None)
                xt_ok[e] = dve.mark(nc.vector.tensor_copy(xet[:, e % 2, :, :], c.ps[:, 4, 0:KD * CAP].rearrange("p (k t) -> p k t", k=KD)))
                c.bank_read[4] = xt_ok[e]

            def up(e):
                slot = e % RING
                pe.need(xt_ok[e])
                nc.tensor.wait_ge(s_ring[slot].sem, it * (32 * NB // RING) + 32 * (e // RING + 1))
                act.need(down_ok[e - 2] if e >= 2 else None)
                for m in range(MF):
                    b = (m // 2) % 4
                    if m % 2 == 0:
                        pe.need(c.bank_read[b])
                    for k in range(KD):
                        ins = nc.tensor.matmul(c.ps[:, b, CAP * (m % 2):CAP * (m % 2) + CAP], w1r[:, slot, k, m:F0:MF],
                                               xet[:, e % 2, k, :], start=(k == 0), stop=(k == KD - 1), skip_group_check=True)
                    if m % 2 == 1:
                        r = pe.mark(ins)
                        act.need(r)
                        for q in (m - 1, m):
                            a = act.mark(nc.scalar.activation(ht[:, e % 2, q, :], c.ps[:, b, CAP * (q % 2):CAP * (q % 2) + CAP],
                                                              ACT.Gelu, bias=b1l[:, e, q:q + 1]))
                        c.bank_read[b] = a
                xt_read[e] = r
                h_ok[e] = a

            def down(e):
                slot = e % RING
                pe.need(h_ok[e], c.bank_read[5])
                for j in range(KD):
                    for m in range(MF):
                        ins = nc.tensor.matmul(c.ps[:, 5, CAP * j:CAP * j + CAP], w2r[:, slot, m, P * j:P * j + P],
                                               ht[:, e % 2, m, :], start=(m == 0), stop=(m == MF - 1), skip_group_check=True)
                down_ok[e] = pe.mark(ins)
                dve.need(down_ok[e], turned[e - 2] if e >= 2 else None)
                for j in range(KD):
                    a = dve.mark(nc.vector.tensor_scalar(yt[:, e % 2, j, :], c.ps[:, 5, CAP * j:CAP * j + CAP], b2l[:, e, j:j + 1], None, ALU.add))
                c.bank_read[5] = a
                yt_ok[e] = a
                if e < refill:
                    sp.need(down_ok[e])
                    load_expert(c, dram, ring, s_ring, slot, first + e + RING)

            def turn_out(e):
                pe.need(yt_ok[e], c.bank_read[6], c.bank_read[7])
                for j in range(KD):
                    nc.tensor.transpose(c.ps[:, 6, P * j:P * j + P], yt[:, e % 2, j, 0:P], con["ident"])
                    t = nc.tensor.transpose(c.ps[0:TAIL, 7, P * j:P * j + P], yt[:, e % 2, j, P:CAP], con["ident"])
                turned[e] = pe.mark(t)
                dve.need(turned[e], y_out[e - 2] if e >= 2 else None)
                a = dve.mark(nc.vector.tensor_copy(ye[:, e % 2, :], c.ps[:, 6, 0:D]))
                a2 = dve.mark(nc.vector.tensor_copy(ye2[:, e % 2, :], c.ps[0:TAIL, 7, 0:D]))
                c.bank_read[6], c.bank_read[7] = a, a2
                sp.need(a, a2)
                s_y[e % 2].mark(nc.sync.dma_start(ye_rows[0:P, bass.ds(first + e, 1), :], ye[:, e % 2:e % 2 + 1, :]))
                y_out[e] = s_y[e % 2].mark(nc.sync.dma_start(ye_rows[P:CAP, bass.ds(first + e, 1), :], ye2[:, e % 2:e % 2 + 1, :]))

            turn_in(0)
            for e in range(NB + 2):
                if e < NB:
                    if e + 1 < NB:
                        turn_in(e + 1)
                    up(e)
                if 1 <= e <= NB:
                    down(e - 1)
                if e >= 2:
                    turn_out(e - 2)
            c.new_epoch()

        c.new_epoch()
        with nc.Fori(0, E0 // NB - 1) as i:
            experts(i * NB, i, NB)
        experts(E0 - NB, E0 // NB - 1, NB - RING)


def load_expert(c, dram, ring, s_ring, slot, e):
    nc = c.nc
    s_ring[slot].mark(nc.sync.dma_start(ring[0][:, slot:slot + 1, :, :].rearrange("p e k f -> p e (k f)"),
                                        dram["w1"].rearrange("e (p k) f -> p e (k f)", p=P)[:, bass.ds(e, 1), :]))
    s_ring[slot].mark(nc.sync.dma_start(ring[1][:, slot:slot + 1, :, :].rearrange("p e m d -> p e (m d)"),
                                        dram["w2"].rearrange("e (p m) d -> p e (m d)", p=P)[:, bass.ds(e, 1), :]))


class Gathers:

    def __init__(self, c, sb, persist, table, name):
        self.c, self.persist, self.table = c, persist, table
        self.idx = sb(name + "_gi", [P, GS, 2], U32)
        self.rows = sb(name + "_g", [P, GS, 2, D])
        self.stream = c.stream(name + "_gather", reset=False)

    def fetch(self, group, free):
        c, nc = self.c, self.c.nc
        c.dve.need(free)
        m = c.dve.mark(nc.vector.tensor_copy(self.idx[:, :, :], self.persist["gidx"][:, bass.ds(group * GS, GS), :]))
        c.pool.need(m, free)
        for s in range(GS):
            for k in range(2):
                self.stream.mark(nc.gpsimd.indirect_dma_start(
                    out=self.rows[:, s, k, :], out_offset=None, in_=self.table,
                    in_offset=bass.IndirectOffsetOnAxis(ap=self.idx[:, s, k:k + 1], axis=0)))

    def wait(self, lane, rounds):
        lane.eng.wait_ge(self.stream.sem, rounds * (16 * 2 * GS))


def rms_rows(c, buf, x, out, eps, ready, free=None):
    nc, dve, act, pool = c.nc, c.dve, c.act, c.pool
    act.need(ready)
    for s in range(GS):
        a = act.mark(nc.scalar.activation(buf["AO"][:, :], x[:, s, :], ACT.Square, accum_out=buf["ss"][:, s:s + 1]))
        act.need(a)
    dve.need(a)
    v = dve.mark(nc.vector.tensor_scalar(buf["ve"][:, :], buf["ss"][:, :], 1.0 / D, eps, ALU.mult, ALU.add))
    pool.need(v)
    r = pool.mark(nc.gpsimd.tensor_tensor(buf["rs"][:, :], buf["ve"][:, :], buf["mhalf"][:, :], ALU.pow))
    dve.need(r, free)
    for s in range(GS):
        m = dve.mark(nc.vector.tensor_scalar(out[:, s, :], x[:, s, :], buf["rs"][:, s:s + 1], None, ALU.mult))
    return m


def phase_c(c, con, dram, persist):
    nc, pe, dve, act, pool, sp = c.nc, c.pe, c.dve, c.act, c.pool, c.sp
    with ExitStack() as ctx:
        def sb(name, shape, dt=F32):
            return ctx.enter_context(nc.sbuf_tensor("c_" + name, shape, dt))

        ident = con["ident"]
        wa = sb("wa", [P, 4, KD, D])
        wc = sb("wc", [P, 3, KD, D])
        wf = sb("wf", [P, 5, KD, D])
        wv = sb("wv", [P, KD, 4 * HD])
        gw = sb("gw", [P, KD, E1])
        cols = sb("cols", [P, 4, KD])
        rows = sb("rows", [P, 2, D])
        beta = sb("beta", [P, 3])
        coef = sb("coef", [P, 1])
        tiny = sb("tiny", [P, 1])
        xg = sb("xg", [P, GS, D])
        xn = sb("xn", [P, GS, D])
        xt = sb("xt", [P, KD, GT])
        ct = sb("ct", [P, KD, GT])
        ao = sb("ao", [P, GS, D])
        phi = sb("phi", [P, GS, P])
        buf = {"mhalf": con["mhalf"]}
        for name, shape, dt in (("st", [P, GS, 6], F32), ("mv", [P, GS, 2], F32), ("ve", [P, GS], F32), ("ss", [P, GS], F32),
                                ("rs", [P, GS], F32), ("mx", [P, NH], F32), ("rz", [P, NH], F32), ("zz", [P, NH], F32),
                                ("en", [P, NH], F32), ("po", [P, NH], F32), ("gt", [P, NH], F32),
                                ("m8", [P, 8], F32), ("i8", [P, 8], U32), ("gap", [P, 1], F32), ("idx", [P, 2], F32),
                                ("oh", [P, 2, E1], F32), ("den", [P, 1], F32), ("ohs", [P, E1], BF16),
                                ("w", [P, 2], F32), ("pr", [P, 2, E1], F32),
                                ("pos", [P, 2], F32), ("lg", [P, E1], F32), ("slot", [P, GS, 2], U32),
                                ("gwl", [P, GS, 2], F32), ("gwt", [P, GS, 2], F32), ("cho", [P, GS, 2], F32), ("pla", [P, GS, 2], F32), ("m4", [P, GS], F32), ("z4", [P, GS], F32)):
            buf[name] = sb(name, shape, dt)
        buf["total"] = persist["total"]
        qt, kp = attention_buffers(nc, ctx, "c_", buf)
        buf["E"] = sb("E", [P, NH, P])
        buf["L"] = buf["PT"]
        gath = Gathers(c, sb, persist, dram["ye"], "c")

        w_load = c.stream("c_w")
        for dst, src in ((wa, "wa"), (wc, "wc"), (wf, "wf"), (wv, "wv"), (gw, "gw1"), (cols, "cols")):
            w_load.mark(nc.sync.dma_start(dst[:], dram[src]))
        w_load.mark(nc.sync.dma_start(rows[:, 0, :], dram["bo"].partition_broadcast(P)))
        w_load.mark(nc.sync.dma_start(rows[:, 1, :], dram["bv"].partition_broadcast(P)))
        for n in range(3):
            m = w_load.mark(nc.sync.dma_start(beta[:, n:n + 1], dram["beta%d" % n].partition_broadcast(P)))
        dve.need(m)
        a = dve.mark(nc.vector.tensor_tensor(coef[:, :], beta[:, 0:1], beta[:, 1:2], ALU.add))
        dve.need(a)
        a = dve.mark(nc.vector.tensor_tensor(coef[:, :], coef[:, :], beta[:, 2:3], ALU.subtract))
        a = dve.mark(nc.vector.memset(tiny[:, :], 1e-9))
        a = dve.mark(nc.vector.memset(buf["total"][:, :], 0.0))
        vz = v_constants(c, buf)
        gath.fetch(0, a)
        c.new_epoch()
        x_all = persist["x"]
        s_ct, s_disp = c.stream("c_ct"), c.stream("c_disp", reset=False)

        def token_values(s, slot, free, w, n, ready, copy):
            pe.need(c.bank_read[5], *ready)
            for k in range(KD):
                ins = nc.tensor.matmul(c.ps[:, 5, 0:n], xt[:, k, P * s:P * s + P], w[:, k, :], start=(k == 0), stop=(k == KD - 1))
            r = pe.mark(ins)
            act.need(r, free)
            a = copy(slot)
            c.bank_read[5] = a
            return a

        def out_projection(ready, w, use):
            t = transpose_group(c, ao, xt, ident, ready)
            for s in range(GS):
                b = 2 + s % 2
                r = project(c, b, [xt[:, k, P * s:P * s + P] for k in range(KD)], [w[:, k, :] for k in range(KD)], (t,))
                dve.need(r)
                m = use(s, b)
                c.bank_read[b] = m
            return m

        def to_ao(s, ot, mark):
            done[0] = normalized(c, buf, ao[:, s, :], ot, mark)
            return done[0]

        done = [None]
        with nc.Fori(0, NG) as i:
            ct_in = s_ct.mark(nc.sync.dma_start(ct[:, :, :], dram["ctx_t"][:, :, bass.ds(i * GT, GT)]))
            ct_in = s_ct.mark(nc.sync.dma_start(phi[:, :, :], dram["phi"][:, bass.ds(i * GS, GS), :]))
            a = act.mark(nc.scalar.activation(buf["gwl"][:, :, :], persist["gwt"][:, bass.ds(i * GS, GS), :], ACT.Copy))
            x_in = act.mark(nc.scalar.activation(xg[:, :, :], x_all[:, bass.ds(i * GS, GS), :], ACT.Copy))
            dve.need(x_in, a)
            gath.wait(dve, i + 1)
            for k in range(2):
                for s in range(GS):
                    a = dve.mark(nc.vector.scalar_tensor_tensor(out=xg[:, s, :], in0=gath.rows[:, s, k, :], scalar=buf["gwl"][:, s, k:k + 1],
                                                                in1=xg[:, s, :], op0=ALU.mult, op1=ALU.add))
                dve.need(a)
            x_in = a
            gath.fetch(i + 1, a)

            if STOP != "b":
                _, xt_ok = layernorm(c, buf, xg, xn, xt, ident, x_in)
                for ch in range(KD):
                    r = project(c, 2 + ch, [wa[:, 0, k, P * ch:P * ch + P] for k in range(KD)], [xt[:, k, :] for k in range(KD)], (xt_ok,))
                    act.need(r)
                    q_ok = act.mark(nc.scalar.activation(qt[:, ch, :], c.ps[:, 2 + ch, :], ACT.Copy, scale=HD ** -0.5))
                    c.bank_read[2 + ch] = q_ok
                    r = project(c, 4 + ch, [wa[:, 1, k, P * ch:P * ch + P] for k in range(KD)], [xt[:, k, :] for k in range(KD)], (xt_ok,))
                    k_ok = head_keys(c, 4 + ch, kp, ch, con["par"], r)

                def values(s, slot, free):
                    return token_values(s, slot, free, wa[:, 2, :, :], D, (xt_ok,), lambda v: act.mark(nc.scalar.activation(
                        buf["V"][:, v, :, 0:HD], c.ps[:, 5, 0:D].rearrange("p (h e) -> p h e", e=HD), ACT.Copy)))

                def temperature(s, sub):
                    dd, ee, ll = buf["D"][:, :, :], buf["E"][:, :, :], buf["L"][:, :, :]
                    act.need(sub)
                    e1 = act.mark(nc.scalar.activation(ee, dd, ACT.Exp))
                    dve.need(e1)
                    a = dve.mark(nc.vector.tensor_reduce(buf["zz"][:, :], ee, AX, ALU.add))
                    dve.need(a)
                    a = dve.mark(nc.vector.reciprocal(buf["zz"][:, :], buf["zz"][:, :]))
                    dve.need(a)
                    a = dve.mark(nc.vector.tensor_tensor(ee, ee, buf["zz"][:, :, None].to_broadcast([P, NH, P]), ALU.mult))
                    act.need(a, (pe, pe.count))
                    a = act.mark(nc.scalar.activation(ll, ee, ACT.Ln, bias=tiny[:, 0:1]))
                    dve.need(a)
                    a = dve.mark(nc.vector.tensor_tensor(ee, ee, ll, ALU.mult))
                    dve.need(a)
                    a = dve.mark(nc.vector.tensor_reduce(buf["en"][:, :], ee, AX, ALU.add, negate=True))
                    en, po = buf["en"][:, :], buf["po"][:, :]
                    dve.need(a)
                    g = dve.mark(nc.vector.tensor_scalar(buf["gt"][:, :], en, 0.5, None, ALU.is_gt))
                    a = dve.mark(nc.vector.tensor_scalar(po, en, POLY[0], None, ALU.mult))
                    for q in POLY[1:4]:
                        dve.need(a)
                        a = dve.mark(nc.vector.scalar_tensor_tensor(out=po, in0=po, scalar=q, in1=en, op0=ALU.add, op1=ALU.mult))
                    dve.need(a)
                    a = dve.mark(nc.vector.tensor_scalar(po, po, POLY[4], 1.0, ALU.add, ALU.max))
                    dve.need(a)
                    a = dve.mark(nc.vector.scalar_tensor_tensor(out=po, in0=po, scalar=-1.0, in1=buf["gt"][:, :], op0=ALU.add, op1=ALU.mult))
                    dve.need(a)
                    a = dve.mark(nc.vector.tensor_scalar(po, po, 1.0, None, ALU.add))
                    dve.need(a)
                    a = dve.mark(nc.vector.tensor_tensor(dd, dd, buf["po"][:, :, None].to_broadcast([P, NH, P]), ALU.mult))
                    act.need(a)
                    return act.mark(nc.scalar.activation(dd, dd, ACT.Exp))

                attention(c, buf, con, qt, kp, values, to_ao, (q_ok, k_ok), mask=con["mask"], adaptive=temperature)

                def add_out(s, b):
                    a = dve.mark(nc.vector.tensor_tensor(xg[:, s, :], xg[:, s, :], c.ps[:, b, 0:D], ALU.add))
                    dve.need(a)
                    return dve.mark(nc.vector.tensor_tensor(xg[:, s, :], xg[:, s, :], rows[:, 0, :], ALU.add))

                x_in = out_projection(done[0], wa[:, 3, :, :], add_out)

            if STOP not in ("b", "c1"):
                _, xt_ok = layernorm(c, buf, xg, xn, xt, ident, x_in)
                v_all = ao
                for ch in range(KD):
                    r = project(c, 2 + ch, [wc[:, 0, k, P * ch:P * ch + P] for k in range(KD)], [xt[:, k, :] for k in range(KD)], (xt_ok,))
                    dve.need(r)
                    q_ok = dve.mark(nc.vector.tensor_scalar(qt[:, ch, :], c.ps[:, 2 + ch, :], cols[:, 0, ch:ch + 1], D ** -0.5, ALU.add, ALU.mult))
                    c.bank_read[2 + ch] = q_ok
                    r = project(c, 4 + ch, [wc[:, 1, k, P * ch:P * ch + P] for k in range(KD)], [ct[:, k, :] for k in range(KD)], (ct_in,))
                    act.need(r)
                    k_ok = act.mark(nc.scalar.activation(kp[:, ch, 0, :], c.ps[:, 4 + ch, :], ACT.Identity, bias=cols[:, 1, ch:ch + 1]))
                    c.bank_read[4 + ch] = k_ok
                for s in range(GS):
                    b = 6 + s % 2
                    r = project(c, b, [ct[:, k, P * s:P * s + P] for k in range(KD)], [wc[:, 2, k, :] for k in range(KD)], (ct_in,))
                    dve.need(r)
                    v_ok = dve.mark(nc.vector.tensor_tensor(v_all[:, s, :], c.ps[:, b, 0:D], rows[:, 1, :], ALU.add))
                    c.bank_read[b] = v_ok
                pe.need(q_ok, k_ok, c.bank_read[0])
                for s in range(GS):
                    for ch in range(KD):
                        ins = nc.tensor.matmul(c.ps[:, 0, P * s:P * s + P], qt[:, ch, P * s:P * s + P], kp[:, ch, 0, P * s:P * s + P],
                                               start=(ch == 0), stop=(ch == KD - 1), skip_group_check=True)
                r = pe.mark(ins)
                dd = buf["D"][:, 0:GS, :]
                dve.need(r, ct_in)
                a = dve.mark(nc.vector.scalar_tensor_tensor(out=dd, in0=phi[:, :, :], scalar=coef[:, 0:1],
                                                            in1=c.ps[:, 0, :].rearrange("p (s t) -> p s t", s=GS), op0=ALU.mult, op1=ALU.add))
                c.bank_read[0] = a
                dve.need(a)
                a = dve.mark(nc.vector.tensor_reduce(buf["m4"][:, :], dd, AX, ALU.max))
                dve.need(a)
                a = dve.mark(nc.vector.tensor_tensor(dd, dd, buf["m4"][:, :, None].to_broadcast([P, GS, P]), ALU.subtract))
                act.need(a)
                e = act.mark(nc.scalar.activation(dd, dd, ACT.Exp))
                dve.need(e)
                z = dve.mark(nc.vector.tensor_reduce(buf["z4"][:, :], dd, AX, ALU.add))
                t = c.transposes(1, [(P * s, buf["D"][:, s, :]) for s in range(GS)], ident, e)
                act.need(t)
                a = act.mark(nc.scalar.activation(buf["PT"][:, 0:GS, :].rearrange("p h k -> p (h k)"), c.ps[:, 1, :], ACT.Copy))
                c.bank_read[1] = a
                dve.need(z)
                z = dve.mark(nc.vector.reciprocal(buf["z4"][:, :], buf["z4"][:, :]))
                for s in range(GS):
                    b = 2 + s
                    r = project(c, b, [buf["PT"][:, s, :]], [v_all[:, s, :]], (a, v_ok))
                    dve.need(r, z)
                    x_in = dve.mark(nc.vector.scalar_tensor_tensor(out=xg[:, s, :], in0=c.ps[:, b, 0:D], scalar=buf["z4"][:, s:s + 1],
                                                                   in1=xg[:, s, :], op0=ALU.mult, op1=ALU.add))
                    c.bank_read[b] = x_in

            if STOP not in ("b", "c1", "c2"):
                u_ok, _ = layernorm(c, buf, xg, xn, xt, ident, x_in)
                h_ok = rms_rows(c, buf, xn, ao, 1e-5, u_ok, r)
                xt_ok = transpose_group(c, ao, xt, ident, h_ok, scale=cols[:, 2, :])
                for what in range(2):
                    for ch in range(KD):
                        plain = project(c, 2, [wf[:, 2 * what, k, P * ch:P * ch + P] for k in range(KD)], [xt[:, k, :] for k in range(KD)], (xt_ok,))
                        turned = project(c, 3, [wf[:, 2 * what + 1, k, P * ch:P * ch + P] for k in range(KD)], [xt[:, k, :] for k in range(KD)], (xt_ok,))
                        dst = qt[:, ch, :] if what == 0 else ct[:, ch, :]
                        by_seq = dst.rearrange("p (s l) -> p s l", l=P)
                        tmp = buf["D"][:, 0:GS, :]
                        dve.need(plain)
                        a = dve.mark(nc.vector.tensor_tensor(by_seq, c.ps[:, 2, :].rearrange("p (s l) -> p s l", l=P),
                                                             con["rope"][:, 2 * what, None, :].to_broadcast([P, GS, P]), ALU.mult))
                        c.bank_read[2] = a
                        dve.need(turned)
                        a = dve.mark(nc.vector.tensor_tensor(tmp, c.ps[:, 3, :].rearrange("p (s l) -> p s l", l=P),
                                                             con["rope"][:, 2 * what + 1, None, :].to_broadcast([P, GS, P]), ALU.mult))
                        c.bank_read[3] = a
                        dve.need(a)
                        q_ok = dve.mark(nc.vector.tensor_tensor(by_seq, by_seq, tmp, ALU.add))
                        dve.need(q_ok)
                        if what == 1:
                            act.need(q_ok)
                            for j in range(2):
                                k_ok = act.mark(nc.scalar.activation(kp[:, ch, j, :], ct[:, ch, :], ACT.Copy, scale=con["par"][:, j:j + 1]))

                def grouped_values(s, slot, free):
                    return token_values(s, slot, free, wv, 4 * HD, (xt_ok,), lambda v: act.mark(nc.scalar.activation(
                        buf["V"][:, v, :, 0:HD].rearrange("p (g r) e -> p g r e", r=4),
                        c.ps[:, 5, 0:4 * HD].rearrange("p (g e) -> p g e", e=HD)[:, :, None, :].to_broadcast([P, 4, 4, HD]), ACT.Copy)))

                attention(c, buf, con, qt, kp, grouped_values, to_ao, (q_ok, k_ok), mask=con["mask"])

                def add_u(s, b):
                    return dve.mark(nc.vector.tensor_tensor(xn[:, s, :], xn[:, s, :], c.ps[:, b, 0:D], ALU.add))

                u_ok = out_projection(done[0], wf[:, 4, :, :], add_u)
                dve.need(u_ok)
                x_in = dve.mark(nc.vector.tensor_tensor(xg[:, :, :], xg[:, :, :], xn[:, :, :], ALU.add))
                h_ok = rms_rows(c, buf, xn, ao, 1e-5, u_ok)
                xt_ok = transpose_group(c, ao, xt, ident, h_ok, scale=cols[:, 3, :])
                for s in range(GS):
                    b = 2 + s % 2
                    r = project(c, b, [xt[:, k, P * s:P * s + P] for k in range(KD)], [gw[:, k, :] for k in range(KD)], (xt_ok,))
                    dve.need(r)
                    lg = dve.mark(nc.vector.tensor_copy(buf["lg"][:, :], c.ps[:, b, 0:E1]))
                    c.bank_read[b] = lg
                    pos, w = top2(c, buf, con, E1, buf["lg"][:, :], lg, 4 + s % 2, s)
                    dve.need(pos, w)
                    a = dve.mark(nc.vector.scalar_tensor_tensor(out=buf["slot"][:, s, :], in0=buf["idx"][:, :], scalar=float(R1), in1=buf["pos"][:, :], op0=ALU.mult, op1=ALU.add))
                    dve.mark(nc.vector.tensor_copy(buf["cho"][:, s, :], buf["idx"][:, :]))
                    dve.mark(nc.vector.tensor_copy(buf["pla"][:, s, :], buf["pos"][:, :]))
                    wt = dve.mark(nc.vector.tensor_copy(buf["gwt"][:, s, :], buf["w"][:, :]))
                    pool.need(a, h_ok)
                    for k in range(2):
                        s_disp.mark(nc.gpsimd.indirect_dma_start(
                            out=dram["xd"], out_offset=bass.IndirectOffsetOnAxis(ap=buf["slot"][:, s, k:k + 1], axis=0),
                            in_=ao[:, s, :], in_offset=None))
                dve.need(wt, a)
                dve.mark(nc.vector.tensor_copy(persist["gwt"][:, bass.ds(i * GS, GS), :], buf["gwt"][:, :, :]))
                for name, part in (("choice", "cho"), ("place", "pla")):
                    dve.mark(nc.vector.tensor_copy(persist[name][:, bass.ds(i * GS, GS), :], buf[part][:, :, :]))
                nc.sync.wait_ge(s_disp.sem, (i + 1) * s_disp.count)
            act.need(x_in)
            act.mark(nc.scalar.activation(x_all[:, bass.ds(i * GS, GS), :], xg[:, :, :], ACT.Copy))
            c.new_epoch()
        gath.wait(pool, NG + 1)


def phase_d(c, con, dram, persist, w13, w_ready, out):
    nc, pe, dve, act, pool, sp = c.nc, c.pe, c.dve, c.act, c.pool, c.sp
    MF = F1 // P
    with ExitStack() as ctx:
        def sb(name, shape, dt=F32):
            return ctx.enter_context(nc.sbuf_tensor("d_" + name, shape, dt))

        w2 = sb("w2", [P, E1 * F1 // P, D])
        dconst = sb("dconst", [P, dram["dconst"].shape[1]])
        cols = sb("cols", [P, 4, KD])
        cnt = sb("cnt", [P, E1])
        tail = sb("tail", [P, E1], U32)
        cmp = sb("cmp", [P, NT1, 16])
        til = sb("til", [P, E1])
        end = sb("end", [P, E1])
        ej = sb("ej", [P, NT1])
        sj = sb("sj", [P, NT1])
        look = sb("look", [P, 2 * NSEQ, E1])
        base = sb("base", [P, 2 * NSEQ])
        row = sb("row", [P, NT1], I32)
        wex = sb("wex", [P, NT1], I32)
        xd = sb("xd", [P, ND, D])
        xt = sb("xt", [P, 2, KD, P])
        gs = sb("gs", [P, 2, F1])
        g = sb("g", [P, 2, F1])
        gt = sb("gt", [P, 2, MF, P])
        yd = sb("yd", [P, ND, D])
        k_tail, k_tile, k_upto, k_j, k_jrow = (dconst[:, a:b] for a, b in DCONST)
        s_c = c.stream("d_c")
        s_c.mark(nc.sync.dma_start(dconst[:, :], dram["dconst"]))
        m = s_c.mark(nc.sync.dma_start(cols[:, :, :], dram["cols"]))
        w2_in = c.stream("d_w2").mark(nc.sync.dma_start(w2[:, :, :], dram["w2d"]))
        pe.need(c.bank_read[0])
        r = pe.mark(nc.tensor.matmul(c.ps[:, 0, 0:E1], con["ones_bf"], persist["total"][:, :], start=True, stop=True))
        dve.need(r, m)
        a = dve.mark(nc.vector.tensor_copy(cnt[:, :], c.ps[:, 0, 0:E1]))
        dve.need(a)
        tl = dve.mark(nc.vector.tensor_tensor(tail[:, :], cnt[:, :], k_tail, ALU.add))
        pool.need(tl)
        s_tail = c.stream("d_tail", reset=False)
        for e in range(E1):
            t_in = s_tail.mark(nc.gpsimd.indirect_dma_start(
                out=dram["xd"], out_offset=bass.IndirectOffsetOnAxis(ap=tail[:, e:e + 1], axis=0),
                in_=con["zero"][:, 0:D], in_offset=None))
        pool.need(t_in)
        cv = cmp[:, 0:E1, :]
        a = dve.mark(nc.vector.tensor_tensor(cv, cnt[:, :, None].to_broadcast([P, E1, 16]), k_tile[:, None, :].to_broadcast([P, E1, 16]), ALU.is_gt))
        dve.need(a)
        a = dve.mark(nc.vector.tensor_reduce(til[:, :], cv, AX, ALU.add))
        dve.need(a)
        cv = cmp[:, 0:E1, 0:E1]
        a = dve.mark(nc.vector.tensor_tensor(cv, til[:, None, :].to_broadcast([P, E1, E1]), k_upto.rearrange("p (a b) -> p a b", a=E1), ALU.mult))
        dve.need(a)
        a = dve.mark(nc.vector.tensor_reduce(end[:, :], cv, AX, ALU.add))
        dve.need(a)
        flat = lambda t: t[:, :, :].rearrange("p s k -> p (s k)")
        dve.need(a)
        a = dve.mark(nc.vector.tensor_tensor(look[:, :, :], flat(persist["choice"])[:, :, None].to_broadcast([P, 2 * NSEQ, E1]),
                                             con["iota"][:, None, 0:E1].to_broadcast([P, 2 * NSEQ, E1]), ALU.is_equal))
        a = dve.mark(nc.vector.tensor_tensor(ej[:, 0:E1], end[:, :], til[:, :], ALU.subtract))
        dve.need(a)
        a = dve.mark(nc.vector.tensor_tensor(look[:, :, :], look[:, :, :], ej[:, None, 0:E1].to_broadcast([P, 2 * NSEQ, E1]), ALU.mult))
        dve.need(a)
        a = dve.mark(nc.vector.tensor_reduce(base[:, :], look[:, :, :], AX, ALU.add))
        dve.need(a)
        a = dve.mark(nc.vector.scalar_tensor_tensor(out=flat(persist["gidx"])[:, 0:2 * NSEQ], in0=base[:, :], scalar=float(P),
                                                    in1=flat(persist["place"]), op0=ALU.mult, op1=ALU.add))
        cv = cmp[:, :, 0:E1]
        a = dve.mark(nc.vector.tensor_tensor(cv, end[:, None, :].to_broadcast([P, NT1, E1]), k_j[:, :, None].to_broadcast([P, NT1, E1]), ALU.is_le))
        dve.need(a)
        a = dve.mark(nc.vector.tensor_reduce(ej[:, :], cv, AX, ALU.add))
        a = dve.mark(nc.vector.tensor_tensor(cv, cv, til[:, None, :].to_broadcast([P, NT1, E1]), ALU.mult))
        dve.need(a)
        a = dve.mark(nc.vector.tensor_reduce(sj[:, :], cv, AX, ALU.add))
        dve.need(a)
        a = dve.mark(nc.vector.scalar_tensor_tensor(out=sj[:, :], in0=sj[:, :], scalar=-float(P), in1=k_jrow, op0=ALU.mult, op1=ALU.add))
        dve.need(a)
        a = dve.mark(nc.vector.scalar_tensor_tensor(out=row[:, :], in0=ej[:, :], scalar=float(R1), in1=sj[:, :], op0=ALU.mult, op1=ALU.add))
        a = dve.mark(nc.vector.tensor_scalar(wex[:, :], ej[:, :], float(E1 - 1), None, ALU.min))
        pe.need(w_ready, w2_in)
        c.new_epoch()

        s_x, s_y = c.stream("d_x"), c.stream("d_y")
        with nc.Fori(0, NT1 // ND) as i:
            at = [sp.eng.value_load(row[0:1, bass.ds(i * ND + n, 1)], min_val=0, max_val=E1 * R1 + 7 * P) for n in range(ND)]
            x_in = [s_x.mark(nc.sync.dma_start(xd[:, n, :], dram["xd"][bass.ds(at[n], P), :])) for n in range(ND)]
            x_in = [x_in[-1]] * ND
            xt_ok, up_ok, g_ok, gt_ok, dn_ok, gt_tr = ([None] * ND for _ in range(6))

            def turn_in(n):
                b = 6
                pe.need(x_in[n], c.bank_read[b])
                for k in range(KD):
                    t = nc.tensor.transpose(c.ps[:, b, P * k:P * k + P], xd[:, n, P * k:P * k + P], con["ident"])
                t = pe.mark(t)
                act.need(t, up_ok[n - 2] if n >= 2 else None)
                for k in range(KD):
                    a = act.mark(nc.scalar.activation(xt[:, n % 2, k, :], c.ps[:, b, P * k:P * k + P], ACT.Copy, scale=cols[:, 3, k:k + 1]))
                c.bank_read[b] = a
                xt_ok[n] = a

            def up(n):
                e = pe.eng.value_load(wex[0:1, bass.ds(i * ND + n, 1)], min_val=0, max_val=E1 - 1)
                for half in range(2):
                    b = 2 * (n % 2) + half
                    pe.need(xt_ok[n], c.bank_read[b])
                    for k in range(KD):
                        ins = nc.tensor.matmul(c.ps[:, b, :], xt[:, n % 2, k, :], w13[:, bass.ds(e * (2 * KD) + 2 * k + half, 1), :],
                                               start=(k == 0), stop=(k == KD - 1))
                    r = pe.mark(ins)
                    if half == 0:
                        act.need(r)
                        a = act.mark(nc.scalar.activation(gs[:, n % 2, :], c.ps[:, b, :], ACT.Silu))
                        c.bank_read[b] = a
                    else:
                        dve.need(r, a, gt_tr[n - 2] if n >= 2 else None)
                        g_ok[n] = dve.mark(nc.vector.tensor_tensor(g[:, n % 2, :], gs[:, n % 2, :], c.ps[:, b, :], ALU.mult))
                        c.bank_read[b] = g_ok[n]
                up_ok[n] = r
                return e

            def turn_hidden(n):
                t = c.transposes(4, [(P * m, g[:, n % 2, P * m:P * m + P]) for m in range(MF)], con["ident"], g_ok[n])
                gt_tr[n] = t
                dve.need(t, dn_ok[n - 2] if n >= 2 else None)
                gt_ok[n] = dve.mark(nc.vector.tensor_copy(gt[:, n % 2, :, :].rearrange("p m t -> p (m t)"), c.ps[:, 4, :]))
                c.bank_read[4] = gt_ok[n]

            def down(n, e):
                pe.need(gt_ok[n], c.bank_read[5])
                for m in range(MF):
                    ins = nc.tensor.matmul(c.ps[:, 5, 0:D], gt[:, n % 2, m, :], w2[:, bass.ds(e * MF + m, 1), :], start=(m == 0), stop=(m == MF - 1))
                dn_ok[n] = pe.mark(ins)
                dve.need(dn_ok[n])
                a = dve.mark(nc.vector.tensor_copy(yd[:, n, :], c.ps[:, 5, 0:D]))
                c.bank_read[5] = a
                sp.need(a)
                s_y.mark(nc.sync.dma_start(dram["yd"][bass.ds((i * ND + n) * P, P), :], yd[:, n, :]))

            es = [None] * ND
            turn_in(0)
            es[0] = up(0)
            turn_in(1)
            for n in range(ND):
                if n + 1 < ND:
                    es[n + 1] = up(n + 1)
                turn_hidden(n)
                if n + 2 < ND:
                    turn_in(n + 2)
                down(n, es[n])
            c.new_epoch()

        gath = Gathers(c, sb, persist, dram["yd"], "d")
        xo = sb("xo", [P, GS, D])
        gwl = sb("gwl", [P, GS, 2])
        s_o = c.stream("out")
        gath.fetch(0, None)
        c.new_epoch()
        with nc.Fori(0, NG) as i:
            a = act.mark(nc.scalar.activation(gwl[:, :, :], persist["gwt"][:, bass.ds(i * GS, GS), :], ACT.Copy))
            a = act.mark(nc.scalar.activation(xo[:, :, :], persist["x"][:, bass.ds(i * GS, GS), :], ACT.Copy))
            dve.need(a)
            gath.wait(dve, i + 1)
            for k in range(2):
                for s in range(GS):
                    a = dve.mark(nc.vector.scalar_tensor_tensor(out=xo[:, s, :], in0=gath.rows[:, s, k, :], scalar=gwl[:, s, k:k + 1],
                                                                in1=xo[:, s, :], op0=ALU.mult, op1=ALU.add))
                dve.need(a)
            gath.fetch(i + 1, a)
            sp.need(a)
            s_o.mark(nc.sync.dma_start(out.rearrange("s l d -> l s d")[:, bass.ds(i * GS, GS), :], xo[:, :, :]))
            c.new_epoch()
        gath.wait(pool, NG + 1)


def build(nc, dram, out, stop=STOP):
    for name, n in (("xe", E0 * CAP), ("ye", E0 * CAP), ("xd", E1 * R1 + E1 * P), ("yd", NT1 * P)):
        dram[name] = nc.dram_tensor(name, (n, D), F32, kind="Internal").ap()
    with ExitStack() as ctx:
        c = Core(nc, ctx)
        dve, pool, pe, act = c.dve, c.pool, c.pe, c.act

        def sb(name, shape, dt=F32):
            return ctx.enter_context(nc.sbuf_tensor(name, shape, dt))

        cf = sb("cf", [P, dram["cf"].shape[1]])
        cb = sb("cb", [P, dram["cb"].shape[1]], BF16)
        persist = {"x": sb("x_all", [P, NSEQ, D]), "gidx": sb("gidx_all", [P, NSEQ + GS, 2], U32),
                   "gwt": sb("gwt_all", [P, NSEQ, 2]), "total": sb("total1", [P, E1], BF16), "choice": sb("choice", [P, NSEQ, 2]),
                   "place": sb("place", [P, NSEQ, 2])}
        con = {"ident": cf[:, 0:128], "par": cf[:, 128:130], "iota": cf[:, 130:162], "mhalf": cf[:, 162:166],
               "ones": cf[:, 166:294], "rope": cf[:, 294:806].rearrange("p (n l) -> p n l", l=P), "ident_bf": cb[:, 0:128], "mask": cb[:, 128:640],
               "before_bf": cb[:, 640:768], "ones_bf": cb[:, 768:896]}
        zero = sb("zero", [P, 512])
        s_in = c.stream("in")
        with nc.sbuf_tensor("cb_f32", list(dram["cb"].shape), F32) as cb_f32:
            s_in.mark(nc.sync.dma_start(cf[:, :], dram["cf"]))
            m = s_in.mark(nc.sync.dma_start(cb_f32[:, :], dram["cb"]))
            dve.need(m)
            c.sp.need(dve.mark(nc.vector.tensor_copy(cb[:, :], cb_f32[:, :])))
        m = s_in.mark(nc.sync.dma_start(persist["x"][:, :, :], dram["x"]))
        for lane in (pe, dve, act, pool):
            lane.need(m)
        zm = dve.mark(nc.vector.memset(zero[:, 0:512], 0.0))
        c.sp.need(zm)
        s_zero = c.stream("zero")
        per = E0 * CAP * D // P
        xe_flat = dram["xe"].rearrange("r d -> (r d)").rearrange("(p e) -> p e", p=P)
        n = per // 512
        c.sp.need(s_zero.mark(nc.sync.dma_start(xe_flat[:, 0:n * 512].rearrange("p (n e) -> p n e", e=512),
                                 zero[:, None, :].to_broadcast([P, n, 512]))))
        if per % 512:
            c.sp.need(s_zero.mark(nc.sync.dma_start(xe_flat[:, n * 512:per], zero[:, 0:per % 512])))
        xd_tail = dram["xd"][E1 * R1:, :].rearrange("(p r) d -> p (r d)", p=P)
        c.sp.need(s_zero.mark(nc.sync.dma_start(xd_tail.rearrange("p (n e) -> p n e", e=512), zero[:, None, :].to_broadcast([P, 4, 512]))))
        con["zero"] = zero
        gz = dve.mark(nc.vector.memset(persist["gidx"][:, NSEQ:, :], 0))
        with ExitStack() as stack:
            ring = (stack.enter_context(nc.sbuf_tensor("ring1", [P, RING, KD, F0], F32)),
                    stack.enter_context(nc.sbuf_tensor("ring2", [P, RING, F0 // P, D], F32)))
            s_ring = [c.stream("ring%d" % n, reset=False) for n in range(RING)]
            for n in range(RING):
                load_expert(c, dram, ring, s_ring, n, n)
            phase_a(c, con, dram, persist)
            if stop != "a":
                phase_b(c, con, dram, ring, s_ring)
        if stop != "a":
            with ExitStack() as stack:
                w13 = stack.enter_context(nc.sbuf_tensor("w13", [P, E1 * KD * 2, F1], F32))
                s_w = c.stream("w_d", reset=False)
                w_ready = s_w.mark(nc.sync.dma_start(w13[:, :, :], dram["w13"]))
                phase_c(c, con, dram, persist)
                if stop is None:
                    phase_d(c, con, dram, persist, w13, w_ready, out)
        if stop is not None:
            s = c.stream("o")
            c.sp.need(s.mark(nc.sync.dma_start(out.rearrange("s l d -> l s d"), persist["x"][:, :, :])))


def constants():
    p = np.arange(P)
    par = np.stack([(p // HD) % 2 == j for j in range(2)], 1).astype(np.float32)
    cf = np.concatenate([np.eye(P), par, np.tile(np.arange(E0), (P, 1)), np.full((P, GS), -0.5),
                         np.ones((P, P))], 1).astype(np.float32)
    freq = (1.0 / np.float32(10000.0) ** (np.arange(0, HD, 2, dtype=np.float32) / HD)).astype(np.float32)
    ang = (np.arange(P, dtype=np.float32)[:, None] * freq[None, :]).astype(np.float32)
    ang = np.tile(np.concatenate([ang, ang], 1).T, (P // HD, 1))
    sign = np.where(p % HD < HD // 2, -1.0, 1.0)[:, None]
    cos, sin = np.cos(ang), np.sin(ang) * sign
    cf = np.concatenate([cf, cos * HD ** -0.5, sin * HD ** -0.5, cos, sin], 1).astype(np.float32)
    e8, j = np.arange(E1), np.arange(NT1)
    dconst = np.concatenate([p[:, None] + R1 * e8[None, :]] + [np.tile(v.reshape(1, -1), (P, 1)) for v in (
        P * np.arange(16), e8[None, :] <= e8[:, None], j, P * j)], 1).astype(np.float32)
    causal = np.where(p[None, :] > p[:, None], NEG, 0.0)
    cb = np.concatenate([np.eye(P), np.tile(causal, (1, 4)), (p[:, None] < p[None, :]).astype(np.float32), np.ones((P, P))], 1).astype(np.float32)
    return {"cf": cf, "cb": cb, "dconst": dconst}


def layouts(x):
    def chunks(w):
        return np.ascontiguousarray(w.reshape(-1, P, w.shape[1]).transpose(1, 0, 2))

    a = {}
    a["x"] = np.ascontiguousarray(x["x"].transpose(1, 0, 2))
    a["ctx_t"] = chunks(x["ctx_1024"].reshape(NSEQ * P, D).T)
    a["win"] = chunks(x["L0_attn_W_in"].T)
    w = x["L0_attn_W_xproj"].T
    pad = np.zeros((DI, 16), w.dtype)
    a["wx"] = chunks(np.concatenate([w[:, :16], pad, w[:, 16:32], pad, w[:, 32:]], 1))
    a["wo"] = chunks(x["L0_attn_W_out"].T)
    a["conv"] = chunks(np.concatenate([x["L0_attn_conv_w"], x["L0_attn_conv_b"][:, None]], 1))
    a["dvec"] = np.ascontiguousarray(x["L0_attn_D"].reshape(KI, P).T)
    bd = np.zeros((P, 3, P), np.float32)
    for n, name in enumerate(("L0_xattn_Wq", "L0_xattn_Wk", "L0_xattn_Wv")):
        for h in range(P // HD):
            bd[HD * h:HD * h + HD, n, HD * h:HD * h + HD] = x[name].T
    a["bd"] = bd
    a["gw"] = chunks(x["L0_ffn_gate_w"])
    a["gb"] = x["L0_ffn_gate_b"]
    a["w1"], a["w2"] = x["L0_ffn_w1"], x["L0_ffn_w2"]
    a["b1"] = np.ascontiguousarray(x["L0_ffn_b1"].reshape(E0, P, F0 // P).transpose(1, 0, 2))
    a["b2"] = np.ascontiguousarray(x["L0_ffn_b2"].reshape(E0, KD, P).transpose(2, 0, 1))
    stack = lambda ws: np.ascontiguousarray(np.stack([chunks(w) for w in ws], 1))
    a["wa"] = stack([x["L1_attn_W" + n].T for n in "qkvo"])
    a["wc"] = stack([x["L1_xattn_W" + n].T for n in "qkv"])
    qkv = x["L1_ffn_wqkv"]
    swap = np.arange(D).reshape(-1, 2, HD // 2)[:, ::-1].reshape(-1)
    q = qkv[:D]
    kv = HD * (NH // 4)
    k = np.repeat(qkv[D:D + kv].reshape(4, HD, D), 4, axis=0).reshape(D, D)
    a["wf"] = stack([q.T, q[swap].T, k.T, k[swap].T, x["L1_ffn_wo"].T])
    a["wv"] = chunks(qkv[D + kv:].T)
    a["gw1"] = chunks(x["L1_ffn_gate_w"].T)
    col = lambda v: v.reshape(KD, P).T
    a["cols"] = np.ascontiguousarray(np.stack([col(x[n]) for n in ("L1_xattn_bq", "L1_xattn_bk", "L1_ffn_ln1_w", "L1_ffn_ln2_w")], 1))
    a["bo"], a["bv"] = x["L1_attn_bo"], x["L1_xattn_bv"]
    for n, name in enumerate(("risk", "prio", "impl")):
        a["beta%d" % n] = np.asarray(x["L1_xattn_beta_" + name]).reshape(1)
    a["phi"] = np.ascontiguousarray(x["fside_BxSxS2_0"].transpose(1, 0, 2))
    w13 = x["L1_ffn_w13"].reshape(E1, 2, F1, KD, P)
    a["w13"] = np.ascontiguousarray(w13.transpose(4, 0, 3, 1, 2).reshape(P, E1 * KD * 2, F1))
    w2 = x["L1_ffn_w2"].reshape(E1, D, F1 // P, P)
    a["w2d"] = np.ascontiguousarray(w2.transpose(3, 0, 2, 1).reshape(P, E1 * F1 // P, D))
    return a


def kernel(**inputs):
    import concourse.bacc as bacc
    from concourse.bass_utils import run_bass_kernel_spmd

    nc = bacc.Bacc("TRN2", target_bir_lowering=False, num_devices=1)
    arrays = {"in_" + k: v for k, v in {**layouts({k: np.asarray(v) for k, v in inputs.items()}), **constants()}.items()}
    dram = {k[3:]: nc.dram_tensor(k, v.shape, mybir.dt.from_np(v.dtype), kind="ExternalInput").ap() for k, v in arrays.items()}
    out = nc.dram_tensor("out_dram", (NSEQ, P, D), F32, kind="ExternalOutput").ap()
    build(nc, dram, out)
    r = run_bass_kernel_spmd(nc, [arrays], core_ids=[0])
    return r.results[0]["out_dram"]
```

```python
from contextlib import ExitStack

import numpy as np
import concourse.bass as bass
from concourse import mybir

F32 = mybir.dt.float32
BF16 = mybir.dt.bfloat16
I32 = mybir.dt.int32
U32 = mybir.dt.uint32
ALU = mybir.AluOpType
ACT = mybir.ActivationFunctionType
AX = mybir.AxisListType.X

P = 128
NSEQ = 16
D = 256
KD = D // P
NTH = 2
GS = 2
GT = GS * P
RS = NTH * GS
RT = RS * P
NROUND = NSEQ // RS
NBANK = 8 // NTH
NU = 8
NH, HD = 16, 16
DI = 512
KI = DI // P
DSTATE = 16
E0, F0 = 32, 1024
CAP = 154
E1, F1 = 8, 512
R1 = NSEQ * P + P
NT1 = NSEQ * P * 2 // P + E1
NEG = -1.0e30
LN_EXP = "natural_log_exp_and_others"
POLY = [-0.037, 0.481, -2.3, 4.917, -1.791]
RING = 4
NB = 8
ND = 8
DCONST = [(0, 8), (8, 24), (24, 88), (88, 88 + NT1), (88 + NT1, 88 + 2 * NT1)]
STOP = None


class Lane:

    def __init__(self, eng, sem, step=1):
        self.eng, self.sem, self.step, self.count, self.seen = eng, sem, step, 0, {}

    def mark(self, ins):
        self.count += self.step
        ins.then_inc(self.sem, self.step)
        return (self, self.count)

    def need(self, *marks):
        for m in marks:
            if m is not None and self.seen.get(m[0], 0) < m[1]:
                self.eng.wait_ge(m[0].sem, m[1])
                self.seen[m[0]] = m[1]


class Core:

    def __init__(self, nc, ctx):
        self.nc, self.ctx = nc, ctx
        self.pe = Lane(nc.tensor, self.sem("pe"))
        self.dve = Lane(nc.vector, self.sem("dve"))
        self.act = Lane(nc.scalar, self.sem("act"))
        self.pool = Lane(nc.gpsimd, self.sem("pool"))
        self.sp = Lane(nc.sync, self.sem("sp"))
        self.lanes = [self.pe, self.dve, self.act, self.pool, self.sp]
        self.streams = []
        self.ps = ctx.enter_context(nc.psum_tensor("ps", [P, 8, 512], F32))
        self.bank_read = [None] * 8

    def sem(self, name):
        return self.ctx.enter_context(self.nc.semaphore("s_" + name))

    def stream(self, name, reset=True):
        s = Lane(None, self.sem(name), 16)
        if reset:
            self.streams.append(s)
        return s

    def new_epoch(self):
        for lane in self.lanes:
            lane.need((lane, lane.count))
        for s in self.streams:
            self.sp.need((s, s.count))
        self.nc.all_engine_barrier()
        for x in self.lanes + self.streams:
            if x.count:
                self.nc.sync.sem_clear(x.sem)
            x.count = 0
        for x in self.lanes:
            x.seen = {}
        self.bank_read = [None] * 8
        self.nc.all_engine_barrier()

    def transposes(self, bank, pairs, ident, *marks):
        self.pe.need(self.bank_read[bank], *marks)
        for col, src in pairs:
            n = src.shape[0]
            ins = self.nc.tensor.transpose(self.ps[0:src.shape[1], bank, col:col + n], src, ident[0:n, 0:n])
        return self.pe.mark(ins)

    def products(self, bank, parts, *marks):
        self.pe.need(self.bank_read[bank], *marks)
        for col, w, x in parts:
            for k in range(len(w)):
                out = self.ps[0:w[k].shape[-1], bank, col:col + x[k].shape[-1]]
                ins = self.nc.tensor.matmul(out, w[k], x[k], start=(k == 0), stop=(k == len(w) - 1), skip_group_check=True)
        return self.pe.mark(ins)


def alternate(threads):
    threads = list(threads)
    while threads:
        for t in list(threads):
            try:
                next(t)
            except StopIteration:
                threads.remove(t)


class Thread:

    def __init__(self, n, nc, ctx, prefix):
        self.n, self.nc, self.ctx, self.prefix = n, nc, ctx, prefix
        self.banks = [NBANK * n + b for b in range(NBANK)]
        self.seqs = slice(GS * n, GS * n + GS)
        self.tok = slice(GT * n, GT * n + GT)

    def sb(self, name, shape, dt=F32, ctx=None):
        return (ctx or self.ctx).enter_context(self.nc.sbuf_tensor(self.prefix + name + str(self.n), shape, dt))

    def common(self):
        self.xg = self.sb("xg", [P, GS, D])
        self.xn = self.sb("xn", [P, GS, D])
        self.xt = self.sb("xt", [P, KD, GT])
        self.st, self.mv = self.sb("st", [P, GS, 6]), self.sb("mv", [P, GS, 2])
        self.ve, self.rs, self.r2, self.ss = (self.sb(x, [P, GS]) for x in ("ve", "rs", "r2", "ss"))
        self.ao = self.sb("ao", [P, GS, D])

    def for_attention(self, ctx):
        sb = lambda name, shape: self.sb(name, shape, F32, ctx)
        self.qt, self.kp = sb("qt", [P, KD, GT]), sb("kp", [P, KD, 4, GT])
        self.dd = [sb("da", [P, NU, P]), sb("db", [P, NU, P])]
        self.pt, self.vv = sb("pt", [P, NU, P]), sb("vv", [P, 2, NH, 32])
        self.os = sb("os", [P, GT])
        self.mx = [sb("mxa", [P, NU]), sb("mxb", [P, NU])]
        self.rz = sb("rz", [P, NU])


def layernorm(c, t, con, x_ready, xn_free=None, want_t=True, out=None):
    nc, dve = c.nc, c.dve
    out = t.xn if out is None else out
    dve.need(x_ready, xn_free)
    for s in range(GS):
        m = dve.mark(nc.vector.bn_stats(t.st[:, s, :], t.xg[:, s, :]))
    dve.need(m)
    for s in range(GS):
        m = dve.mark(nc.vector.bn_aggr(t.mv[:, s, :], t.st[:, s, :]))
    dve.need(m)
    m = dve.mark(nc.vector.tensor_scalar(t.ve[:, :], t.mv[:, :, 1], 1e-5, None, ALU.add))
    m = yield from inverse_root(c, t, m)
    dve.need(m)
    for s in range(GS):
        n = dve.mark(nc.vector.tensor_scalar(out[:, s, :], t.xg[:, s, :], t.mv[:, s, 0:1], t.rs[:, s:s + 1],
                                             ALU.subtract, ALU.mult))
    if not want_t:
        return n, None
    yield
    return n, (yield from transpose_rows(c, t, con, out, n))


def inverse_root(c, t, ready):
    nc, dve, act = c.nc, c.dve, c.act
    ve, rs, r2 = t.ve[:, :], t.rs[:, :], t.r2[:, :]
    act.need(ready)
    m = act.mark(nc.scalar.activation(rs, ve, ACT.Ln))
    act.need(m)
    m = act.mark(nc.scalar.activation(rs, rs, ACT.Exp, scale=-0.5))
    yield
    dve.need(m)
    m = dve.mark(nc.vector.tensor_tensor(r2, rs, rs, ALU.mult))
    dve.need(m)
    m = dve.mark(nc.vector.tensor_tensor(r2, r2, ve, ALU.mult))
    dve.need(m)
    m = dve.mark(nc.vector.tensor_scalar(r2, r2, -0.5, 1.5, ALU.mult, ALU.add))
    dve.need(m)
    return dve.mark(nc.vector.tensor_tensor(rs, rs, r2, ALU.mult))


def transpose_rows(c, t, con, x, ready, scale=None):
    nc, act = c.nc, c.act
    b = t.banks[0]
    m = c.transposes(b, [(GT * k + P * s, x[:, s, P * k:P * k + P]) for k in range(KD) for s in range(GS)], con["ident"], ready)
    act.need(m)
    if scale is None:
        m = act.mark(nc.scalar.activation(t.xt[:, :, :], c.ps[:, b, :], ACT.Copy))
    else:
        for k in range(KD):
            m = act.mark(nc.scalar.activation(t.xt[:, k, :], c.ps[:, b, GT * k:GT * k + GT], ACT.Copy, scale=scale[:, k:k + 1]))
    c.bank_read[b] = m
    yield
    return m


def by_channel(c, bank, w, x, ready):
    return c.products(bank, [(GT * ch, [w[:, k, P * ch:P * ch + P] for k in range(KD)], [x[:, k, :] for k in range(KD)])
                             for ch in range(KD)], *ready)


def by_token(c, bank, w, x, ready):
    n = w.shape[-1]
    return c.products(bank, [(n * s, [x[:, k, P * s:P * s + P] for k in range(w.shape[1])], [w[:, k, :] for k in range(w.shape[1])])
                             for s in range(GS)], *ready)


def head_keys(c, kp, src, par, mark):
    nc, act = c.nc, c.act
    act.need(mark)
    for j in range(4):
        m = act.mark(nc.scalar.activation(kp[:, :, j, :], src.rearrange("p (c t) -> p c t", c=KD), ACT.Copy, scale=par[:, j:j + 1]))
    return m


def attention(c, t, con, make_v, ready, mask=None, temperature=None):
    nc, pe, dve, act = c.nc, c.pe, c.dve, c.act
    sa, sb_, pb, ob = t.banks
    units = [(s, ch) for s in range(GS) for ch in range(KD)]
    view = c.ps[:, sa:sa + 2, :].rearrange("p b (h k) -> p (b h) k", k=P)
    pt_free, os_free, v_free = None, None, [None] * GS
    d_free = [None, None]

    def scores(u):
        s, ch = units[u]
        tok = slice(P * s, P * s + P)
        pe.need(*ready, c.bank_read[sa], c.bank_read[sb_])
        if mask is not None:
            for b in (sa, sb_):
                nc.tensor.matmul(c.ps[:, b, :], con["ident_bf"], mask, start=True, stop=True, skip_group_check=True)
        for b in range(2):
            ins = nc.tensor.matmul(c.ps[:, (sa, sb_)[b], :], t.qt[64 * b:64 * b + 64, ch, tok],
                                   t.kp[64 * b:64 * b + 64, ch, :, tok], start=(mask is None), stop=True,
                                   tile_position=(64 * b, 0), skip_group_check=True)
        return pe.mark(ins)

    def less_maximum(u, m_scores):
        d, mx = t.dd[u % 2], t.mx[u % 2]
        dve.need(m_scores, d_free[u % 2])
        m = dve.mark(nc.vector.tensor_reduce(mx[:, :], view, AX, ALU.max))
        dve.need(m)
        m = dve.mark(nc.vector.tensor_tensor(d[:, :, :], view, mx[:, :, None].to_broadcast([P, NU, P]), ALU.subtract))
        c.bank_read[sa] = c.bank_read[sb_] = m
        return m

    def exponentials(u, m):
        d = t.dd[u % 2]
        if temperature is not None:
            m = yield from temperature(d, m)
        act.need(m)
        return act.mark(nc.scalar.activation(d[:, :, :], d[:, :, :], ACT.Exp))

    v = [make_v(0), None]
    m = scores(0)
    yield
    m = less_maximum(0, m)
    e = yield from exponentials(0, m)
    yield
    for u, (s, ch) in enumerate(units):
        more = u + 1 < len(units)
        if more:
            if ch == KD - 1:
                v[1] = make_v(s + 1)
            m = scores(u + 1)
            yield
        d = t.dd[u % 2]
        for q in range(2):
            tr = c.transposes(pb, [(P * n, d[:, 4 * q + n, :]) for n in range(4)], con["ident"], e)
            act.need(tr, pt_free)
            cp = act.mark(nc.scalar.activation(t.pt[:, 4 * q:4 * q + 4, :].rearrange("p h k -> p (h k)"), c.ps[:, pb, :], ACT.Copy))
            c.bank_read[pb] = cp
            yield
        d_free[u % 2] = tr
        if more:
            m = less_maximum(u + 1, m)
        pe.need(cp, v[0], c.bank_read[ob])
        for n in range(NU):
            r, at = n % 4, n // 4
            ins = nc.tensor.matmul(c.ps[32 * r:32 * r + 32, ob, P * at:P * at + P], t.vv[:, s % 2, NU * ch + n, :],
                                   t.pt[:, n, :], start=True, stop=True, tile_position=(0, 32 * r), skip_group_check=True)
        pt_free = pe.mark(ins)
        act.need(pt_free, os_free)
        m_os = act.mark(nc.scalar.activation(t.os[:, :], c.ps[:, ob, 0:GT], ACT.Copy))
        c.bank_read[ob] = m_os
        yield
        if more:
            e = yield from exponentials(u + 1, m)
        os_free = c.transposes(ob, [(P * at, t.os[:, P * at:P * at + P]) for at in range(2)], con["ident"], m_os)
        ot = c.ps[:, ob, 0:GT].rearrange("p (h e) -> p h e", e=32)
        dve.need(os_free)
        m_r = dve.mark(nc.vector.reciprocal(t.rz[:, :], ot[:, :, HD]))
        dve.need(m_r)
        done = dve.mark(nc.vector.tensor_tensor(t.ao[:, s, P * ch:P * ch + P].rearrange("p (h e) -> p h e", e=HD), ot[:, :, 0:HD],
                                                t.rz[:, :, None].to_broadcast([P, NU, HD]), ALU.mult))
        c.bank_read[ob] = done
        if ch == KD - 1:
            v[0] = v[1]
        yield
    return done


class Router:

    def __init__(self, c, ctx, con, prefix, n_exp):
        def sb(name, shape, dt=F32):
            return ctx.enter_context(c.nc.sbuf_tensor(prefix + name, shape, dt))
        self.c, self.con, self.n_exp = c, con, n_exp
        self.lg = sb("lg", [P, RS, n_exp])
        self.m8, self.i8 = sb("m8", [P, RS, 8]), sb("i8", [P, RS, 8], U32)
        self.gap, self.den = sb("gap", [P, RS]), sb("den", [P, RS])
        self.idx, self.w, self.pos = sb("idx", [P, RS, 2]), sb("w", [P, RS, 2]), sb("pos", [P, RS, 2])
        self.oh, self.pr = sb("oh", [P, RS, 2, n_exp]), sb("pr", [P, RS, 2, n_exp])
        self.ohs = sb("ohs", [P, RS, n_exp], BF16)

    def run(self, ready, total):
        c, nc, con, n_exp = self.c, self.c.nc, self.con, self.n_exp
        pe, dve, act = c.pe, c.dve, c.act
        dve.need(ready)
        for s in range(RS):
            m = dve.mark(nc.vector.max(out=self.m8[:, s, :], in_=self.lg[:, s, :]))
        dve.need(m)
        for s in range(RS):
            i = dve.mark(nc.vector.max_index(out=self.i8[:, s, :], in_max=self.m8[:, s, :], in_values=self.lg[:, s, :]))
        m = dve.mark(nc.vector.tensor_tensor(self.gap[:, :], self.m8[:, :, 1], self.m8[:, :, 0], ALU.subtract))
        act.need(m)
        ex = act.mark(nc.scalar.activation(self.gap[:, :], self.gap[:, :], ACT.Exp))
        dve.need(i)
        m = dve.mark(nc.vector.tensor_copy(self.idx[:, :, :], self.i8[:, :, 0:2]))
        dve.need(m)
        iota = con["iota"][:, None, 0:n_exp].to_broadcast([P, 2 * RS, n_exp])
        oh = self.oh[:, :, :, :].rearrange("p s k e -> p (s k) e")
        pr = self.pr[:, :, :, :].rearrange("p s k e -> p (s k) e")
        idx = self.idx[:, :, :].rearrange("p s k -> p (s k)")
        m = dve.mark(nc.vector.tensor_tensor(oh, iota, idx[:, :, None].to_broadcast([P, 2 * RS, n_exp]), ALU.is_equal))
        dve.need(m)
        m = dve.mark(nc.vector.tensor_tensor(self.ohs[:, :, :], self.oh[:, :, 0, :], self.oh[:, :, 1, :], ALU.add))
        b = 7
        pe.need(m, c.bank_read[b])
        for s in range(RS):
            at = c.ps[:, b, n_exp * s:n_exp * s + n_exp]
            nc.tensor.matmul(at, con["before_bf"], self.ohs[:, s, :], start=True, stop=False, skip_group_check=True)
            for q in range(s):
                nc.tensor.matmul(at, con["ones_bf"], self.ohs[:, q, :], start=False, stop=False, skip_group_check=True)
            ins = nc.tensor.matmul(at, con["ones_bf"], total, start=False, stop=True, skip_group_check=True)
        places = pe.mark(ins)
        dve.need(ex)
        m = dve.mark(nc.vector.tensor_scalar(self.den[:, :], self.gap[:, :], 1.0, None, ALU.add))
        dve.need(m)
        m = dve.mark(nc.vector.reciprocal(self.w[:, :, 0], self.den[:, :]))
        dve.need(m)
        w = dve.mark(nc.vector.tensor_tensor(self.w[:, :, 1], self.gap[:, :], self.w[:, :, 0], ALU.mult))
        dve.need(places)
        by = c.ps[:, b, 0:RS * n_exp].rearrange("p (s e) -> p s e", e=n_exp)
        for k in range(2):
            m = dve.mark(nc.vector.tensor_tensor(self.pr[:, :, k, :], self.oh[:, :, k, :], by, ALU.mult))
        c.bank_read[b] = m
        for s in range(RS):
            dve.mark(nc.vector.tensor_tensor(total, total, self.ohs[:, s, :], ALU.add))
            dve.need((dve, dve.count))
        pos = dve.mark(nc.vector.tensor_reduce(self.pos[:, :, :].rearrange("p s k -> p (s k)"), pr, AX, ALU.add))
        return pos, w


def phase_a(c, con, dram, persist, s_zero, load_ahead):
    nc, pe, dve, act, pool, sp = c.nc, c.pe, c.dve, c.act, c.pool, c.sp
    with ExitStack() as ctx:
        def sb(name, shape, dt=F32):
            return ctx.enter_context(nc.sbuf_tensor("a_" + name, shape, dt))

        win = sb("win", [P, KD, 2 * DI])
        wx = sb("wx", [P, KI, 64 + DI])
        wo = sb("wo", [P, KI, D])
        conv = sb("conv", [P, KI, 5])
        dvec = sb("dvec", [P, KI])
        bd = sb("bd", [P, 3, P])
        gw = sb("gw", [P, KD, E0])
        gb = sb("gb", [P, E0])
        total = sb("total", [P, E0], BF16)
        ct = sb("ct", [P, KD, RT])
        over, clip, sidx = (sb(x, [P, RS, 2]) for x in ("over", "clip", "sidx"))
        slot, gidx = sb("slot", [P, RS, 2], U32), sb("gidx", [P, RS, 2], U32)
        gwt = sb("gwt", [P, RS, 2])
        router = Router(c, ctx, con, "a_", E0)
        threads = [Thread(n, nc, ctx, "a_") for n in range(NTH)]
        for t in threads:
            t.common()

        w_load = c.stream("a_w")
        for dst, src in ((win, "win"), (wx, "wx"), (wo, "wo"), (conv, "conv"), (dvec, "dvec"), (gw, "gw")):
            w_load.mark(nc.sync.dma_start(dst[:], dram[src]))
        w_load.mark(nc.sync.dma_start(gb[:, :], dram["gb"].partition_broadcast(P)))
        m = w_load.mark(nc.sync.dma_start(bd[:, :, :], dram["bd"]))
        z = dve.mark(nc.vector.memset(total[:, :], 0.0))
        z = dve.mark(nc.vector.memset(slot[:, :, :], E0 * CAP))
        for t in threads:
            z = dve.mark(nc.vector.memset(t.ao[:, :, :], 0.0))
        for lane in (pe, dve, act, pool):
            lane.need(m, z)
        c.new_epoch()

        load_ahead()
        x_all = persist["x"]
        s_ct, s_disp = c.stream("a_ct"), c.stream("a_disp", reset=False)

        def dispatch():
            for s in range(RS):
                for k in range(2):
                    s_disp.mark(nc.gpsimd.indirect_dma_start(
                        out=dram["xe"], out_offset=bass.IndirectOffsetOnAxis(ap=slot[:, s, k:k + 1], axis=0),
                        in_=threads[s // GS].ao[:, s % GS, :], in_offset=None, bounds_check=E0 * CAP - 1, oob_is_err=False))

        def gated_block(t, x_in):
            ba, bb, bc_, bd_ = t.banks
            _, xt_ok = yield from layernorm(c, t, con, x_in)
            xs = [t.xt[:, k, :] for k in range(KD)]
            pair = lambda tile, m: tile[:, m:m + 2, :].rearrange("p m t -> p (m t)")
            for m in range(0, 2 * KI, 2):
                b = t.banks[m // 2]
                r = c.products(b, [(GT * q, [win[:, k, P * (m + q):P * (m + q) + P] for k in range(KD)], xs) for q in range(2)], xt_ok)
                act.need(r)
                if m < KI:
                    for q in range(2):
                        a = act.mark(nc.scalar.activation(t.xb[:, m + q, :, 3:P + 3],
                                                          c.ps[:, b, GT * q:GT * q + GT].rearrange("p (s l) -> p s l", l=P), ACT.Copy))
                    xb_ok = a
                else:
                    a = z_ok = act.mark(nc.scalar.activation(pair(t.sz, m - KI), c.ps[:, b, :], ACT.Silu))
                c.bank_read[b] = a
                yield
            dve.need(t.pad, xb_ok)
            for m in range(KI):
                tv = t.t1[:, m, :].rearrange("p (s l) -> p s l", l=P)
                a = dve.mark(nc.vector.tensor_scalar(tv, t.xb[:, m, :, 0:P], conv[:, m, 0:1], conv[:, m, 4:5], ALU.mult, ALU.add))
            for k in range(1, 4):
                for m in range(KI):
                    tv = t.t1[:, m, :].rearrange("p (s l) -> p s l", l=P)
                    dve.need((dve, dve.count - KI + 1))
                    a = dve.mark(nc.vector.scalar_tensor_tensor(out=tv, in0=t.xb[:, m, :, k:k + P], scalar=conv[:, m, k:k + 1],
                                                                in1=tv, op0=ALU.mult, op1=ALU.add))
            act.need(a)
            xc_ok = act.mark(nc.scalar.activation(t.xc[:, :, :], t.t1[:, :, :], ACT.Silu))
            yield
            xcs = [t.xc[:, k, :] for k in range(KI)]
            r = c.products(bc_, [(0, [wx[:, k, 0:64] for k in range(KI)], xcs)], xc_ok)
            nc.scalar.preload_act_table_set(LN_EXP)
            act.need(r)
            a = act.mark(nc.scalar.activation(t.cs[:, :], c.ps[32:32 + DSTATE, bc_, 0:GT], ACT.Copy))
            dve.need(a)
            b_ok = dve.mark(nc.vector.tensor_tensor(t.bc[:, :], c.ps[0:DSTATE, bc_, 0:GT], t.cs[:, :], ALU.mult))
            c.bank_read[bc_] = b_ok
            yield
            for m in range(0, KI, 2):
                b = (ba, bb)[m // 2]
                r = c.products(b, [(GT * q, [wx[:, k, 64 + P * (m + q):64 + P * (m + q) + P] for k in range(KI)], xcs) for q in range(2)], xc_ok)
                if m == 0:
                    bc_ok = c.products(bd_, [(0, [con["ones"][0:DSTATE, :]], [t.bc[:, :]])], b_ok)
                y = pair(t.t1, m)
                act.need(r)
                a = act.mark(nc.scalar.activation(y, c.ps[:, b, :], ACT.Abs))
                act.need(a)
                a = act.mark(nc.scalar.activation(y, y, ACT.Exp, scale=-1.0))
                act.need(a)
                a = act.mark(nc.scalar.activation(y, y, ACT.Ln, bias=1.0))
                yield
                dve.need(a, r, bc_ok)
                a = dve.mark(nc.vector.scalar_tensor_tensor(out=y, in0=c.ps[:, b, :], scalar=0.0, in1=y, op0=ALU.max, op1=ALU.add))
                c.bank_read[b] = a
                dve.need(a)
                a = dve.mark(nc.vector.tensor_tensor(t.t1[:, m:m + 2, :], t.t1[:, m:m + 2, :],
                                                     c.ps[:, bd_, None, 0:GT].to_broadcast([P, 2, GT]), ALU.mult))
                c.bank_read[bd_] = a
                dve.need(a)
                for q in range(m, m + 2):
                    a = dve.mark(nc.vector.scalar_tensor_tensor(out=t.t1[:, q, :], in0=t.t1[:, q, :], scalar=dvec[:, q:q + 1], in1=t.xc[:, q, :], op0=ALU.add, op1=ALU.mult))
                dve.need(a, z_ok)
                y_ok = dve.mark(nc.vector.tensor_tensor(y, y, pair(t.sz, m), ALU.mult))
            yield
            r = by_token(c, bc_, wo, t.t1, (y_ok,))
            dve.need(r)
            a = dve.mark(nc.vector.tensor_tensor(t.xg[:, :, :].rearrange("p s d -> p (s d)"), t.xg[:, :, :].rearrange("p s d -> p (s d)"),
                                                 c.ps[:, bc_, :], ALU.add))
            c.bank_read[bc_] = a
            yield
            return a

        def cross_attention(t, x_in, ct_in):
            ba, bb, bc_, bd_ = t.banks
            ctt = ct[:, :, t.tok]
            dve.need((pe, pe.count))
            act.need((pe, pe.count))
            vz = v_constants(c, t)
            r = c.products(bb, [(GT * ch, [bd[:, 1, :]], [ctt[:, ch, :]]) for ch in range(KD)], ct_in)
            k_ok = head_keys(c, t.kp, c.ps[:, bb, :], con["par"], r)
            c.bank_read[bb] = k_ok
            _, xt_ok = yield from layernorm(c, t, con, x_in)
            r = c.products(bc_, [(GT * ch, [bd[:, 0, :]], [t.xt[:, ch, :]]) for ch in range(KD)], xt_ok)
            act.need(r)
            q_ok = act.mark(nc.scalar.activation(t.qt[:, :, :].rearrange("p c t -> p (c t)"), c.ps[:, bc_, :], ACT.Copy, scale=HD ** -0.5))
            c.bank_read[bc_] = q_ok
            yield

            def make_v(s):
                r = c.products(bd_, [(P * ch, [ctt[:, ch, P * s:P * s + P]], [bd[:, 2, :]]) for ch in range(KD)], ct_in)
                act.need(r, vz)
                a = act.mark(nc.scalar.activation(t.vv[:, s % 2, :, 0:HD], c.ps[:, bd_, 0:D].rearrange("p (h e) -> p h e", e=HD), ACT.Copy))
                c.bank_read[bd_] = a
                return a

            done = yield from attention(c, t, con, make_v, (q_ok, k_ok))
            dve.need(done)
            return dve.mark(nc.vector.tensor_tensor(t.xg[:, :, :], t.xg[:, :, :], t.ao[:, :, :], ALU.add))

        with nc.Fori(0, NROUND) as i:
            nc.scalar.preload_act_table_set(LN_EXP)
            nc.gpsimd.wait_ge(s_zero.sem, s_zero.count)
            dispatch()
            ct_in = s_ct.mark(nc.sync.dma_start(ct[:, :, :], dram["ctx_t"][:, :, bass.ds(i * RT, RT)]))
            ready = [None] * NTH
            xn_ok = [None] * NTH

            with ExitStack() as inner:
                def block(t):
                    t.xb = t.sb("xb", [P, KI, GS, P + 3], F32, inner)
                    t.xc, t.sz, t.t1 = (t.sb(name, [P, KI, GT], F32, inner) for name in ("xc", "sz", "t1"))
                    t.cs, t.bc = t.sb("cs", [DSTATE, GT], F32, inner), t.sb("bc", [DSTATE, GT], F32, inner)
                    t.pad = pool.mark(nc.gpsimd.memset(t.xb[:, :, :, 0:3], 0.0))
                    m = act.mark(nc.scalar.activation(t.xg[:, :, :], x_all[:, bass.ds(i * RS + GS * t.n, GS), :], ACT.Copy))
                    ready[t.n] = yield from gated_block(t, m)

                alternate(block(t) for t in threads)
            last = [(lane, lane.count) for lane in (pe, dve, act)]
            with ExitStack() as inner:
                def cross(t):
                    t.for_attention(inner)
                    for lane in (pe, dve, act, pool):
                        lane.need(*last)
                    nc.vector.wait_ge(s_disp.sem, (i + 1) * (16 * 2 * RS))
                    x = yield from cross_attention(t, ready[t.n], ct_in)
                    act.need(x)
                    act.mark(nc.scalar.activation(x_all[:, bass.ds(i * RS + GS * t.n, GS), :], t.xg[:, :, :], ACT.Copy))
                    xn_ok[t.n], xt_ok = yield from layernorm(c, t, con, x, out=t.ao)
                    b = t.banks[1]
                    r = by_token(c, b, gw, t.xt, (xt_ok,))
                    dve.need(r)
                    ready[t.n] = dve.mark(nc.vector.tensor_tensor(router.lg[:, t.seqs, :], c.ps[:, b, 0:GS * E0].rearrange("p (s e) -> p s e", e=E0),
                                                                  gb[:, None, :].to_broadcast([P, GS, E0]), ALU.add))
                    c.bank_read[b] = ready[t.n]

                alternate(cross(t) for t in threads)

            pos, w = router.run(ready[-1], total[:, :])
            dve.need(pos)
            a = dve.mark(nc.vector.tensor_scalar(over[:, :, :], router.pos[:, :, :], float(CAP) - 0.5, None, ALU.is_gt))
            a2 = dve.mark(nc.vector.tensor_scalar(clip[:, :, :], router.pos[:, :, :], float(CAP - 1), None, ALU.min))
            dve.need(a, a2)
            a = dve.mark(nc.vector.scalar_tensor_tensor(out=sidx[:, :, :], in0=router.idx[:, :, :], scalar=float(CAP), in1=clip[:, :, :], op0=ALU.mult, op1=ALU.add))
            dve.need(a)
            a = dve.mark(nc.vector.scalar_tensor_tensor(out=slot[:, :, :], in0=over[:, :, :], scalar=float(E0 * CAP), in1=sidx[:, :, :], op0=ALU.mult, op1=ALU.add))
            dve.mark(nc.vector.tensor_copy(persist["gidx"][:, bass.ds(i * RS, RS), :], sidx[:, :, :]))
            a = dve.mark(nc.vector.tensor_scalar(over[:, :, :], over[:, :, :], -1.0, 1.0, ALU.mult, ALU.add))
            dve.need(a, w)
            dve.mark(nc.vector.tensor_tensor(persist["gwt"][:, bass.ds(i * RS, RS), :], router.w[:, :, :], over[:, :, :], ALU.mult))
            c.new_epoch()
        dispatch()
        for lane in (pool, sp):
            lane.need((s_disp, (NROUND + 1) * 16 * 2 * RS))


def v_constants(c, t):
    c.pool.mark(c.nc.gpsimd.memset(t.vv[:, :, :, HD + 1:32], 0.0))
    return c.pool.mark(c.nc.gpsimd.memset(t.vv[:, :, :, HD:HD + 1], 1.0))


def phase_b(c, con, dram, ring, s_ring):
    nc, pe, dve, act, pool, sp = c.nc, c.pe, c.dve, c.act, c.pool, c.sp
    w1r, w2r = ring
    MF = F0 // P
    TAIL = CAP - P
    with ExitStack() as ctx:
        def sb(name, shape, dt=F32):
            return ctx.enter_context(nc.sbuf_tensor("b_" + name, shape, dt))

        b1 = sb("b1", [P, E0, MF])
        b2 = sb("b2", [P, E0, KD])
        b1l = sb("b1l", [P, NB, MF])
        b2l = sb("b2l", [P, NB, KD])
        xe = sb("xe", [P, NB, D])
        xe2 = sb("xe2", [TAIL, NB, D])
        xet = sb("xet", [P, 2, KD, CAP])
        ht = sb("ht", [P, 2, MF, CAP])
        yt = sb("yt", [P, 2, KD, CAP])
        ye = sb("ye", [P, 2, D])
        ye2 = sb("ye2", [TAIL, 2, D])
        s_b = c.stream("b_bias")
        s_x, s_y = c.stream("b_x", reset=False), [c.stream("b_y0"), c.stream("b_y1")]
        s_b.mark(nc.sync.dma_start(b1[:, :, :], dram["b1"]))
        m = s_b.mark(nc.sync.dma_start(b2[:, :, :], dram["b2"]))
        act.need(m)
        xe_rows = dram["xe"].rearrange("(e r) d -> r e d", r=CAP)
        ye_rows = dram["ye"].rearrange("(e r) d -> r e d", r=CAP)

        def load_rows(first):
            s_x.mark(nc.sync.dma_start(xe[:, :, :], xe_rows[0:P, bass.ds(first, NB), :]))
            s_x.mark(nc.sync.dma_start(xe2[:, :, :], xe_rows[P:CAP, bass.ds(first, NB), :]))

        def experts(first, it, refill):
            nc.tensor.wait_ge(s_x.sem, (it + 1) * 32)
            b_in = act.mark(nc.scalar.activation(b1l[:, :, :], b1[:, bass.ds(first, NB), :], ACT.Copy))
            b_in = act.mark(nc.scalar.activation(b2l[:, :, :], b2[:, bass.ds(first, NB), :], ACT.Copy))
            act.need(b_in)
            dve.need(b_in)
            h_ok, down_ok, yt_ok, xt_read, xt_ok = [None] * NB, [None] * NB, [None] * NB, [None] * NB, [None] * NB
            turned = [None] * NB
            y_out = [None] * NB

            def turn_in(e):
                pe.need(c.bank_read[4])
                for k in range(KD):
                    nc.tensor.transpose(c.ps[:, 4, CAP * k:CAP * k + P], xe[:, e, k:D:KD], con["ident"])
                    t = nc.tensor.transpose(c.ps[:, 4, CAP * k + P:CAP * k + CAP], xe2[:, e, k:D:KD], con["ident"][0:TAIL, 0:TAIL])
                t = pe.mark(t)
                if e == NB - 1 and refill == NB:
                    sp.need(t)
                    load_rows(first + NB)
                dve.need(t, xt_read[e - 2] if e >= 2 else None)
                xt_ok[e] = dve.mark(nc.vector.tensor_copy(xet[:, e % 2, :, :], c.ps[:, 4, 0:KD * CAP].rearrange("p (k t) -> p k t", k=KD)))
                c.bank_read[4] = xt_ok[e]

            def up(e):
                slot = e % RING
                pe.need(xt_ok[e])
                nc.tensor.wait_ge(s_ring[slot].sem, it * (32 * NB // RING) + 32 * (e // RING + 1))
                act.need(down_ok[e - 2] if e >= 2 else None)
                for m in range(MF):
                    b = (m // 2) % 4
                    if m % 2 == 0:
                        pe.need(c.bank_read[b])
                    for k in range(KD):
                        ins = nc.tensor.matmul(c.ps[:, b, CAP * (m % 2):CAP * (m % 2) + CAP], w1r[:, slot, k, m:F0:MF],
                                               xet[:, e % 2, k, :], start=(k == 0), stop=(k == KD - 1), skip_group_check=True)
                    if m % 2 == 1:
                        r = pe.mark(ins)
                        act.need(r)
                        for q in (m - 1, m):
                            a = act.mark(nc.scalar.activation(ht[:, e % 2, q, :], c.ps[:, b, CAP * (q % 2):CAP * (q % 2) + CAP],
                                                              ACT.Gelu, bias=b1l[:, e, q:q + 1]))
                        c.bank_read[b] = a
                xt_read[e] = r
                h_ok[e] = a

            def down(e):
                slot = e % RING
                pe.need(h_ok[e], c.bank_read[5])
                for j in range(KD):
                    for m in range(MF):
                        ins = nc.tensor.matmul(c.ps[:, 5, CAP * j:CAP * j + CAP], w2r[:, slot, m, P * j:P * j + P],
                                               ht[:, e % 2, m, :], start=(m == 0), stop=(m == MF - 1), skip_group_check=True)
                down_ok[e] = pe.mark(ins)
                dve.need(down_ok[e], turned[e - 2] if e >= 2 else None)
                for j in range(KD):
                    a = dve.mark(nc.vector.tensor_scalar(yt[:, e % 2, j, :], c.ps[:, 5, CAP * j:CAP * j + CAP], b2l[:, e, j:j + 1], None, ALU.add))
                c.bank_read[5] = a
                yt_ok[e] = a
                if e < refill:
                    sp.need(down_ok[e])
                    load_expert(c, dram, ring, s_ring, slot, first + e + RING)

            def turn_out(e):
                pe.need(yt_ok[e], c.bank_read[6], c.bank_read[7])
                for j in range(KD):
                    nc.tensor.transpose(c.ps[:, 6, P * j:P * j + P], yt[:, e % 2, j, 0:P], con["ident"])
                    t = nc.tensor.transpose(c.ps[0:TAIL, 7, P * j:P * j + P], yt[:, e % 2, j, P:CAP], con["ident"])
                turned[e] = pe.mark(t)
                dve.need(turned[e], y_out[e - 2] if e >= 2 else None)
                a = dve.mark(nc.vector.tensor_copy(ye[:, e % 2, :], c.ps[:, 6, 0:D]))
                a2 = dve.mark(nc.vector.tensor_copy(ye2[:, e % 2, :], c.ps[0:TAIL, 7, 0:D]))
                c.bank_read[6], c.bank_read[7] = a, a2
                sp.need(a, a2)
                s_y[e % 2].mark(nc.sync.dma_start(ye_rows[0:P, bass.ds(first + e, 1), :], ye[:, e % 2:e % 2 + 1, :]))
                y_out[e] = s_y[e % 2].mark(nc.sync.dma_start(ye_rows[P:CAP, bass.ds(first + e, 1), :], ye2[:, e % 2:e % 2 + 1, :]))

            turn_in(0)
            for e in range(NB + 2):
                if e < NB:
                    if e + 1 < NB:
                        turn_in(e + 1)
                    up(e)
                if 1 <= e <= NB:
                    down(e - 1)
                if e >= 2:
                    turn_out(e - 2)
            c.new_epoch()

        load_rows(0)
        c.new_epoch()
        with nc.Fori(0, E0 // NB - 1) as i:
            experts(i * NB, i, NB)
        experts(E0 - NB, E0 // NB - 1, NB - RING)


def load_expert(c, dram, ring, s_ring, slot, e):
    nc = c.nc
    s_ring[slot].mark(nc.sync.dma_start(ring[0][:, slot:slot + 1, :, :].rearrange("p e k f -> p e (k f)"),
                                        dram["w1"].rearrange("e (p k) f -> p e (k f)", p=P)[:, bass.ds(e, 1), :]))
    s_ring[slot].mark(nc.sync.dma_start(ring[1][:, slot:slot + 1, :, :].rearrange("p e m d -> p e (m d)"),
                                        dram["w2"].rearrange("e (p m) d -> p e (m d)", p=P)[:, bass.ds(e, 1), :]))


class Gathers:

    def __init__(self, c, sb, persist, table, name):
        self.c, self.persist, self.table = c, persist, table
        self.idx = sb(name + "_gi", [P, RS, 2], U32)
        self.rows = sb(name + "_g", [P, RS, 2, D])
        self.stream = c.stream(name + "_gather", reset=False)

    def fetch(self, rnd, *free):
        c, nc = self.c, self.c.nc
        c.dve.need(*free)
        m = c.dve.mark(nc.vector.tensor_copy(self.idx[:, :, :], self.persist["gidx"][:, bass.ds(rnd * RS, RS), :]))
        c.pool.need(m, *free)
        for s in range(RS):
            for k in range(2):
                self.stream.mark(nc.gpsimd.indirect_dma_start(
                    out=self.rows[:, s, k, :], out_offset=None, in_=self.table,
                    in_offset=bass.IndirectOffsetOnAxis(ap=self.idx[:, s, k:k + 1], axis=0)))

    def wait(self, lane, rounds):
        lane.eng.wait_ge(self.stream.sem, rounds * (16 * 2 * RS))


def rms_rows(c, t, x, out, ready, free=None):
    nc, dve, act = c.nc, c.dve, c.act
    act.need(ready, free)
    for s in range(GS):
        m = act.mark(nc.scalar.activation(out[:, s, :], x[:, s, :], ACT.Square, accum_out=t.ss[:, s:s + 1]))
    dve.need(m)
    m = dve.mark(nc.vector.tensor_scalar(t.ve[:, :], t.ss[:, :], 1.0 / D, 1e-5, ALU.mult, ALU.add))
    m = yield from inverse_root(c, t, m)
    dve.need(m)
    for s in range(GS):
        m = dve.mark(nc.vector.tensor_scalar(out[:, s, :], x[:, s, :], t.rs[:, s:s + 1], None, ALU.mult))
    yield
    return m


def phase_c(c, con, dram, persist):
    nc, pe, dve, act, pool, sp = c.nc, c.pe, c.dve, c.act, c.pool, c.sp
    with ExitStack() as ctx:
        def sb(name, shape, dt=F32):
            return ctx.enter_context(nc.sbuf_tensor("c_" + name, shape, dt))

        wa = sb("wa", [P, 4, KD, D])
        wc = sb("wc", [P, 3, KD, D])
        wf = sb("wf", [P, 5, KD, D])
        wv = sb("wv", [P, KD, 4 * HD])
        gw = sb("gw", [P, KD, E1])
        cols = sb("cols", [P, 4, KD])
        rows = sb("rows", [P, 2, D])
        beta = sb("beta", [P, 3])
        coef = sb("coef", [P, 1])
        tiny = sb("tiny", [P, 1])
        ct = sb("ct", [P, KD, RT])
        phi = sb("phi", [P, RS, P])
        gwl = sb("gwl", [P, RS, 2])
        slot = sb("slot", [P, RS, 2], U32)
        router = Router(c, ctx, con, "c_", E1)
        total = persist["total"][:, :]
        gath = Gathers(c, sb, persist, dram["ye"], "c")
        threads = [Thread(n, nc, ctx, "c_") for n in range(NTH)]
        for t in threads:
            t.common()
            t.for_attention(ctx)
            t.ee, t.ll = t.sb("ee", [P, NU, P]), t.pt
            t.zz, t.en, t.po, t.gt = (t.sb(x, [P, NU]) for x in ("zz", "en", "po", "gt"))
            t.m4, t.z4 = t.sb("m4", [P, GS]), t.sb("z4", [P, GS])

        w_load = c.stream("c_w")
        for dst, src in ((wa, "wa"), (wc, "wc"), (wf, "wf"), (wv, "wv"), (gw, "gw1"), (cols, "cols")):
            w_load.mark(nc.sync.dma_start(dst[:], dram[src]))
        w_load.mark(nc.sync.dma_start(rows[:, 0, :], dram["bo"].partition_broadcast(P)))
        w_load.mark(nc.sync.dma_start(rows[:, 1, :], dram["bv"].partition_broadcast(P)))
        for n in range(3):
            m = w_load.mark(nc.sync.dma_start(beta[:, n:n + 1], dram["beta%d" % n].partition_broadcast(P)))
        gath.fetch(0)
        dve.need(m)
        a = dve.mark(nc.vector.tensor_tensor(coef[:, :], beta[:, 0:1], beta[:, 1:2], ALU.add))
        dve.need(a)
        dve.mark(nc.vector.tensor_tensor(coef[:, :], coef[:, :], beta[:, 2:3], ALU.subtract))
        dve.mark(nc.vector.memset(tiny[:, :], 1e-9))
        dve.mark(nc.vector.memset(total, 0.0))
        dve.mark(nc.vector.memset(slot[:, :, :], E1 * R1 + E1 * P))
        for t in threads:
            dve.mark(nc.vector.memset(t.ao[:, :, :], 0.0))
            v_constants(c, t)
        c.new_epoch()
        x_all = persist["x"]
        s_ct, s_disp = c.stream("c_ct"), c.stream("c_disp", reset=False)

        def dispatch():
            for s in range(RS):
                for k in range(2):
                    s_disp.mark(nc.gpsimd.indirect_dma_start(
                        out=dram["xd"], out_offset=bass.IndirectOffsetOnAxis(ap=slot[:, s, k:k + 1], axis=0),
                        in_=threads[s // GS].ao[:, s % GS, :], in_offset=None,
                        bounds_check=E1 * R1 + E1 * P - 1, oob_is_err=False))

        def values(t, w, x_ok, copy):
            b = t.banks[3]

            def make_v(s):
                r = c.products(b, [(0, [t.xt[:, k, P * s:P * s + P] for k in range(KD)], [w[:, k, :] for k in range(KD)])], x_ok)
                act.need(r)
                a = act.mark(copy(s % 2, b))
                c.bank_read[b] = a
                return a
            return make_v

        def temperature(t):
            def exponents(d, sub):
                dd, ee, ll = d[:, :, :], t.ee[:, :, :], t.ll[:, :, :]
                wide = lambda x: x[:, :, None].to_broadcast([P, NU, P])
                act.need(sub)
                a = act.mark(nc.scalar.activation(ee, dd, ACT.Exp))
                dve.need(a)
                a = dve.mark(nc.vector.tensor_reduce(t.zz[:, :], ee, AX, ALU.add))
                dve.need(a)
                a = dve.mark(nc.vector.reciprocal(t.zz[:, :], t.zz[:, :]))
                pool.need(a)
                p_ok = pool.mark(nc.gpsimd.tensor_tensor(ee, ee, wide(t.zz), ALU.mult))
                yield
                act.need(p_ok)
                a = act.mark(nc.scalar.activation(ll, ee, ACT.Ln, bias=tiny[:, 0:1]))
                yield
                dve.need(a, p_ok)
                for n in range(NU):
                    a = dve.mark(nc.vector.scalar_tensor_tensor(out=t.ll[:, n, :], in0=t.ee[:, n, :], scalar=-1.0, in1=t.ll[:, n, :],
                                                                op0=ALU.mult, op1=ALU.mult, accum_out=t.en[:, n:n + 1]))
                en, po = t.en[:, :], t.po[:, :]
                dve.need(a)
                dve.mark(nc.vector.tensor_scalar(t.gt[:, :], en, 0.5, None, ALU.is_gt))
                a = dve.mark(nc.vector.tensor_scalar(po, en, POLY[0], None, ALU.mult))
                for q in POLY[1:4]:
                    dve.need(a)
                    a = dve.mark(nc.vector.scalar_tensor_tensor(out=po, in0=po, scalar=q, in1=en, op0=ALU.add, op1=ALU.mult))
                dve.need(a)
                a = dve.mark(nc.vector.tensor_scalar(po, po, POLY[4], 1.0, ALU.add, ALU.max))
                dve.need(a)
                a = dve.mark(nc.vector.scalar_tensor_tensor(out=po, in0=po, scalar=-1.0, in1=t.gt[:, :], op0=ALU.add, op1=ALU.mult))
                dve.need(a)
                a = dve.mark(nc.vector.tensor_scalar(po, po, 1.0, None, ALU.add))
                pool.need(a, sub)
                a = pool.mark(nc.gpsimd.tensor_tensor(dd, dd, wide(t.po), ALU.mult))
                yield
                return a
            return exponents

        def causal_attention(t, x_in):
            ba, bb, bc_, bd_ = t.banks
            _, xt_ok = yield from layernorm(c, t, con, x_in)
            r = by_channel(c, bb, wa[:, 0, :, :], t.xt, (xt_ok,))
            act.need(r)
            q_ok = act.mark(nc.scalar.activation(t.qt[:, :, :].rearrange("p c t -> p (c t)"), c.ps[:, bb, :], ACT.Copy, scale=HD ** -0.5))
            c.bank_read[bb] = q_ok
            yield
            r = by_channel(c, bc_, wa[:, 1, :, :], t.xt, (xt_ok,))
            k_ok = head_keys(c, t.kp, c.ps[:, bc_, :], con["par"], r)
            c.bank_read[bc_] = k_ok
            yield
            make_v = values(t, wa[:, 2, :, :], xt_ok, lambda v, b: nc.scalar.activation(
                t.vv[:, v, :, 0:HD], c.ps[:, b, 0:D].rearrange("p (h e) -> p h e", e=HD), ACT.Copy))
            done = yield from attention(c, t, con, make_v, (q_ok, k_ok), mask=con["mask"], temperature=temperature(t))
            xt_ok = yield from transpose_rows(c, t, con, t.ao, done)
            r = by_token(c, bb, wa[:, 3, :, :], t.xt, (xt_ok,))
            yield
            flat = t.xg[:, :, :].rearrange("p s d -> p (s d)")
            dve.need(r)
            a = dve.mark(nc.vector.tensor_tensor(flat, flat, c.ps[:, bb, :], ALU.add))
            c.bank_read[bb] = a
            dve.need(a)
            return dve.mark(nc.vector.tensor_tensor(t.xg[:, :, :], t.xg[:, :, :], rows[:, 0:1, :].to_broadcast([P, GS, D]), ALU.add))

        def cross_attention(t, x_in, ct_in):
            ba, bb, bc_, bd_ = t.banks
            ctt = ct[:, :, t.tok]
            r = by_channel(c, bc_, wc[:, 1, :, :], ctt, (ct_in,))
            act.need(r)
            for ch in range(KD):
                k_ok = act.mark(nc.scalar.activation(t.kp[:, ch, 0, :], c.ps[:, bc_, GT * ch:GT * ch + GT], ACT.Identity, bias=cols[:, 1, ch:ch + 1]))
            c.bank_read[bc_] = k_ok
            r = by_token(c, bd_, wc[:, 2, :, :], ctt, (ct_in,))
            dve.need(r)
            v_ok = dve.mark(nc.vector.tensor_tensor(t.ao[:, :, :], c.ps[:, bd_, :].rearrange("p (s d) -> p s d", s=GS),
                                                    rows[:, 1:2, :].to_broadcast([P, GS, D]), ALU.add))
            c.bank_read[bd_] = v_ok
            _, xt_ok = yield from layernorm(c, t, con, x_in)
            r = by_channel(c, bb, wc[:, 0, :, :], t.xt, (xt_ok,))
            yield
            dve.need(r)
            for ch in range(KD):
                q_ok = dve.mark(nc.vector.tensor_scalar(t.qt[:, ch, :], c.ps[:, bb, GT * ch:GT * ch + GT], cols[:, 0, ch:ch + 1], D ** -0.5, ALU.add, ALU.mult))
            c.bank_read[bb] = q_ok
            r = c.products(ba, [(P * s, [t.qt[:, ch, P * s:P * s + P] for ch in range(KD)], [t.kp[:, ch, 0, P * s:P * s + P] for ch in range(KD)])
                                for s in range(GS)], q_ok, k_ok)
            yield
            dd = t.dd[0][:, 0:GS, :]
            dve.need(r)
            a = dve.mark(nc.vector.scalar_tensor_tensor(out=dd, in0=phi[:, t.seqs, :], scalar=coef[:, 0:1],
                                                        in1=c.ps[:, ba, 0:GT].rearrange("p (s t) -> p s t", s=GS), op0=ALU.mult, op1=ALU.add))
            c.bank_read[ba] = a
            dve.need(a)
            a = dve.mark(nc.vector.tensor_reduce(t.m4[:, :], dd, AX, ALU.max))
            dve.need(a)
            a = dve.mark(nc.vector.tensor_tensor(dd, dd, t.m4[:, :, None].to_broadcast([P, GS, P]), ALU.subtract))
            act.need(a)
            e = act.mark(nc.scalar.activation(dd, dd, ACT.Exp))
            yield
            dve.need(e)
            z = dve.mark(nc.vector.tensor_reduce(t.z4[:, :], dd, AX, ALU.add))
            r = c.transposes(ba, [(P * s, t.dd[0][:, s, :]) for s in range(GS)], con["ident"], e)
            act.need(r)
            p_ok = act.mark(nc.scalar.activation(t.pt[:, 0:GS, :].rearrange("p h k -> p (h k)"), c.ps[:, ba, 0:GT], ACT.Copy))
            c.bank_read[ba] = p_ok
            dve.need(z)
            z = dve.mark(nc.vector.reciprocal(t.z4[:, :], t.z4[:, :]))
            yield
            r = c.products(bc_, [(D * s, [t.pt[:, s, :]], [t.ao[:, s, :]]) for s in range(GS)], p_ok, v_ok)
            dve.need(r, z)
            for s in range(GS):
                a = dve.mark(nc.vector.scalar_tensor_tensor(out=t.xg[:, s, :], in0=c.ps[:, bc_, D * s:D * s + D], scalar=t.z4[:, s:s + 1],
                                                            in1=t.xg[:, s, :], op0=ALU.mult, op1=ALU.add))
            c.bank_read[bc_] = a
            yield
            return a

        def rotary_attention(t, x_in):
            ba, bb, bc_, bd_ = t.banks
            u_ok, _ = yield from layernorm(c, t, con, x_in, want_t=False)
            h_ok = yield from rms_rows(c, t, t.xn, t.ao, u_ok, (pe, pe.count))
            xt_ok = yield from transpose_rows(c, t, con, t.ao, h_ok, scale=cols[:, 2, :])
            keys = t.ee[:, 0:2 * GS, :]
            for what, dst in ((0, t.qt[:, :, :].rearrange("p c (s l) -> p (c s) l", l=P)), (1, keys)):
                r0 = by_channel(c, bb, wf[:, 2 * what, :, :], t.xt, (xt_ok,))
                r1 = by_channel(c, bc_, wf[:, 2 * what + 1, :, :], t.xt, (xt_ok,))
                yield
                tmp = t.ll[:, 0:2 * GS, :]
                rope = lambda n: con["rope"][:, n:n + 1, :].to_broadcast([P, 2 * GS, P])
                bank = lambda b: c.ps[:, b, :].rearrange("p (n l) -> p n l", l=P)
                dve.need(r0)
                a = dve.mark(nc.vector.tensor_tensor(dst, bank(bb), rope(2 * what), ALU.mult))
                c.bank_read[bb] = a
                dve.need(r1)
                a = dve.mark(nc.vector.tensor_tensor(tmp, bank(bc_), rope(2 * what + 1), ALU.mult))
                c.bank_read[bc_] = a
                dve.need(a)
                ok = dve.mark(nc.vector.tensor_tensor(dst, dst, tmp, ALU.add))
                dve.need(ok)
                if what == 0:
                    q_ok = ok
            k_ok = head_keys(c, t.kp, t.ee[:, 0:2 * GS, :].rearrange("p n l -> p (n l)"), con["par"], ok)
            yield
            make_v = values(t, wv, xt_ok, lambda v, b: nc.scalar.activation(
                t.vv[:, v, :, 0:HD].rearrange("p (g r) e -> p g r e", r=4),
                c.ps[:, b, 0:4 * HD].rearrange("p (g e) -> p g e", e=HD)[:, :, None, :].to_broadcast([P, 4, 4, HD]), ACT.Copy))
            done = yield from attention(c, t, con, make_v, (q_ok, k_ok), mask=con["mask"])
            xt_ok = yield from transpose_rows(c, t, con, t.ao, done)
            r = by_token(c, bb, wf[:, 4, :, :], t.xt, (xt_ok,))
            yield
            flat = t.xn[:, :, :].rearrange("p s d -> p (s d)")
            dve.need(r)
            a = dve.mark(nc.vector.tensor_tensor(flat, flat, c.ps[:, bb, :], ALU.add))
            c.bank_read[bb] = a
            return a

        with nc.Fori(0, NROUND) as i:
            nc.scalar.preload_act_table_set(LN_EXP)
            ct_in = s_ct.mark(nc.sync.dma_start(ct[:, :, :], dram["ctx_t"][:, :, bass.ds(i * RT, RT)]))
            ct_in = s_ct.mark(nc.sync.dma_start(phi[:, :, :], dram["phi"][:, bass.ds(i * RS, RS), :]))
            a = act.mark(nc.scalar.activation(gwl[:, :, :], persist["gwt"][:, bass.ds(i * RS, RS), :], ACT.Copy))
            gath.wait(dve, i + 1)
            read = []
            for t in threads:
                a = act.mark(nc.scalar.activation(t.xg[:, :, :], x_all[:, bass.ds(i * RS + GS * t.n, GS), :], ACT.Copy))
                dve.need(a)
                for k in range(2):
                    for s in range(GS):
                        a = dve.mark(nc.vector.scalar_tensor_tensor(out=t.xg[:, s, :], in0=gath.rows[:, GS * t.n + s, k, :], scalar=gwl[:, GS * t.n + s, k:k + 1],
                                                                    in1=t.xg[:, s, :], op0=ALU.mult, op1=ALU.add))
                    dve.need(a)
                read.append(a)
            dispatch()
            gath.fetch(i + 1, read[-1])
            ready = [None] * NTH

            def layer(t):
                x = read[t.n]
                nc.vector.wait_ge(s_disp.sem, (i + 1) * (16 * 2 * RS))
                x = yield from causal_attention(t, x)
                if STOP != "c1":
                    x = yield from cross_attention(t, x, ct_in)
                if STOP is None:
                    u = yield from rotary_attention(t, x)
                    dve.need(u)
                    x = dve.mark(nc.vector.tensor_tensor(t.xg[:, :, :], t.xg[:, :, :], t.xn[:, :, :], ALU.add))
                    h_ok = yield from rms_rows(c, t, t.xn, t.ao, u, (pe, pe.count))
                    xt_ok = yield from transpose_rows(c, t, con, t.ao, h_ok, scale=cols[:, 3, :])
                    b = t.banks[1]
                    r = by_token(c, b, gw, t.xt, (xt_ok,))
                    dve.need(r)
                    ready[t.n] = dve.mark(nc.vector.tensor_copy(router.lg[:, t.seqs, :], c.ps[:, b, 0:GS * E1].rearrange("p (s e) -> p s e", e=E1)))
                    c.bank_read[b] = ready[t.n]
                act.need(x)
                act.mark(nc.scalar.activation(x_all[:, bass.ds(i * RS + GS * t.n, GS), :], t.xg[:, :, :], ACT.Copy))

            alternate(layer(t) for t in threads)
            if STOP is None:
                pos, w = router.run(ready[-1], total)
                dve.need(pos, w)
                dve.mark(nc.vector.scalar_tensor_tensor(out=slot[:, :, :], in0=router.idx[:, :, :], scalar=float(R1), in1=router.pos[:, :, :], op0=ALU.mult, op1=ALU.add))
                for name, part in (("choice", router.idx), ("place", router.pos), ("gwt", router.w)):
                    dve.mark(nc.vector.tensor_copy(persist[name][:, bass.ds(i * RS, RS), :], part[:, :, :]))
            c.new_epoch()
        dispatch()
        pool.need((s_disp, (NROUND + 1) * 16 * 2 * RS))
        gath.wait(dve, NROUND + 1)
        c.new_epoch()


def phase_d(c, con, dram, persist, w13, w_ready, out):
    nc, pe, dve, act, pool, sp = c.nc, c.pe, c.dve, c.act, c.pool, c.sp
    MF = F1 // P
    with ExitStack() as ctx:
        def sb(name, shape, dt=F32):
            return ctx.enter_context(nc.sbuf_tensor("d_" + name, shape, dt))

        w2 = sb("w2", [P, E1 * F1 // P, D])
        dconst = sb("dconst", [P, dram["dconst"].shape[1]])
        cols = sb("cols", [P, 4, KD])
        cnt = sb("cnt", [P, E1])
        tail = sb("tail", [P, E1], U32)
        cmp = sb("cmp", [P, NT1, 16])
        til = sb("til", [P, E1])
        end = sb("end", [P, E1])
        ej = sb("ej", [P, NT1])
        sj = sb("sj", [P, NT1])
        look = sb("look", [P, 2 * NSEQ, E1])
        base = sb("base", [P, 2 * NSEQ])
        row = sb("row", [P, NT1], I32)
        wex = sb("wex", [P, NT1], I32)
        xd = sb("xd", [P, ND, D])
        xt = sb("xt", [P, 2, KD, P])
        gs = sb("gs", [P, 2, F1])
        g = sb("g", [P, 2, F1])
        gt = sb("gt", [P, 2, MF, P])
        yd = sb("yd", [P, ND, D])
        k_tail, k_tile, k_upto, k_j, k_jrow = (dconst[:, a:b] for a, b in DCONST)
        s_c = c.stream("d_c")
        s_c.mark(nc.sync.dma_start(dconst[:, :], dram["dconst"]))
        m = s_c.mark(nc.sync.dma_start(cols[:, :, :], dram["cols"]))
        w2_in = c.stream("d_w2").mark(nc.sync.dma_start(w2[:, :, :], dram["w2d"]))
        pe.need(c.bank_read[0])
        r = pe.mark(nc.tensor.matmul(c.ps[:, 0, 0:E1], con["ones_bf"], persist["total"][:, :], start=True, stop=True))
        dve.need(r, m)
        a = dve.mark(nc.vector.tensor_copy(cnt[:, :], c.ps[:, 0, 0:E1]))
        dve.need(a)
        tl = dve.mark(nc.vector.tensor_tensor(tail[:, :], cnt[:, :], k_tail, ALU.add))
        pool.need(tl)
        s_tail = c.stream("d_tail", reset=False)
        for e in range(E1):
            t_in = s_tail.mark(nc.gpsimd.indirect_dma_start(
                out=dram["xd"], out_offset=bass.IndirectOffsetOnAxis(ap=tail[:, e:e + 1], axis=0),
                in_=con["zero"][:, 0:D], in_offset=None))
        pool.need(t_in)
        cv = cmp[:, 0:E1, :]
        a = dve.mark(nc.vector.tensor_tensor(cv, cnt[:, :, None].to_broadcast([P, E1, 16]), k_tile[:, None, :].to_broadcast([P, E1, 16]), ALU.is_gt))
        dve.need(a)
        a = dve.mark(nc.vector.tensor_reduce(til[:, :], cv, AX, ALU.add))
        dve.need(a)
        cv = cmp[:, 0:E1, 0:E1]
        a = dve.mark(nc.vector.tensor_tensor(cv, til[:, None, :].to_broadcast([P, E1, E1]), k_upto.rearrange("p (a b) -> p a b", a=E1), ALU.mult))
        dve.need(a)
        a = dve.mark(nc.vector.tensor_reduce(end[:, :], cv, AX, ALU.add))
        dve.need(a)
        flat = lambda t: t[:, :, :].rearrange("p s k -> p (s k)")
        dve.need(a)
        a = dve.mark(nc.vector.tensor_tensor(look[:, :, :], flat(persist["choice"])[:, :, None].to_broadcast([P, 2 * NSEQ, E1]),
                                             con["iota"][:, None, 0:E1].to_broadcast([P, 2 * NSEQ, E1]), ALU.is_equal))
        a = dve.mark(nc.vector.tensor_tensor(ej[:, 0:E1], end[:, :], til[:, :], ALU.subtract))
        dve.need(a)
        a = dve.mark(nc.vector.tensor_tensor(look[:, :, :], look[:, :, :], ej[:, None, 0:E1].to_broadcast([P, 2 * NSEQ, E1]), ALU.mult))
        dve.need(a)
        a = dve.mark(nc.vector.tensor_reduce(base[:, :], look[:, :, :], AX, ALU.add))
        dve.need(a)
        a = dve.mark(nc.vector.scalar_tensor_tensor(out=flat(persist["gidx"])[:, 0:2 * NSEQ], in0=base[:, :], scalar=float(P),
                                                    in1=flat(persist["place"]), op0=ALU.mult, op1=ALU.add))
        cv = cmp[:, :, 0:E1]
        a = dve.mark(nc.vector.tensor_tensor(cv, end[:, None, :].to_broadcast([P, NT1, E1]), k_j[:, :, None].to_broadcast([P, NT1, E1]), ALU.is_le))
        dve.need(a)
        a = dve.mark(nc.vector.tensor_reduce(ej[:, :], cv, AX, ALU.add))
        a = dve.mark(nc.vector.tensor_tensor(cv, cv, til[:, None, :].to_broadcast([P, NT1, E1]), ALU.mult))
        dve.need(a)
        a = dve.mark(nc.vector.tensor_reduce(sj[:, :], cv, AX, ALU.add))
        dve.need(a)
        a = dve.mark(nc.vector.scalar_tensor_tensor(out=sj[:, :], in0=sj[:, :], scalar=-float(P), in1=k_jrow, op0=ALU.mult, op1=ALU.add))
        dve.need(a)
        a = dve.mark(nc.vector.scalar_tensor_tensor(out=row[:, :], in0=ej[:, :], scalar=float(R1), in1=sj[:, :], op0=ALU.mult, op1=ALU.add))
        a = dve.mark(nc.vector.tensor_scalar(wex[:, :], ej[:, :], float(E1 - 1), None, ALU.min))
        pe.need(w_ready, w2_in)
        c.new_epoch()

        s_x, s_y = c.stream("d_x"), c.stream("d_y")
        with nc.Fori(0, NT1 // ND) as i:
            at = [sp.eng.value_load(row[0:1, bass.ds(i * ND + n, 1)], min_val=0, max_val=E1 * R1 + 7 * P) for n in range(ND)]
            x_in = [s_x.mark(nc.sync.dma_start(xd[:, n, :], dram["xd"][bass.ds(at[n], P), :])) for n in range(ND)]
            x_in = [x_in[-1]] * ND
            xt_ok, up_ok, g_ok, gt_ok, dn_ok, gt_tr = ([None] * ND for _ in range(6))

            def turn_in(n):
                b = 6
                pe.need(x_in[n], c.bank_read[b])
                for k in range(KD):
                    t = nc.tensor.transpose(c.ps[:, b, P * k:P * k + P], xd[:, n, P * k:P * k + P], con["ident"])
                t = pe.mark(t)
                act.need(t, up_ok[n - 2] if n >= 2 else None)
                for k in range(KD):
                    a = act.mark(nc.scalar.activation(xt[:, n % 2, k, :], c.ps[:, b, P * k:P * k + P], ACT.Copy, scale=cols[:, 3, k:k + 1]))
                c.bank_read[b] = a
                xt_ok[n] = a

            def up(n):
                e = pe.eng.value_load(wex[0:1, bass.ds(i * ND + n, 1)], min_val=0, max_val=E1 - 1)
                for half in range(2):
                    b = 2 * (n % 2) + half
                    pe.need(xt_ok[n], c.bank_read[b])
                    for k in range(KD):
                        ins = nc.tensor.matmul(c.ps[:, b, :], xt[:, n % 2, k, :], w13[:, bass.ds(e * (2 * KD) + 2 * k + half, 1), :],
                                               start=(k == 0), stop=(k == KD - 1))
                    r = pe.mark(ins)
                    if half == 0:
                        act.need(r)
                        a = act.mark(nc.scalar.activation(gs[:, n % 2, :], c.ps[:, b, :], ACT.Silu))
                        c.bank_read[b] = a
                    else:
                        dve.need(r, a, gt_tr[n - 2] if n >= 2 else None)
                        g_ok[n] = dve.mark(nc.vector.tensor_tensor(g[:, n % 2, :], gs[:, n % 2, :], c.ps[:, b, :], ALU.mult))
                        c.bank_read[b] = g_ok[n]
                up_ok[n] = r
                return e

            def turn_hidden(n):
                t = c.transposes(4, [(P * m, g[:, n % 2, P * m:P * m + P]) for m in range(MF)], con["ident"], g_ok[n])
                gt_tr[n] = t
                dve.need(t, dn_ok[n - 2] if n >= 2 else None)
                gt_ok[n] = dve.mark(nc.vector.tensor_copy(gt[:, n % 2, :, :].rearrange("p m t -> p (m t)"), c.ps[:, 4, :]))
                c.bank_read[4] = gt_ok[n]

            def down(n, e):
                pe.need(gt_ok[n], c.bank_read[5])
                for m in range(MF):
                    ins = nc.tensor.matmul(c.ps[:, 5, 0:D], gt[:, n % 2, m, :], w2[:, bass.ds(e * MF + m, 1), :], start=(m == 0), stop=(m == MF - 1))
                dn_ok[n] = pe.mark(ins)
                dve.need(dn_ok[n])
                a = dve.mark(nc.vector.tensor_copy(yd[:, n, :], c.ps[:, 5, 0:D]))
                c.bank_read[5] = a
                sp.need(a)
                s_y.mark(nc.sync.dma_start(dram["yd"][bass.ds((i * ND + n) * P, P), :], yd[:, n, :]))

            es = [None] * ND
            turn_in(0)
            es[0] = up(0)
            turn_in(1)
            for n in range(ND):
                if n + 1 < ND:
                    es[n + 1] = up(n + 1)
                turn_hidden(n)
                if n + 2 < ND:
                    turn_in(n + 2)
                down(n, es[n])
            c.new_epoch()

        gath = Gathers(c, sb, persist, dram["yd"], "d")
        xo = sb("xo", [P, RS, D])
        gwl = sb("gwl", [P, RS, 2])
        s_o = c.stream("out")
        gath.fetch(0)
        c.new_epoch()
        with nc.Fori(0, NROUND) as i:
            a = act.mark(nc.scalar.activation(gwl[:, :, :], persist["gwt"][:, bass.ds(i * RS, RS), :], ACT.Copy))
            a = act.mark(nc.scalar.activation(xo[:, :, :], persist["x"][:, bass.ds(i * RS, RS), :], ACT.Copy))
            dve.need(a)
            gath.wait(dve, i + 1)
            for k in range(2):
                for s in range(RS):
                    a = dve.mark(nc.vector.scalar_tensor_tensor(out=xo[:, s, :], in0=gath.rows[:, s, k, :], scalar=gwl[:, s, k:k + 1],
                                                                in1=xo[:, s, :], op0=ALU.mult, op1=ALU.add))
                dve.need(a)
            gath.fetch(i + 1, a)
            sp.need(a)
            s_o.mark(nc.sync.dma_start(out.rearrange("s l d -> l s d")[:, bass.ds(i * RS, RS), :], xo[:, :, :]))
            c.new_epoch()
        gath.wait(dve, NROUND + 1)


def build(nc, dram, out, stop=STOP):
    for name, n in (("xe", E0 * CAP), ("ye", E0 * CAP), ("xd", E1 * R1 + E1 * P), ("yd", NT1 * P)):
        dram[name] = nc.dram_tensor(name, (n, D), F32, kind="Internal").ap()
    with ExitStack() as ctx:
        c = Core(nc, ctx)
        dve, pool, pe, act = c.dve, c.pool, c.pe, c.act

        def sb(name, shape, dt=F32):
            return ctx.enter_context(nc.sbuf_tensor(name, shape, dt))

        cf = sb("cf", [P, dram["cf"].shape[1]])
        cb = sb("cb", [P, dram["cb"].shape[1]], BF16)
        persist = {"x": sb("x_all", [P, NSEQ, D]), "gidx": sb("gidx_all", [P, NSEQ + RS, 2], U32),
                   "gwt": sb("gwt_all", [P, NSEQ, 2]), "total": sb("total1", [P, E1], BF16), "choice": sb("choice", [P, NSEQ, 2]),
                   "place": sb("place", [P, NSEQ, 2])}
        con = {"ident": cf[:, 0:128], "par": cf[:, 128:132], "iota": cf[:, 132:164], "mhalf": cf[:, 164:164 + GS],
               "ones": cf[:, 168:296], "rope": cf[:, 296:808].rearrange("p (n l) -> p n l", l=P), "ident_bf": cb[:, 0:128], "mask": cb[:, 128:640],
               "before_bf": cb[:, 640:768], "ones_bf": cb[:, 768:896]}
        zero = sb("zero", [P, D])
        s_in = c.stream("in")
        with nc.sbuf_tensor("cb_f32", list(dram["cb"].shape), F32) as cb_f32:
            s_in.mark(nc.sync.dma_start(cf[:, :], dram["cf"]))
            m = s_in.mark(nc.sync.dma_start(cb_f32[:, :], dram["cb"]))
            dve.need(m)
            c.sp.need(dve.mark(nc.vector.tensor_copy(cb[:, :], cb_f32[:, :])))
        m = s_in.mark(nc.sync.dma_start(persist["x"][:, :, :], dram["x"]))
        for lane in (pe, dve, act, pool):
            lane.need(m)
        zm = dve.mark(nc.vector.memset(zero[:, :], 0.0))
        act.need(zm)
        s_zero = c.stream("zero", reset=False)
        zp = max(n for n in range(1, P + 1) if E0 * CAP % n == 0)
        s_zero.mark(nc.scalar.dma_start(dram["xe"].rearrange("(p n) d -> p n d", p=zp),
                                        zero[0:zp, None, :].to_broadcast([zp, E0 * CAP // zp, D])))
        xd_tail = dram["xd"][E1 * R1:, :].rearrange("(p r) d -> p (r d)", p=P)
        s_zero.mark(nc.scalar.dma_start(xd_tail.rearrange("p (n e) -> p n e", e=D), zero[:, None, :].to_broadcast([P, E1, D])))
        con["zero"] = zero
        gz = dve.mark(nc.vector.memset(persist["gidx"][:, NSEQ:, :], 0))
        with ExitStack() as stack:
            ring = (stack.enter_context(nc.sbuf_tensor("ring1", [P, RING, KD, F0], F32)),
                    stack.enter_context(nc.sbuf_tensor("ring2", [P, RING, F0 // P, D], F32)))
            s_ring = [c.stream("ring%d" % n, reset=False) for n in range(RING)]
            phase_a(c, con, dram, persist, s_zero, lambda: [load_expert(c, dram, ring, s_ring, n, n) for n in range(RING)])
            if stop != "a":
                phase_b(c, con, dram, ring, s_ring)
        if stop != "a":
            with ExitStack() as stack:
                w13 = stack.enter_context(nc.sbuf_tensor("w13", [P, E1 * KD * 2, F1], F32))
                s_w = c.stream("w_d", reset=False)
                w_ready = s_w.mark(nc.sync.dma_start(w13[:, :, :], dram["w13"]))
                phase_c(c, con, dram, persist)
                if stop is None:
                    phase_d(c, con, dram, persist, w13, w_ready, out)
        if stop is not None:
            s = c.stream("o")
            c.sp.need(s.mark(nc.sync.dma_start(out.rearrange("s l d -> l s d"), persist["x"][:, :, :])))


def constants():
    p = np.arange(P)
    par = np.stack([(p // HD) % 4 == j for j in range(4)], 1).astype(np.float32)
    cf = np.concatenate([np.eye(P), par, np.tile(np.arange(E0), (P, 1)), np.full((P, 4), -0.5),
                         np.ones((P, P))], 1).astype(np.float32)
    freq = (1.0 / np.float32(10000.0) ** (np.arange(0, HD, 2, dtype=np.float32) / HD)).astype(np.float32)
    ang = (np.arange(P, dtype=np.float32)[:, None] * freq[None, :]).astype(np.float32)
    ang = np.tile(np.concatenate([ang, ang], 1).T, (P // HD, 1))
    sign = np.where(p % HD < HD // 2, -1.0, 1.0)[:, None]
    cos, sin = np.cos(ang), np.sin(ang) * sign
    cf = np.concatenate([cf, cos * HD ** -0.5, sin * HD ** -0.5, cos, sin], 1).astype(np.float32)
    e8, j = np.arange(E1), np.arange(NT1)
    dconst = np.concatenate([p[:, None] + R1 * e8[None, :]] + [np.tile(v.reshape(1, -1), (P, 1)) for v in (
        P * np.arange(16), e8[None, :] <= e8[:, None], j, P * j)], 1).astype(np.float32)
    causal = np.where(p[None, :] > p[:, None], NEG, 0.0)
    cb = np.concatenate([np.eye(P), np.tile(causal, (1, 4)), (p[:, None] < p[None, :]).astype(np.float32), np.ones((P, P))], 1).astype(np.float32)
    return {"cf": cf, "cb": cb, "dconst": dconst}


def layouts(x):
    def chunks(w):
        return np.ascontiguousarray(w.reshape(-1, P, w.shape[1]).transpose(1, 0, 2))

    a = {}
    a["x"] = np.ascontiguousarray(x["x"].transpose(1, 0, 2))
    a["ctx_t"] = chunks(x["ctx_1024"].reshape(NSEQ * P, D).T)
    a["win"] = chunks(x["L0_attn_W_in"].T)
    w = x["L0_attn_W_xproj"].T
    pad = np.zeros((DI, 16), w.dtype)
    a["wx"] = chunks(np.concatenate([w[:, :16], pad, w[:, 16:32], pad, w[:, 32:]], 1))
    a["wo"] = chunks(x["L0_attn_W_out"].T)
    a["conv"] = chunks(np.concatenate([x["L0_attn_conv_w"], x["L0_attn_conv_b"][:, None]], 1))
    a["dvec"] = np.ascontiguousarray(x["L0_attn_D"].reshape(KI, P).T)
    bd = np.zeros((P, 3, P), np.float32)
    for n, name in enumerate(("L0_xattn_Wq", "L0_xattn_Wk", "L0_xattn_Wv")):
        for h in range(P // HD):
            bd[HD * h:HD * h + HD, n, HD * h:HD * h + HD] = x[name].T
    a["bd"] = bd
    a["gw"] = chunks(x["L0_ffn_gate_w"])
    a["gb"] = x["L0_ffn_gate_b"]
    a["w1"], a["w2"] = x["L0_ffn_w1"], x["L0_ffn_w2"]
    a["b1"] = np.ascontiguousarray(x["L0_ffn_b1"].reshape(E0, P, F0 // P).transpose(1, 0, 2))
    a["b2"] = np.ascontiguousarray(x["L0_ffn_b2"].reshape(E0, KD, P).transpose(2, 0, 1))
    stack = lambda ws: np.ascontiguousarray(np.stack([chunks(w) for w in ws], 1))
    a["wa"] = stack([x["L1_attn_W" + n].T for n in "qkvo"])
    a["wc"] = stack([x["L1_xattn_W" + n].T for n in "qkv"])
    qkv = x["L1_ffn_wqkv"]
    swap = np.arange(D).reshape(-1, 2, HD // 2)[:, ::-1].reshape(-1)
    q = qkv[:D]
    kv = HD * (NH // 4)
    k = np.repeat(qkv[D:D + kv].reshape(4, HD, D), 4, axis=0).reshape(D, D)
    a["wf"] = stack([q.T, q[swap].T, k.T, k[swap].T, x["L1_ffn_wo"].T])
    a["wv"] = chunks(qkv[D + kv:].T)
    a["gw1"] = chunks(x["L1_ffn_gate_w"].T)
    col = lambda v: v.reshape(KD, P).T
    a["cols"] = np.ascontiguousarray(np.stack([col(x[n]) for n in ("L1_xattn_bq", "L1_xattn_bk", "L1_ffn_ln1_w", "L1_ffn_ln2_w")], 1))
    a["bo"], a["bv"] = x["L1_attn_bo"], x["L1_xattn_bv"]
    for n, name in enumerate(("risk", "prio", "impl")):
        a["beta%d" % n] = np.asarray(x["L1_xattn_beta_" + name]).reshape(1)
    a["phi"] = np.ascontiguousarray(x["fside_BxSxS2_0"].transpose(1, 0, 2))
    w13 = x["L1_ffn_w13"].reshape(E1, 2, F1, KD, P)
    a["w13"] = np.ascontiguousarray(w13.transpose(4, 0, 3, 1, 2).reshape(P, E1 * KD * 2, F1))
    w2 = x["L1_ffn_w2"].reshape(E1, D, F1 // P, P)
    a["w2d"] = np.ascontiguousarray(w2.transpose(3, 0, 2, 1).reshape(P, E1 * F1 // P, D))
    return a


def kernel(**inputs):
    import concourse.bacc as bacc
    from concourse.bass_utils import run_bass_kernel_spmd

    nc = bacc.Bacc("TRN2", target_bir_lowering=False, num_devices=1)
    arrays = {"in_" + k: v for k, v in {**layouts({k: np.asarray(v) for k, v in inputs.items()}), **constants()}.items()}
    dram = {k[3:]: nc.dram_tensor(k, v.shape, mybir.dt.from_np(v.dtype), kind="ExternalInput").ap() for k, v in arrays.items()}
    out = nc.dram_tensor("out_dram", (NSEQ, P, D), F32, kind="ExternalOutput").ap()
    build(nc, dram, out)
    r = run_bass_kernel_spmd(nc, [arrays], core_ids=[0])
    return r.results[0]["out_dram"]
```

```python
from contextlib import ExitStack

import numpy as np
import concourse.bass as bass
from concourse import mybir

F32 = mybir.dt.float32
BF16 = mybir.dt.bfloat16
I32 = mybir.dt.int32
U32 = mybir.dt.uint32
ALU = mybir.AluOpType
ACT = mybir.ActivationFunctionType
AX = mybir.AxisListType.X

P = 128
NSEQ = 16
D = 256
KD = D // P
NTH = 2
GS = 2
GT = GS * P
RS = NTH * GS
RT = RS * P
NROUND = NSEQ // RS
NBANK = 8 // NTH
NU = 8
NH, HD = 16, 16
DI = 512
KI = DI // P
DSTATE = 16
E0, F0 = 32, 1024
CAP = 154
E1, F1 = 8, 512
R1 = NSEQ * P + P
NT1 = NSEQ * P * 2 // P + E1
NEG = -1.0e30
LN_EXP = "natural_log_exp_and_others"
POLY = [-0.037, 0.481, -2.3, 4.917, -1.791]
RING = 4
NB = 8
ND = 10
DCONST = [(0, 8), (8, 24), (24, 88), (88, 88 + NT1), (88 + NT1, 88 + 2 * NT1)]
REGION = 12 * KD * D + KD * (4 * HD + E1 + 4) + 2 * D + 3 + DCONST[-1][1]
LAG_GATED, LAG_CROSS, LAG_C = 0, 1, 1
LAG_UNIT = 2
LAG_ROUTING = 2


class Lane:

    def __init__(self, eng, sem, step=1):
        self.eng, self.sem, self.step, self.count, self.seen = eng, sem, step, 0, {}

    def mark(self, ins):
        self.count += self.step
        ins.then_inc(self.sem, self.step)
        return (self, self.count)

    def need(self, *marks):
        for m in marks:
            if m is not None and self.seen.get(m[0], 0) < m[1]:
                self.eng.wait_ge(m[0].sem, m[1])
                self.seen[m[0]] = m[1]


class Core:

    def __init__(self, nc, ctx):
        self.nc, self.ctx = nc, ctx
        self.pe = Lane(nc.tensor, self.sem("pe"))
        self.dve = Lane(nc.vector, self.sem("dve"))
        self.act = Lane(nc.scalar, self.sem("act"))
        self.pool = Lane(nc.gpsimd, self.sem("pool"))
        self.sp = Lane(nc.sync, self.sem("sp"))
        self.lanes = [self.pe, self.dve, self.act, self.pool, self.sp]
        self.streams = []
        self.ps = ctx.enter_context(nc.psum_tensor("ps", [P, 8, 512], F32))
        self.bank_read = [None] * 8

    def sem(self, name):
        return self.ctx.enter_context(self.nc.semaphore("s_" + name))

    def stream(self, name, reset=True):
        s = Lane(None, self.sem(name), 16)
        if reset:
            self.streams.append(s)
        return s

    def new_epoch(self):
        for lane in self.lanes:
            lane.need((lane, lane.count))
        for s in self.streams:
            self.sp.need((s, s.count))
        self.nc.all_engine_barrier()
        for x in self.lanes + self.streams:
            if x.count:
                self.nc.sync.sem_clear(x.sem)
            x.count = 0
        for x in self.lanes:
            x.seen = {}
        self.bank_read = [None] * 8
        self.nc.all_engine_barrier()

    def transposes(self, bank, pairs, ident, *marks):
        self.pe.need(self.bank_read[bank], *marks)
        for col, src in pairs:
            n = src.shape[0]
            ins = self.nc.tensor.transpose(self.ps[0:src.shape[1], bank, col:col + n], src, ident[0:n, 0:n])
        return self.pe.mark(ins)

    def products(self, bank, parts, *marks):
        self.pe.need(self.bank_read[bank], *marks)
        for col, w, x in parts:
            for k in range(len(w)):
                out = self.ps[0:w[k].shape[-1], bank, col:col + x[k].shape[-1]]
                ins = self.nc.tensor.matmul(out, w[k], x[k], start=(k == 0), stop=(k == len(w) - 1), skip_group_check=True)
        return self.pe.mark(ins)


class Region:

    def __init__(self, tile):
        self.tile, self.used = tile, 0

    def take(self, *shape):
        n = int(np.prod(shape))
        flat = self.tile[:, self.used:self.used + n]
        self.used += n
        axes = "abcd"[:len(shape)]
        if len(shape) == 1:
            return flat
        return flat.rearrange("p (%s) -> p %s" % (" ".join(axes), " ".join(axes)), **dict(zip(axes, shape)))


def alternate(threads, lag=0, beside=()):
    for _ in alternately(threads, lag, beside):
        pass


def alternately(threads, lag=0, beside=()):
    threads, turn = list(threads), 0
    starts = {t: lag * n for n, t in enumerate(threads)}
    starts.update((t, LAG_ROUTING) for t in beside)
    threads += beside
    while threads:
        turn += 1
        for t in [t for t in threads if turn > starts[t]]:
            try:
                next(t)
            except StopIteration:
                threads.remove(t)
        yield


class Thread:

    def __init__(self, n, nc, ctx, prefix):
        self.n, self.nc, self.ctx, self.prefix = n, nc, ctx, prefix
        self.copy = ""
        self.banks = [NBANK * n + b for b in range(NBANK)]
        self.seqs = slice(GS * n, GS * n + GS)
        self.tok = slice(GT * n, GT * n + GT)

    def sb(self, name, shape, dt=F32, ctx=None):
        name = self.prefix + name + str(self.n) + self.copy
        return (ctx or self.ctx).enter_context(self.nc.sbuf_tensor(name, shape, dt))

    def common(self):
        self.xg = self.sb("xg", [P, GS, D])
        self.xn = self.sb("xn", [P, GS, D])
        self.xt = self.sb("xt", [P, KD, GT])
        self.st, self.mv = self.sb("st", [P, GS, 6]), self.sb("mv", [P, GS, 2])
        self.ve, self.rs, self.r2, self.ss = (self.sb(x, [P, GS]) for x in ("ve", "rs", "r2", "ss"))
        self.ao = self.sb("ao", [P, GS, D])

    def for_attention(self, ctx, spare=None):
        sb = lambda name, shape: self.sb(name, shape, F32, ctx)
        self.qt, self.kp = sb("qt", [P, KD, GT]), sb("kp", [P, KD, 4, GT])
        self.vv = sb("vv", [P, GS, NH, 32])
        self.units = [Unit(ch, self, sb, spare) for ch in range(KD)]


class Unit:

    def __init__(self, ch, t, sb, spare):
        self.ch, self.t, self.banks = ch, t, t.banks[2 * ch:2 * ch + 2]
        name = lambda x: x + "ab"[ch]
        big = lambda x: next(spare) if spare and ch else sb(name(x), [P, NU, P])
        self.d, self.pt = big("d"), big("pt")
        self.os = sb(name("os"), [P, 2 * P])
        self.mx, self.rz = sb(name("mx"), [P, NU]), sb(name("rz"), [P, NU])
        if spare:
            self.ee, self.ll = big("ee"), self.pt
            self.zz, self.en, self.po, self.gt = (sb(name(x), [P, NU]) for x in ("zz", "en", "po", "gt"))


def layernorm(c, t, con, x_ready, want_t=True, out=None):
    nc, dve = c.nc, c.dve
    out = t.xn if out is None else out
    dve.need(x_ready)
    for s in range(GS):
        m = dve.mark(nc.vector.bn_stats(t.st[:, s, :], t.xg[:, s, :]))
    dve.need(m)
    for s in range(GS):
        m = dve.mark(nc.vector.bn_aggr(t.mv[:, s, :], t.st[:, s, :]))
    dve.need(m)
    m = dve.mark(nc.vector.tensor_scalar(t.ve[:, :], t.mv[:, :, 1], 1e-5, None, ALU.add))
    m = yield from inverse_root(c, t, m)
    dve.need(m)
    for s in range(GS):
        n = dve.mark(nc.vector.tensor_scalar(out[:, s, :], t.xg[:, s, :], t.mv[:, s, 0:1], t.rs[:, s:s + 1],
                                             ALU.subtract, ALU.mult))
    if not want_t:
        return n, None
    yield
    return n, (yield from transpose_rows(c, t, con, out, n))


def inverse_root(c, t, ready):
    nc, dve, act = c.nc, c.dve, c.act
    ve, rs, r2 = t.ve[:, :], t.rs[:, :], t.r2[:, :]
    act.need(ready)
    m = act.mark(nc.scalar.activation(rs, ve, ACT.Ln))
    act.need(m)
    m = act.mark(nc.scalar.activation(rs, rs, ACT.Exp, scale=-0.5))
    yield
    dve.need(m)
    m = dve.mark(nc.vector.tensor_tensor(r2, rs, rs, ALU.mult))
    dve.need(m)
    m = dve.mark(nc.vector.tensor_tensor(r2, r2, ve, ALU.mult))
    dve.need(m)
    m = dve.mark(nc.vector.tensor_scalar(r2, r2, -0.5, 1.5, ALU.mult, ALU.add))
    dve.need(m)
    return dve.mark(nc.vector.tensor_tensor(rs, rs, r2, ALU.mult))


def transpose_rows(c, t, con, x, ready, scale=None):
    nc, act = c.nc, c.act
    b = t.banks[0]
    m = c.transposes(b, [(GT * k + P * s, x[:, s, P * k:P * k + P]) for k in range(KD) for s in range(GS)], con["ident"], ready)
    act.need(m)
    if scale is None:
        m = act.mark(nc.scalar.activation(t.xt[:, :, :], c.ps[:, b, :], ACT.Copy))
    else:
        for k in range(KD):
            m = act.mark(nc.scalar.activation(t.xt[:, k, :], c.ps[:, b, GT * k:GT * k + GT], ACT.Copy, scale=scale[:, k:k + 1]))
    c.bank_read[b] = m
    yield
    return m


def by_channel(c, bank, w, x, ready):
    return c.products(bank, [(GT * ch, [w[:, k, P * ch:P * ch + P] for k in range(KD)], [x[:, k, :] for k in range(KD)])
                             for ch in range(KD)], *ready)


def by_token(c, bank, w, x, ready):
    n = w.shape[-1]
    return c.products(bank, [(n * s, [x[:, k, P * s:P * s + P] for k in range(w.shape[1])], [w[:, k, :] for k in range(w.shape[1])])
                             for s in range(GS)], *ready)


def head_keys(c, kp, src, par, mark):
    nc, act = c.nc, c.act
    act.need(mark)
    for j in range(4):
        m = act.mark(nc.scalar.activation(kp[:, :, j, :], src.rearrange("p (c t) -> p c t", c=KD), ACT.Copy, scale=par[:, j:j + 1]))
    return m


def attention(c, t, con, make_v, ready, mask=None, temperature=None):
    nc, pe, dve, act = c.nc, c.pe, c.dve, c.act

    def unit(u, s, v_ok):
        b0, b1 = u.banks
        ch, tok = u.ch, slice(P * s, P * s + P)
        both = c.ps[:, b0:b0 + 2, :].rearrange("p b (h k) -> p (b h) k", k=P)
        pe.need(*ready, c.bank_read[b0], c.bank_read[b1])
        if mask is not None:
            for b in (b0, b1):
                nc.tensor.matmul(c.ps[:, b, :], con["ident_bf"], mask, start=True, stop=True, skip_group_check=True)
        for b in range(2):
            ins = nc.tensor.matmul(c.ps[:, b0 + b, :], t.qt[64 * b:64 * b + 64, ch, tok],
                                   t.kp[64 * b:64 * b + 64, ch, :, tok], start=(mask is None), stop=True,
                                   tile_position=(64 * b, 0), skip_group_check=True)
        m = pe.mark(ins)
        yield
        dve.need(m)
        m = dve.mark(nc.vector.tensor_reduce(u.mx[:, :], both, AX, ALU.max))
        dve.need(m)
        m = dve.mark(nc.vector.tensor_tensor(u.d[:, :, :], both, u.mx[:, :, None].to_broadcast([P, NU, P]), ALU.subtract))
        c.bank_read[b0] = c.bank_read[b1] = m
        yield
        if temperature is not None:
            m = yield from temperature(u, m)
        act.need(m)
        m = act.mark(nc.scalar.activation(u.d[:, :, :], u.d[:, :, :], ACT.Exp))
        yield
        for b in range(2):
            tr = c.transposes(b0 + b, [(P * n, u.d[:, 4 * b + n, :]) for n in range(4)], con["ident"], m)
        act.need(tr)
        m = act.mark(nc.scalar.activation(u.pt[:, :, :], both, ACT.Copy))
        c.bank_read[b0] = c.bank_read[b1] = m
        yield
        pe.need(m, v_ok, c.bank_read[b0])
        for n in range(NU):
            r, at = n % 4, n // 4
            ins = nc.tensor.matmul(c.ps[32 * r:32 * r + 32, b0, P * at:P * at + P], t.vv[:, s, NU * ch + n, :],
                                   u.pt[:, n, :], start=True, stop=True, tile_position=(0, 32 * r), skip_group_check=True)
        m = pe.mark(ins)
        act.need(m)
        m = act.mark(nc.scalar.activation(u.os[:, :], c.ps[:, b0, 0:2 * P], ACT.Copy))
        c.bank_read[b0] = m
        yield
        m = c.transposes(b1, [(P * at, u.os[:, P * at:P * at + P]) for at in range(2)], con["ident"], m)
        ot = c.ps[:, b1, 0:2 * P].rearrange("p (h e) -> p h e", e=32)
        dve.need(m)
        m = dve.mark(nc.vector.reciprocal(u.rz[:, :], ot[:, :, HD]))
        dve.need(m)
        m = dve.mark(nc.vector.tensor_tensor(t.ao[:, s, P * ch:P * ch + P].rearrange("p (h e) -> p h e", e=HD), ot[:, :, 0:HD],
                                             u.rz[:, :, None].to_broadcast([P, NU, HD]), ALU.mult))
        c.bank_read[b1] = u.done = m
        yield

    v_ok = [make_v(s) for s in range(GS)]
    yield

    def half(u):
        for s in range(GS):
            yield from unit(u, s, v_ok[s])

    yield from alternately((half(u) for u in t.units), LAG_UNIT)
    return max((u.done for u in t.units), key=lambda m: m[1])


class Router:

    def __init__(self, c, ctx, con, prefix, n_exp):
        def sb(name, shape, dt=F32):
            return ctx.enter_context(c.nc.sbuf_tensor(prefix + name, shape, dt))
        self.c, self.con, self.n_exp = c, con, n_exp
        self.lg = sb("lg", [P, RS, n_exp])
        self.m8, self.i8 = sb("m8", [P, RS, 8]), sb("i8", [P, RS, 8], U32)
        self.gap, self.den = sb("gap", [P, RS]), sb("den", [P, RS])
        self.idx, self.w, self.pos = sb("idx", [P, RS, 2]), sb("w", [P, RS, 2]), sb("pos", [P, RS, 2])
        self.oh, self.pr = sb("oh", [P, RS, 2, n_exp]), sb("pr", [P, RS, 2, n_exp])
        self.ohs = sb("ohs", [P, RS, n_exp], BF16)

    def run(self, total):
        c, nc, con, n_exp = self.c, self.c.nc, self.con, self.n_exp
        pe, dve, act = c.pe, c.dve, c.act
        for s in range(RS):
            m = dve.mark(nc.vector.max(out=self.m8[:, s, :], in_=self.lg[:, s, :]))
        dve.need(m)
        for s in range(RS):
            i = dve.mark(nc.vector.max_index(out=self.i8[:, s, :], in_max=self.m8[:, s, :], in_values=self.lg[:, s, :]))
        m = dve.mark(nc.vector.tensor_tensor(self.gap[:, :], self.m8[:, :, 1], self.m8[:, :, 0], ALU.subtract))
        act.need(m)
        ex = act.mark(nc.scalar.activation(self.gap[:, :], self.gap[:, :], ACT.Exp))
        dve.need(i)
        m = dve.mark(nc.vector.tensor_copy(self.idx[:, :, :], self.i8[:, :, 0:2]))
        dve.need(m)
        iota = con["iota"][:, None, 0:n_exp].to_broadcast([P, 2 * RS, n_exp])
        oh = self.oh[:, :, :, :].rearrange("p s k e -> p (s k) e")
        pr = self.pr[:, :, :, :].rearrange("p s k e -> p (s k) e")
        idx = self.idx[:, :, :].rearrange("p s k -> p (s k)")
        m = dve.mark(nc.vector.tensor_tensor(oh, iota, idx[:, :, None].to_broadcast([P, 2 * RS, n_exp]), ALU.is_equal))
        dve.need(m)
        m = dve.mark(nc.vector.tensor_tensor(self.ohs[:, :, :], self.oh[:, :, 0, :], self.oh[:, :, 1, :], ALU.add))
        yield
        b = 7
        pe.need(m, c.bank_read[b])
        for s in range(RS):
            at = c.ps[:, b, n_exp * s:n_exp * s + n_exp]
            nc.tensor.matmul(at, con["before_bf"], self.ohs[:, s, :], start=True, stop=False, skip_group_check=True)
            for q in range(s):
                nc.tensor.matmul(at, con["ones_bf"], self.ohs[:, q, :], start=False, stop=False, skip_group_check=True)
            ins = nc.tensor.matmul(at, con["ones_bf"], total, start=False, stop=True, skip_group_check=True)
        places = pe.mark(ins)
        dve.need(ex)
        m = dve.mark(nc.vector.tensor_scalar(self.den[:, :], self.gap[:, :], 1.0, None, ALU.add))
        dve.need(m)
        m = dve.mark(nc.vector.reciprocal(self.w[:, :, 0], self.den[:, :]))
        dve.need(m)
        w = dve.mark(nc.vector.tensor_tensor(self.w[:, :, 1], self.gap[:, :], self.w[:, :, 0], ALU.mult))
        dve.need(places)
        by = c.ps[:, b, 0:RS * n_exp].rearrange("p (s e) -> p s e", e=n_exp)
        for k in range(2):
            m = dve.mark(nc.vector.tensor_tensor(self.pr[:, :, k, :], self.oh[:, :, k, :], by, ALU.mult))
        c.bank_read[b] = m
        for s in range(RS):
            dve.mark(nc.vector.tensor_tensor(total, total, self.ohs[:, s, :], ALU.add))
            dve.need((dve, dve.count))
        yield
        pos = dve.mark(nc.vector.tensor_reduce(self.pos[:, :, :].rearrange("p s k -> p (s k)"), pr, AX, ALU.add))
        return pos, w


def phase_a(c, con, dram, persist, region, x_in, s_zero, load_ahead):
    nc, pe, dve, act, pool, sp = c.nc, c.pe, c.dve, c.act, c.pool, c.sp
    with ExitStack() as ctx:
        def sb(name, shape, dt=F32):
            return ctx.enter_context(nc.sbuf_tensor("a_" + name, shape, dt))

        win, wx, wo, bd = region.take(KD, 2 * DI), region.take(KI, 64 + DI), region.take(KI, D), region.take(3, P)
        conv, dvec = region.take(KI, 5), region.take(KI)
        gw, gb = region.take(KD, E0), region.take(E0)
        total = sb("total", [P, E0], BF16)
        ct = sb("ct", [P, KD, RT])
        over, clip, sidx = (sb(x, [P, RS, 2]) for x in ("over", "clip", "sidx"))
        slot, gidx = sb("slot", [P, RS, 2], U32), sb("gidx", [P, RS, 2], U32)
        gwt = sb("gwt", [P, RS, 2])
        router = Router(c, ctx, con, "a_", E0)
        threads = [Thread(n, nc, ctx, "a_") for n in range(NTH)]
        for t in threads:
            t.common()
            t.rows = t.sb("rows", [P, GS, D])

        w_load, w_load2 = c.stream("a_w", reset=False), c.stream("a_w2", reset=False)
        for dst, src in ((conv, "conv"), (dvec, "dvec"), (win, "win")):
            win_in = w_load.mark(nc.sync.dma_start(dst, dram[src]))
        for dst, src in ((wx, "wx"), (wo, "wo"), (bd, "bd"), (gw, "gw")):
            w_load2.mark(nc.sync.dma_start(dst, dram[src]))
        rest_in = w_load2.mark(nc.sync.dma_start(gb, dram["gb"].partition_broadcast(P)))
        dve.mark(nc.vector.memset(total[:, :], 0.0))
        c.new_epoch()

        x_all = persist["x"]
        s_ct, s_disp = c.stream("a_ct"), c.stream("a_disp", reset=False)

        def dispatch():
            for s in range(RS):
                for k in range(2):
                    s_disp.mark(nc.gpsimd.indirect_dma_start(
                        out=dram["xe"], out_offset=bass.IndirectOffsetOnAxis(ap=slot[:, s, k:k + 1], axis=0),
                        in_=threads[s // GS].rows[:, s % GS, :], in_offset=None, bounds_check=E0 * CAP - 1, oob_is_err=False))

        def gated_block(t, x_ok, first):
            ba, bb, bc_, bd_ = t.banks
            _, xt_ok = yield from layernorm(c, t, con, x_ok)
            if first:
                for lane in (pe, dve, act):
                    lane.need(win_in)
            xs = [t.xt[:, k, :] for k in range(KD)]
            pair = lambda tile, m: tile[:, m:m + 2, :].rearrange("p m t -> p (m t)")
            for m in range(0, 2 * KI, 2):
                b = t.banks[m // 2]
                r = c.products(b, [(GT * q, [win[:, k, P * (m + q):P * (m + q) + P] for k in range(KD)], xs) for q in range(2)], xt_ok)
                act.need(r)
                if m < KI:
                    for q in range(2):
                        a = act.mark(nc.scalar.activation(t.xb[:, m + q, :, 3:P + 3],
                                                          c.ps[:, b, GT * q:GT * q + GT].rearrange("p (s l) -> p s l", l=P), ACT.Copy))
                    xb_ok = a
                    act.need(t.pad, a)
                    for q in range(m, m + 2):
                        tap_ok = act.mark(nc.scalar.activation(t.t1[:, q, :].rearrange("p (s l) -> p s l", l=P), t.xb[:, q, :, 0:P],
                                                               ACT.Identity, bias=conv[:, q, 4:5], scale=conv[:, q, 0:1]))
                else:
                    a = z_ok = act.mark(nc.scalar.activation(pair(t.sz, m - KI), c.ps[:, b, :], ACT.Silu))
                c.bank_read[b] = a
                yield
            dve.need(t.pad, xb_ok, tap_ok)
            for k in range(1, 4):
                for m in range(KI):
                    tv = t.t1[:, m, :].rearrange("p (s l) -> p s l", l=P)
                    if k > 1:
                        dve.need((dve, dve.count - KI + 1))
                    a = dve.mark(nc.vector.scalar_tensor_tensor(out=tv, in0=t.xb[:, m, :, k:k + P], scalar=conv[:, m, k:k + 1],
                                                                in1=tv, op0=ALU.mult, op1=ALU.add))
            act.need(a)
            xc_ok = act.mark(nc.scalar.activation(t.xc[:, :, :], t.t1[:, :, :], ACT.Silu))
            yield
            if first:
                for lane in (pe, dve):
                    lane.need(rest_in)
            xcs = [t.xc[:, k, :] for k in range(KI)]
            r = c.products(bc_, [(0, [wx[:, k, 0:64] for k in range(KI)], xcs)], xc_ok)
            if t.n == 0:
                nc.scalar.preload_act_table_set(LN_EXP)
            act.need(r)
            a = act.mark(nc.scalar.activation(t.cs[:, :], c.ps[32:32 + DSTATE, bc_, 0:GT], ACT.Copy))
            dve.need(a)
            b_ok = dve.mark(nc.vector.tensor_tensor(t.bc[:, :], c.ps[0:DSTATE, bc_, 0:GT], t.cs[:, :], ALU.mult))
            c.bank_read[bc_] = b_ok
            yield
            for m in range(0, KI, 2):
                b = (ba, bb)[m // 2]
                r = c.products(b, [(GT * q, [wx[:, k, 64 + P * (m + q):64 + P * (m + q) + P] for k in range(KI)], xcs) for q in range(2)], xc_ok)
                if m == 0:
                    bc_ok = c.products(bd_, [(0, [con["ones"][0:DSTATE, :]], [t.bc[:, :]])], b_ok)
                y = pair(t.t1, m)
                act.need(r)
                a = act.mark(nc.scalar.activation(y, c.ps[:, b, :], ACT.Abs))
                act.need(a)
                a = act.mark(nc.scalar.activation(y, y, ACT.Exp, scale=-1.0))
                act.need(a)
                a = act.mark(nc.scalar.activation(y, y, ACT.Ln, bias=1.0))
                yield
                dve.need(a, r, bc_ok)
                a = dve.mark(nc.vector.scalar_tensor_tensor(out=y, in0=c.ps[:, b, :], scalar=0.0, in1=y, op0=ALU.max, op1=ALU.add))
                c.bank_read[b] = a
                dve.need(a)
                a = dve.mark(nc.vector.tensor_tensor(t.t1[:, m:m + 2, :], t.t1[:, m:m + 2, :],
                                                     c.ps[:, bd_, None, 0:GT].to_broadcast([P, 2, GT]), ALU.mult))
                c.bank_read[bd_] = a
                dve.need(a)
                for q in range(m, m + 2):
                    a = dve.mark(nc.vector.scalar_tensor_tensor(out=t.t1[:, q, :], in0=t.t1[:, q, :], scalar=dvec[:, q:q + 1], in1=t.xc[:, q, :], op0=ALU.add, op1=ALU.mult))
                dve.need(a, z_ok)
                y_ok = dve.mark(nc.vector.tensor_tensor(y, y, pair(t.sz, m), ALU.mult))
            yield
            r = by_token(c, bc_, wo, t.t1, (y_ok,))
            dve.need(r)
            a = dve.mark(nc.vector.tensor_tensor(t.xg[:, :, :].rearrange("p s d -> p (s d)"), t.xg[:, :, :].rearrange("p s d -> p (s d)"),
                                                 c.ps[:, bc_, :], ALU.add))
            c.bank_read[bc_] = a
            yield
            return a

        def cross_attention(t, x_in, ct_in):
            ba, bb, bc_, bd_ = t.banks
            ctt = ct[:, :, t.tok]
            norm = layernorm(c, t, con, x_in)
            next(norm)
            yield
            for lane in (pe, dve, act, pool):
                lane.need(*t.last)
            vz = v_constants(c, t)
            r = c.products(bb, [(GT * ch, [bd[:, 1, :]], [ctt[:, ch, :]]) for ch in range(KD)], ct_in)
            k_ok = head_keys(c, t.kp, c.ps[:, bb, :], con["par"], r)
            c.bank_read[bb] = k_ok
            _, xt_ok = yield from norm
            r = c.products(bc_, [(GT * ch, [bd[:, 0, :]], [t.xt[:, ch, :]]) for ch in range(KD)], xt_ok)
            act.need(r)
            q_ok = act.mark(nc.scalar.activation(t.qt[:, :, :].rearrange("p c t -> p (c t)"), c.ps[:, bc_, :], ACT.Copy, scale=HD ** -0.5))
            c.bank_read[bc_] = q_ok
            yield

            def make_v(s):
                r = c.products(bd_, [(P * ch, [ctt[:, ch, P * s:P * s + P]], [bd[:, 2, :]]) for ch in range(KD)], ct_in)
                act.need(r, vz)
                a = act.mark(nc.scalar.activation(t.vv[:, s, :, 0:HD], c.ps[:, bd_, 0:D].rearrange("p (h e) -> p h e", e=HD), ACT.Copy))
                c.bank_read[bd_] = a
                return a

            done = yield from attention(c, t, con, make_v, (q_ok, k_ok))
            dve.need(done)
            return dve.mark(nc.vector.tensor_tensor(t.xg[:, :, :], t.xg[:, :, :], t.ao[:, :, :], ALU.add))

        def routing(rnd):
            pos, w = yield from router.run(total[:, :])
            dve.need(pos)
            a = dve.mark(nc.vector.tensor_scalar(over[:, :, :], router.pos[:, :, :], float(CAP) - 0.5, None, ALU.is_gt))
            a2 = dve.mark(nc.vector.tensor_scalar(clip[:, :, :], router.pos[:, :, :], float(CAP - 1), None, ALU.min))
            dve.need(a, a2)
            a = dve.mark(nc.vector.scalar_tensor_tensor(out=sidx[:, :, :], in0=router.idx[:, :, :], scalar=float(CAP), in1=clip[:, :, :], op0=ALU.mult, op1=ALU.add))
            dve.need(a)
            a = dve.mark(nc.vector.scalar_tensor_tensor(out=slot[:, :, :], in0=over[:, :, :], scalar=float(E0 * CAP), in1=sidx[:, :, :], op0=ALU.mult, op1=ALU.add))
            dve.mark(nc.vector.tensor_copy(persist["gidx"][:, bass.ds(rnd * RS, RS), :], sidx[:, :, :]))
            nc.gpsimd.wait_ge(s_zero.sem, s_zero.count)
            pool.need(a)
            dispatch()
            a = dve.mark(nc.vector.tensor_scalar(over[:, :, :], over[:, :, :], -1.0, 1.0, ALU.mult, ALU.add))
            dve.need(a, w)
            dve.mark(nc.vector.tensor_tensor(persist["gwt"][:, bass.ds(rnd * RS, RS), :], router.w[:, :, :], over[:, :, :], ALU.mult))

        def a_round(rnd, before=None):
            nc.scalar.preload_act_table_set(LN_EXP)
            ct_in = s_ct.mark(nc.sync.dma_start(ct[:, :, :], dram["ctx_t"][:, :, bass.ds(rnd * RT, RT)]))
            first = before is None
            if first:
                load_ahead()
                act.need(x_in)
            ready = [None] * NTH

            with ExitStack() as inner:
                def block(t):
                    t.copy = "_first" if before is None else ""
                    t.xb = t.sb("xb", [P, KI, GS, P + 3], F32, inner)
                    t.xc, t.sz, t.t1 = (t.sb(name, [P, KI, GT], F32, inner) for name in ("xc", "sz", "t1"))
                    t.cs, t.bc = t.sb("cs", [DSTATE, GT], F32, inner), t.sb("bc", [DSTATE, GT], F32, inner)
                    t.pad = pool.mark(nc.gpsimd.memset(t.xb[:, :, :, 0:3], 0.0))
                    m = act.mark(nc.scalar.activation(t.xg[:, :, :], x_all[:, bass.ds(rnd * RS + GS * t.n, GS), :], ACT.Copy))
                    ready[t.n] = yield from gated_block(t, m, first)

                alternate((block(t) for t in threads), LAG_GATED, [] if before is None else [routing(before)])
            for t in threads:
                t.last = [(lane, lane.count) for lane in (pe, dve, act)]
            with ExitStack() as inner:
                def cross(t):
                    t.for_attention(inner)
                    x = yield from cross_attention(t, ready[t.n], ct_in)
                    act.need(x)
                    act.mark(nc.scalar.activation(x_all[:, bass.ds(rnd * RS + GS * t.n, GS), :], t.xg[:, :, :], ACT.Copy))
                    if before is not None:
                        nc.vector.wait_ge(s_disp.sem, (before + 1) * (16 * 2 * RS))
                    _, xt_ok = yield from layernorm(c, t, con, x, out=t.rows)
                    b = t.banks[1]
                    r = by_token(c, b, gw, t.xt, (xt_ok,))
                    dve.need(r)
                    c.bank_read[b] = dve.mark(nc.vector.tensor_tensor(router.lg[:, t.seqs, :], c.ps[:, b, 0:GS * E0].rearrange("p (s e) -> p s e", e=E0),
                                                                      gb[:, None, :].to_broadcast([P, GS, E0]), ALU.add))

                alternate((cross(t) for t in threads), LAG_CROSS)
            c.new_epoch()

        a_round(0)
        with nc.Fori(0, NROUND - 1) as i:
            a_round(i + 1, before=i)
        alternate([routing(NROUND - 1)])
        pool.need((s_disp, NROUND * 16 * 2 * RS))
        c.new_epoch()


def v_constants(c, t):
    c.pool.mark(c.nc.gpsimd.memset(t.vv[:, :, :, HD + 1:32], 0.0))
    return c.pool.mark(c.nc.gpsimd.memset(t.vv[:, :, :, HD:HD + 1], 1.0))


def phase_b(c, con, dram, ring, s_ring, load_weights_c):
    nc, pe, dve, act, pool, sp = c.nc, c.pe, c.dve, c.act, c.pool, c.sp
    w1r, w2r = ring
    MF = F0 // P
    TAIL = CAP - P
    with ExitStack() as ctx:
        def sb(name, shape, dt=F32):
            return ctx.enter_context(nc.sbuf_tensor("b_" + name, shape, dt))

        b1 = sb("b1", [P, E0, MF])
        b2 = sb("b2", [P, E0, KD])
        b1l = sb("b1l", [P, NB, MF])
        b2l = sb("b2l", [P, NB, KD])
        xe = sb("xe", [P, NB, D])
        xe2 = sb("xe2", [TAIL, NB, D])
        xet = sb("xet", [P, 2, KD, CAP])
        ht = sb("ht", [P, 2, MF, CAP])
        yt = sb("yt", [P, 2, KD, CAP])
        ye = sb("ye", [P, 2, D])
        ye2 = sb("ye2", [TAIL, 2, D])
        s_x, s_y = c.stream("b_x", reset=False), [c.stream("b_y%d" % n, reset=False) for n in range(2)]
        xe_rows = dram["xe"].rearrange("(e r) d -> r e d", r=CAP)
        ye_rows = dram["ye"].rearrange("(e r) d -> r e d", r=CAP)

        def load_rows(first):
            s_x.mark(nc.sync.dma_start(xe[:, :, :], xe_rows[0:P, bass.ds(first, NB), :]))
            s_x.mark(nc.sync.dma_start(xe2[:, :, :], xe_rows[P:CAP, bass.ds(first, NB), :]))

        def experts(first, it, refill):
            nc.tensor.wait_ge(s_x.sem, (it + 1) * 32)
            b_in = act.mark(nc.scalar.activation(b1l[:, :, :], b1[:, bass.ds(first, NB), :], ACT.Copy))
            b_in = act.mark(nc.scalar.activation(b2l[:, :, :], b2[:, bass.ds(first, NB), :], ACT.Copy))
            act.need(b_in)
            dve.need(b_in)
            h_ok, down_ok, yt_ok, xt_read, xt_ok = [None] * NB, [None] * NB, [None] * NB, [None] * NB, [None] * NB
            turned = [None] * NB
            def turn_in(e):
                pe.need(c.bank_read[4])
                for k in range(KD):
                    nc.tensor.transpose(c.ps[:, 4, CAP * k:CAP * k + P], xe[:, e, k:D:KD], con["ident"])
                    t = nc.tensor.transpose(c.ps[:, 4, CAP * k + P:CAP * k + CAP], xe2[:, e, k:D:KD], con["ident"][0:TAIL, 0:TAIL])
                t = pe.mark(t)
                if e == NB - 1 and refill == NB:
                    sp.need(t)
                    load_rows(first + NB)
                dve.need(t, xt_read[e - 2] if e >= 2 else None)
                xt_ok[e] = dve.mark(nc.vector.tensor_copy(xet[:, e % 2, :, :], c.ps[:, 4, 0:KD * CAP].rearrange("p (k t) -> p k t", k=KD)))
                c.bank_read[4] = xt_ok[e]

            def up(e):
                slot = e % RING
                pe.need(xt_ok[e])
                nc.tensor.wait_ge(s_ring[slot].sem, it * (32 * NB // RING) + 32 * (e // RING + 1))
                act.need(down_ok[e - 2] if e >= 2 else None)
                for m in range(MF):
                    b = (m // 2) % 4
                    if m % 2 == 0:
                        pe.need(c.bank_read[b])
                    for k in range(KD):
                        ins = nc.tensor.matmul(c.ps[:, b, CAP * (m % 2):CAP * (m % 2) + CAP], w1r[:, slot, k, m:F0:MF],
                                               xet[:, e % 2, k, :], start=(k == 0), stop=(k == KD - 1), skip_group_check=True)
                    if m % 2 == 1:
                        r = pe.mark(ins)
                        act.need(r)
                        for q in (m - 1, m):
                            a = act.mark(nc.scalar.activation(ht[:, e % 2, q, :], c.ps[:, b, CAP * (q % 2):CAP * (q % 2) + CAP],
                                                              ACT.Gelu, bias=b1l[:, e, q:q + 1]))
                        c.bank_read[b] = a
                xt_read[e] = r
                h_ok[e] = a

            def down(e):
                slot = e % RING
                pe.need(h_ok[e], c.bank_read[5])
                for j in range(KD):
                    for m in range(MF):
                        ins = nc.tensor.matmul(c.ps[:, 5, CAP * j:CAP * j + CAP], w2r[:, slot, m, P * j:P * j + P],
                                               ht[:, e % 2, m, :], start=(m == 0), stop=(m == MF - 1), skip_group_check=True)
                down_ok[e] = pe.mark(ins)
                dve.need(down_ok[e], turned[e - 2] if e >= 2 else None)
                for j in range(KD):
                    a = dve.mark(nc.vector.tensor_scalar(yt[:, e % 2, j, :], c.ps[:, 5, CAP * j:CAP * j + CAP], b2l[:, e, j:j + 1], None, ALU.add))
                c.bank_read[5] = a
                yt_ok[e] = a
                if e < refill:
                    sp.need(down_ok[e])
                    load_expert(c, dram, ring, s_ring, slot, first + e + RING)

            def turn_out(e):
                pe.need(yt_ok[e], c.bank_read[6], c.bank_read[7])
                for j in range(KD):
                    nc.tensor.transpose(c.ps[:, 6, P * j:P * j + P], yt[:, e % 2, j, 0:P], con["ident"])
                    t = nc.tensor.transpose(c.ps[0:TAIL, 7, P * j:P * j + P], yt[:, e % 2, j, P:CAP], con["ident"])
                turned[e] = pe.mark(t)
                dve.need(turned[e])
                nc.vector.wait_ge(s_y[e % 2].sem, it * (32 * NB // 2) + 16 + 32 * (e // 2))
                a = dve.mark(nc.vector.tensor_copy(ye[:, e % 2, :], c.ps[:, 6, 0:D]))
                a2 = dve.mark(nc.vector.tensor_copy(ye2[:, e % 2, :], c.ps[0:TAIL, 7, 0:D]))
                c.bank_read[6], c.bank_read[7] = a, a2
                sp.need(a, a2)
                s_y[e % 2].mark(nc.sync.dma_start(ye_rows[0:P, bass.ds(first + e, 1), :], ye[:, e % 2:e % 2 + 1, :]))
                s_y[e % 2].mark(nc.sync.dma_start(ye_rows[P:CAP, bass.ds(first + e, 1), :], ye2[:, e % 2:e % 2 + 1, :]))

            turn_in(0)
            for e in range(NB + 2):
                if e < NB:
                    if e + 1 < NB:
                        turn_in(e + 1)
                    up(e)
                if 1 <= e <= NB:
                    down(e - 1)
                if e >= 2:
                    turn_out(e - 2)
            c.new_epoch()

        load_rows(0)
        act.need(s_y[0].mark(nc.scalar.dma_start(b1[:, :, :], dram["b1"])), s_y[1].mark(nc.scalar.dma_start(b2[:, :, :], dram["b2"])))
        c.new_epoch()
        with nc.Fori(0, E0 // NB - 1) as i:
            experts(i * NB, i, NB)
        weights_c = load_weights_c()
        experts(E0 - NB, E0 // NB - 1, NB - RING)
        for s in s_y:
            sp.need((s, 16 + 32 * E0 // 2))
        c.new_epoch()
    return weights_c


def load_expert(c, dram, ring, s_ring, slot, e):
    nc = c.nc
    s_ring[slot].mark(nc.sync.dma_start(ring[0][:, slot:slot + 1, :, :].rearrange("p e k f -> p e (k f)"),
                                        dram["w1"].rearrange("e (p k) f -> p e (k f)", p=P)[:, bass.ds(e, 1), :]))
    s_ring[slot].mark(nc.sync.dma_start(ring[1][:, slot:slot + 1, :, :].rearrange("p e m d -> p e (m d)"),
                                        dram["w2"].rearrange("e (p m) d -> p e (m d)", p=P)[:, bass.ds(e, 1), :]))


class Gathers:

    def __init__(self, c, sb, persist, table, name):
        self.c, self.persist, self.table = c, persist, table
        self.idx = sb(name + "_gi", [P, RS, 2], U32)
        self.rows = sb(name + "_g", [P, RS, 2, D])
        self.stream = c.stream(name + "_gather", reset=False)

    def fetch(self, rnd, *free):
        c, nc = self.c, self.c.nc
        c.dve.need(*free)
        m = c.dve.mark(nc.vector.tensor_copy(self.idx[:, :, :], self.persist["gidx"][:, bass.ds(rnd * RS, RS), :]))
        c.pool.need(m, *free)
        for s in range(RS):
            for k in range(2):
                self.stream.mark(nc.gpsimd.indirect_dma_start(
                    out=self.rows[:, s, k, :], out_offset=None, in_=self.table,
                    in_offset=bass.IndirectOffsetOnAxis(ap=self.idx[:, s, k:k + 1], axis=0)))

    def wait(self, lane, rounds):
        lane.eng.wait_ge(self.stream.sem, rounds * (16 * 2 * RS))


def rms_rows(c, t, x, out, ready, free=None):
    nc, dve, act = c.nc, c.dve, c.act
    act.need(ready, free)
    for s in range(GS):
        m = act.mark(nc.scalar.activation(out[:, s, :], x[:, s, :], ACT.Square, accum_out=t.ss[:, s:s + 1]))
    yield
    dve.need(m)
    m = dve.mark(nc.vector.tensor_scalar(t.ve[:, :], t.ss[:, :], 1.0 / D, 1e-5, ALU.mult, ALU.add))
    m = yield from inverse_root(c, t, m)
    dve.need(m)
    for s in range(GS):
        m = dve.mark(nc.vector.tensor_scalar(out[:, s, :], x[:, s, :], t.rs[:, s:s + 1], None, ALU.mult))
    yield
    return m


class WeightsC:

    def __init__(self, c, dram, region):
        nc = c.nc
        wa = region.take(4, KD, D)
        wc = region.take(3, KD, D)
        wf = region.take(5, KD, D)
        wv, gw = region.take(KD, 4 * HD), region.take(KD, E1)
        cols = region.take(4, KD)
        rows = region.take(2, D)
        beta = region.take(3)
        load = c.stream("c_w", reset=False)
        for dst, src in ((wa, "wa"), (wc, "wc"), (wf, "wf"), (wv, "wv"), (gw, "gw1"), (cols, "cols")):
            load.mark(nc.scalar.dma_start(dst, dram[src]))
        load.mark(nc.scalar.dma_start(rows[:, 0, :], dram["bo"].partition_broadcast(P)))
        load.mark(nc.scalar.dma_start(rows[:, 1, :], dram["bv"].partition_broadcast(P)))
        for n in range(3):
            load.mark(nc.scalar.dma_start(beta[:, n:n + 1], dram["beta%d" % n].partition_broadcast(P)))
        self.dconst = region.take(DCONST[-1][1])
        self.loaded = load.mark(nc.scalar.dma_start(self.dconst, dram["dconst"]))
        self.tiles = (wa, wc, wf, wv, gw, cols, rows, beta)


def phase_c(c, con, dram, persist, weights, spare, load_ahead):
    nc, pe, dve, act, pool, sp = c.nc, c.pe, c.dve, c.act, c.pool, c.sp
    with ExitStack() as ctx:
        def sb(name, shape, dt=F32):
            return ctx.enter_context(nc.sbuf_tensor("c_" + name, shape, dt))

        wa, wc, wf, wv, gw, cols, rows, beta = weights.tiles
        coef = sb("coef", [P, 1])
        tiny = sb("tiny", [P, 1])
        ct = sb("ct", [P, KD, RT])
        phi = sb("phi", [P, RS, P])
        gwl = sb("gwl", [P, RS, 2])
        slot = sb("slot", [P, RS, 2], U32)
        router = Router(c, ctx, con, "c_", E1)
        total = persist["total"][:, :]
        gath = Gathers(c, sb, persist, dram["ye"], "c")
        threads = [Thread(n, nc, ctx, "c_") for n in range(NTH)]
        for t in threads:
            t.common()
            t.rows = t.sb("rows", [P, GS, D])
            t.for_attention(ctx, spare)
            t.m4, t.z4 = t.sb("m4", [P, GS]), t.sb("z4", [P, GS])

        gath.fetch(0)
        for lane in (pe, dve, act):
            lane.need(weights.loaded)
        a = dve.mark(nc.vector.tensor_tensor(coef[:, :], beta[:, 0:1], beta[:, 1:2], ALU.add))
        dve.need(a)
        dve.mark(nc.vector.tensor_tensor(coef[:, :], coef[:, :], beta[:, 2:3], ALU.subtract))
        dve.mark(nc.vector.memset(tiny[:, :], 1e-9))
        dve.mark(nc.vector.memset(total, 0.0))
        for t in threads:
            v_constants(c, t)
        c.new_epoch()
        x_all = persist["x"]
        s_ct, s_disp = c.stream("c_ct"), c.stream("c_disp", reset=False)

        def dispatch():
            for s in range(RS):
                for k in range(2):
                    s_disp.mark(nc.gpsimd.indirect_dma_start(
                        out=dram["xd"], out_offset=bass.IndirectOffsetOnAxis(ap=slot[:, s, k:k + 1], axis=0),
                        in_=threads[s // GS].rows[:, s % GS, :], in_offset=None))

        def values(t, w, x_ok, copy):
            b = t.banks[3]

            def make_v(s):
                r = c.products(b, [(0, [t.xt[:, k, P * s:P * s + P] for k in range(KD)], [w[:, k, :] for k in range(KD)])], x_ok)
                act.need(r)
                a = act.mark(copy(s, b))
                c.bank_read[b] = a
                return a
            return make_v

        def temperature():
            def exponents(u, sub):
                dd, ee, ll = u.d[:, :, :], u.ee[:, :, :], u.ll[:, :, :]
                wide = lambda x: x[:, :, None].to_broadcast([P, NU, P])
                act.need(sub)
                for n in range(NU):
                    a = act.mark(nc.scalar.activation(u.ee[:, n, :], u.d[:, n, :], ACT.Exp, accum_out=u.zz[:, n:n + 1]))
                yield
                dve.need(a)
                a = dve.mark(nc.vector.reciprocal(u.zz[:, :], u.zz[:, :]))
                yield
                pool.need(a)
                p_ok = pool.mark(nc.gpsimd.tensor_tensor(ee, ee, wide(u.zz), ALU.mult))
                yield
                act.need(p_ok)
                a = act.mark(nc.scalar.activation(ll, ee, ACT.Ln, bias=tiny[:, 0:1]))
                yield
                dve.need(a, p_ok)
                for n in range(NU):
                    a = dve.mark(nc.vector.scalar_tensor_tensor(out=u.ll[:, n, :], in0=u.ee[:, n, :], scalar=-1.0, in1=u.ll[:, n, :],
                                                                op0=ALU.mult, op1=ALU.mult, accum_out=u.en[:, n:n + 1]))
                en, po = u.en[:, :], u.po[:, :]
                dve.need(a)
                dve.mark(nc.vector.tensor_scalar(u.gt[:, :], en, 0.5, None, ALU.is_gt))
                a = dve.mark(nc.vector.tensor_scalar(po, en, POLY[0], None, ALU.mult))
                for q in POLY[1:4]:
                    dve.need(a)
                    a = dve.mark(nc.vector.scalar_tensor_tensor(out=po, in0=po, scalar=q, in1=en, op0=ALU.add, op1=ALU.mult))
                dve.need(a)
                a = dve.mark(nc.vector.tensor_scalar(po, po, POLY[4], 1.0, ALU.add, ALU.max))
                dve.need(a)
                a = dve.mark(nc.vector.scalar_tensor_tensor(out=po, in0=po, scalar=-1.0, in1=u.gt[:, :], op0=ALU.add, op1=ALU.mult))
                dve.need(a)
                a = dve.mark(nc.vector.tensor_scalar(po, po, 1.0, None, ALU.add))
                yield
                pool.need(a, sub)
                a = pool.mark(nc.gpsimd.tensor_tensor(dd, dd, wide(u.po), ALU.mult))
                yield
                return a
            return exponents

        def causal_attention(t, x_in):
            ba, bb, bc_, bd_ = t.banks
            _, xt_ok = yield from layernorm(c, t, con, x_in)
            r = by_channel(c, bb, wa[:, 0, :, :], t.xt, (xt_ok,))
            act.need(r)
            q_ok = act.mark(nc.scalar.activation(t.qt[:, :, :].rearrange("p c t -> p (c t)"), c.ps[:, bb, :], ACT.Copy, scale=HD ** -0.5))
            c.bank_read[bb] = q_ok
            yield
            r = by_channel(c, bc_, wa[:, 1, :, :], t.xt, (xt_ok,))
            k_ok = head_keys(c, t.kp, c.ps[:, bc_, :], con["par"], r)
            c.bank_read[bc_] = k_ok
            yield
            make_v = values(t, wa[:, 2, :, :], xt_ok, lambda v, b: nc.scalar.activation(
                t.vv[:, v, :, 0:HD], c.ps[:, b, 0:D].rearrange("p (h e) -> p h e", e=HD), ACT.Copy))
            done = yield from attention(c, t, con, make_v, (q_ok, k_ok), mask=con["mask"], temperature=temperature())
            xt_ok = yield from transpose_rows(c, t, con, t.ao, done)
            r = by_token(c, bb, wa[:, 3, :, :], t.xt, (xt_ok,))
            yield
            flat = t.xg[:, :, :].rearrange("p s d -> p (s d)")
            dve.need(r)
            a = dve.mark(nc.vector.tensor_tensor(flat, flat, c.ps[:, bb, :], ALU.add))
            c.bank_read[bb] = a
            dve.need(a)
            return dve.mark(nc.vector.tensor_tensor(t.xg[:, :, :], t.xg[:, :, :], rows[:, 0:1, :].to_broadcast([P, GS, D]), ALU.add))

        def cross_attention(t, x_in, ct_in):
            ba, bb, bc_, bd_ = t.banks
            ctt = ct[:, :, t.tok]
            norm = layernorm(c, t, con, x_in)
            next(norm)
            r = by_channel(c, bc_, wc[:, 1, :, :], ctt, (ct_in,))
            act.need(r)
            for ch in range(KD):
                k_ok = act.mark(nc.scalar.activation(t.kp[:, ch, 0, :], c.ps[:, bc_, GT * ch:GT * ch + GT], ACT.Identity, bias=cols[:, 1, ch:ch + 1]))
            c.bank_read[bc_] = k_ok
            r = by_token(c, bd_, wc[:, 2, :, :], ctt, (ct_in,))
            dve.need(r)
            v_ok = dve.mark(nc.vector.tensor_tensor(t.ao[:, :, :], c.ps[:, bd_, :].rearrange("p (s d) -> p s d", s=GS),
                                                    rows[:, 1:2, :].to_broadcast([P, GS, D]), ALU.add))
            c.bank_read[bd_] = v_ok
            _, xt_ok = yield from norm
            r = by_channel(c, bb, wc[:, 0, :, :], t.xt, (xt_ok,))
            yield
            dve.need(r)
            for ch in range(KD):
                q_ok = dve.mark(nc.vector.tensor_scalar(t.qt[:, ch, :], c.ps[:, bb, GT * ch:GT * ch + GT], cols[:, 0, ch:ch + 1], D ** -0.5, ALU.add, ALU.mult))
            c.bank_read[bb] = q_ok
            r = c.products(ba, [(P * s, [t.qt[:, ch, P * s:P * s + P] for ch in range(KD)], [t.kp[:, ch, 0, P * s:P * s + P] for ch in range(KD)])
                                for s in range(GS)], q_ok, k_ok)
            yield
            dd = t.units[0].d[:, 0:GS, :]
            dve.need(r)
            a = dve.mark(nc.vector.scalar_tensor_tensor(out=dd, in0=phi[:, t.seqs, :], scalar=coef[:, 0:1],
                                                        in1=c.ps[:, ba, 0:GT].rearrange("p (s t) -> p s t", s=GS), op0=ALU.mult, op1=ALU.add))
            c.bank_read[ba] = a
            dve.need(a)
            a = dve.mark(nc.vector.tensor_reduce(t.m4[:, :], dd, AX, ALU.max))
            dve.need(a)
            a = dve.mark(nc.vector.tensor_tensor(dd, dd, t.m4[:, :, None].to_broadcast([P, GS, P]), ALU.subtract))
            act.need(a)
            e = act.mark(nc.scalar.activation(dd, dd, ACT.Exp))
            yield
            dve.need(e)
            z = dve.mark(nc.vector.tensor_reduce(t.z4[:, :], dd, AX, ALU.add))
            r = c.transposes(ba, [(P * s, t.units[0].d[:, s, :]) for s in range(GS)], con["ident"], e)
            act.need(r)
            p_ok = act.mark(nc.scalar.activation(t.units[0].pt[:, 0:GS, :].rearrange("p h k -> p (h k)"), c.ps[:, ba, 0:GT], ACT.Copy))
            c.bank_read[ba] = p_ok
            dve.need(z)
            z = dve.mark(nc.vector.reciprocal(t.z4[:, :], t.z4[:, :]))
            yield
            r = c.products(bc_, [(D * s, [t.units[0].pt[:, s, :]], [t.ao[:, s, :]]) for s in range(GS)], p_ok, v_ok)
            dve.need(r, z)
            for s in range(GS):
                a = dve.mark(nc.vector.scalar_tensor_tensor(out=t.xg[:, s, :], in0=c.ps[:, bc_, D * s:D * s + D], scalar=t.z4[:, s:s + 1],
                                                            in1=t.xg[:, s, :], op0=ALU.mult, op1=ALU.add))
            c.bank_read[bc_] = a
            yield
            return a

        def rotary_attention(t, x_in):
            ba, bb, bc_, bd_ = t.banks
            u_ok, _ = yield from layernorm(c, t, con, x_in, want_t=False)
            h_ok = yield from rms_rows(c, t, t.xn, t.ao, u_ok, (pe, pe.count))
            xt_ok = yield from transpose_rows(c, t, con, t.ao, h_ok, scale=cols[:, 2, :])
            keys = t.units[0].ee[:, 0:2 * GS, :]
            for what, dst in ((0, t.qt[:, :, :].rearrange("p c (s l) -> p (c s) l", l=P)), (1, keys)):
                r0 = by_channel(c, bb, wf[:, 2 * what, :, :], t.xt, (xt_ok,))
                r1 = by_channel(c, bc_, wf[:, 2 * what + 1, :, :], t.xt, (xt_ok,))
                yield
                tmp = t.units[0].ll[:, 0:2 * GS, :]
                rope = lambda n: con["rope"][:, n:n + 1, :].to_broadcast([P, 2 * GS, P])
                bank = lambda b: c.ps[:, b, :].rearrange("p (n l) -> p n l", l=P)
                dve.need(r0)
                a = dve.mark(nc.vector.tensor_tensor(dst, bank(bb), rope(2 * what), ALU.mult))
                c.bank_read[bb] = a
                dve.need(r1)
                a = dve.mark(nc.vector.tensor_tensor(tmp, bank(bc_), rope(2 * what + 1), ALU.mult))
                c.bank_read[bc_] = a
                dve.need(a)
                ok = dve.mark(nc.vector.tensor_tensor(dst, dst, tmp, ALU.add))
                dve.need(ok)
                if what == 0:
                    q_ok = ok
            k_ok = head_keys(c, t.kp, t.units[0].ee[:, 0:2 * GS, :].rearrange("p n l -> p (n l)"), con["par"], ok)
            yield
            make_v = values(t, wv, xt_ok, lambda v, b: nc.scalar.activation(
                t.vv[:, v, :, 0:HD].rearrange("p (g r) e -> p g r e", r=4),
                c.ps[:, b, 0:4 * HD].rearrange("p (g e) -> p g e", e=HD)[:, :, None, :].to_broadcast([P, 4, 4, HD]), ACT.Copy))
            done = yield from attention(c, t, con, make_v, (q_ok, k_ok), mask=con["mask"])
            xt_ok = yield from transpose_rows(c, t, con, t.ao, done)
            r = by_token(c, bb, wf[:, 4, :, :], t.xt, (xt_ok,))
            yield
            flat = t.xn[:, :, :].rearrange("p s d -> p (s d)")
            dve.need(r)
            a = dve.mark(nc.vector.tensor_tensor(flat, flat, c.ps[:, bb, :], ALU.add))
            c.bank_read[bb] = a
            return a

        def routing(rnd):
            pos, w = yield from router.run(total)
            dve.need(pos, w)
            a = dve.mark(nc.vector.scalar_tensor_tensor(out=slot[:, :, :], in0=router.idx[:, :, :], scalar=float(R1), in1=router.pos[:, :, :], op0=ALU.mult, op1=ALU.add))
            pool.need(a)
            dispatch()
            for name, part in (("choice", router.idx), ("place", router.pos), ("gwt", router.w)):
                dve.mark(nc.vector.tensor_copy(persist[name][:, bass.ds(rnd * RS, RS), :], part[:, :, :]))

        def c_round(rnd, before=None):
            nc.scalar.preload_act_table_set(LN_EXP)
            ct_in = s_ct.mark(nc.sync.dma_start(ct[:, :, :], dram["ctx_t"][:, :, bass.ds(rnd * RT, RT)]))
            ct_in = s_ct.mark(nc.sync.dma_start(phi[:, :, :], dram["phi"][:, bass.ds(rnd * RS, RS), :]))
            if before is None:
                sp.need((gath.stream, 16 * 2 * RS))
                load_ahead()
            gw_in = act.mark(nc.scalar.activation(gwl[:, :, :], persist["gwt"][:, bass.ds(rnd * RS, RS), :], ACT.Copy))
            gath.wait(dve, rnd + 1)
            read = [None] * NTH

            def layer(t):
                a = act.mark(nc.scalar.activation(t.xg[:, :, :], x_all[:, bass.ds(rnd * RS + GS * t.n, GS), :], ACT.Copy))
                dve.need(gw_in, a)
                for k in range(2):
                    for s in range(GS):
                        a = dve.mark(nc.vector.scalar_tensor_tensor(out=t.xg[:, s, :], in0=gath.rows[:, GS * t.n + s, k, :], scalar=gwl[:, GS * t.n + s, k:k + 1],
                                                                    in1=t.xg[:, s, :], op0=ALU.mult, op1=ALU.add))
                    dve.need(a)
                read[t.n] = a
                x = yield from causal_attention(t, a)
                x = yield from cross_attention(t, x, ct_in)
                u = yield from rotary_attention(t, x)
                dve.need(u)
                x = dve.mark(nc.vector.tensor_tensor(t.xg[:, :, :], t.xg[:, :, :], t.xn[:, :, :], ALU.add))
                act.need(x)
                act.mark(nc.scalar.activation(x_all[:, bass.ds(rnd * RS + GS * t.n, GS), :], t.xg[:, :, :], ACT.Copy))
                if before is not None:
                    nc.vector.wait_ge(s_disp.sem, (before + 1) * (16 * 2 * RS))
                    act.need(dve.mark(nc.vector.tensor_copy(t.mv[:, 0, 0:1], t.mv[:, 0, 0:1])))
                h_ok = yield from rms_rows(c, t, t.xn, t.rows, u, (pe, pe.count))
                xt_ok = yield from transpose_rows(c, t, con, t.rows, h_ok, scale=cols[:, 3, :])
                b = t.banks[1]
                r = by_token(c, b, gw, t.xt, (xt_ok,))
                dve.need(r)
                c.bank_read[b] = dve.mark(nc.vector.tensor_copy(router.lg[:, t.seqs, :], c.ps[:, b, 0:GS * E1].rearrange("p (s e) -> p s e", e=E1)))

            def between():
                if before is not None:
                    yield from routing(before)
                while None in read:
                    yield
                gath.fetch(rnd + 1, *read)

            alternate((layer(t) for t in threads), LAG_C, [between()])
            c.new_epoch()

        c_round(0)
        with nc.Fori(0, NROUND - 1) as i:
            c_round(i + 1, before=i)
        alternate([routing(NROUND - 1)])
        pool.need((s_disp, NROUND * 16 * 2 * RS))
        gath.wait(dve, NROUND + 1)
        c.new_epoch()


def phase_d(c, con, dram, persist, weights, w13, w_ready, out):
    nc, pe, dve, act, pool, sp = c.nc, c.pe, c.dve, c.act, c.pool, c.sp
    MF = F1 // P
    with ExitStack() as ctx:
        def sb(name, shape, dt=F32):
            return ctx.enter_context(nc.sbuf_tensor("d_" + name, shape, dt))

        w2 = sb("w2", [P, E1 * F1 // P, D])
        dconst, cols = weights.dconst, weights.tiles[5]
        cnt = sb("cnt", [P, E1])
        tail = sb("tail", [P, E1], U32)
        cmp = sb("cmp", [P, NT1, 16])
        til = sb("til", [P, E1])
        end = sb("end", [P, E1])
        ej = sb("ej", [P, NT1])
        sj = sb("sj", [P, NT1])
        look = sb("look", [P, 2 * NSEQ, E1])
        base = sb("base", [P, 2 * NSEQ])
        row = sb("row", [P, NT1 + ND], I32)
        wex = sb("wex", [P, NT1], I32)
        xd = sb("xd", [P, ND, D])
        xt = sb("xt", [P, 2, KD, P])
        gs = sb("gs", [P, 2, F1])
        g = sb("g", [P, 2, F1])
        gt = sb("gt", [P, 2, MF, P])
        yd = sb("yd", [P, 2, D])
        k_tail, k_tile, k_upto, k_j, k_jrow = (dconst[:, a:b] for a, b in DCONST)
        s_x = [c.stream("d_x%d" % n, reset=False) for n in range(2)]
        s_y = [c.stream("d_y%d" % n, reset=False) for n in range(2)]
        half = E1 * F1 // P // 2
        w2_in = [s_y[n].mark(nc.sync.dma_start(w2[:, half * n:half * n + half, :], dram["w2d"][:, half * n:half * n + half, :])) for n in range(2)]
        pe.need(c.bank_read[0])
        r = pe.mark(nc.tensor.matmul(c.ps[:, 0, 0:E1], con["ones_bf"], persist["total"][:, :], start=True, stop=True))
        dve.need(r)
        a = dve.mark(nc.vector.tensor_copy(cnt[:, :], c.ps[:, 0, 0:E1]))
        dve.need(a)
        tl = dve.mark(nc.vector.tensor_tensor(tail[:, :], cnt[:, :], k_tail, ALU.add))
        pool.need(tl)
        s_tail = c.stream("d_tail", reset=False)
        for e in range(E1):
            t_in = s_tail.mark(nc.gpsimd.indirect_dma_start(
                out=dram["xd"], out_offset=bass.IndirectOffsetOnAxis(ap=tail[:, e:e + 1], axis=0),
                in_=con["zero"][:, 0:D], in_offset=None))
        pool.need(t_in)
        cv = cmp[:, 0:E1, :]
        a = dve.mark(nc.vector.tensor_tensor(cv, cnt[:, :, None].to_broadcast([P, E1, 16]), k_tile[:, None, :].to_broadcast([P, E1, 16]), ALU.is_gt))
        dve.need(a)
        a = dve.mark(nc.vector.tensor_reduce(til[:, :], cv, AX, ALU.add))
        dve.need(a)
        cv = cmp[:, 0:E1, 0:E1]
        a = dve.mark(nc.vector.tensor_tensor(cv, til[:, None, :].to_broadcast([P, E1, E1]), k_upto.rearrange("p (a b) -> p a b", a=E1), ALU.mult))
        dve.need(a)
        a = dve.mark(nc.vector.tensor_reduce(end[:, :], cv, AX, ALU.add))
        dve.need(a)
        flat = lambda t: t[:, :, :].rearrange("p s k -> p (s k)")
        dve.need(a)
        a = dve.mark(nc.vector.tensor_tensor(look[:, :, :], flat(persist["choice"])[:, :, None].to_broadcast([P, 2 * NSEQ, E1]),
                                             con["iota"][:, None, 0:E1].to_broadcast([P, 2 * NSEQ, E1]), ALU.is_equal))
        a = dve.mark(nc.vector.tensor_tensor(ej[:, 0:E1], end[:, :], til[:, :], ALU.subtract))
        dve.need(a)
        a = dve.mark(nc.vector.tensor_tensor(look[:, :, :], look[:, :, :], ej[:, None, 0:E1].to_broadcast([P, 2 * NSEQ, E1]), ALU.mult))
        dve.need(a)
        a = dve.mark(nc.vector.tensor_reduce(base[:, :], look[:, :, :], AX, ALU.add))
        dve.need(a)
        a = dve.mark(nc.vector.scalar_tensor_tensor(out=flat(persist["gidx"])[:, 0:2 * NSEQ], in0=base[:, :], scalar=float(P),
                                                    in1=flat(persist["place"]), op0=ALU.mult, op1=ALU.add))
        cv = cmp[:, :, 0:E1]
        a = dve.mark(nc.vector.tensor_tensor(cv, end[:, None, :].to_broadcast([P, NT1, E1]), k_j[:, :, None].to_broadcast([P, NT1, E1]), ALU.is_le))
        dve.need(a)
        a = dve.mark(nc.vector.tensor_reduce(ej[:, :], cv, AX, ALU.add))
        a = dve.mark(nc.vector.tensor_tensor(cv, cv, til[:, None, :].to_broadcast([P, NT1, E1]), ALU.mult))
        dve.need(a)
        a = dve.mark(nc.vector.tensor_reduce(sj[:, :], cv, AX, ALU.add))
        dve.need(a)
        a = dve.mark(nc.vector.scalar_tensor_tensor(out=sj[:, :], in0=sj[:, :], scalar=-float(P), in1=k_jrow, op0=ALU.mult, op1=ALU.add))
        dve.need(a)
        dve.mark(nc.vector.memset(row[:, NT1:], 0))
        row_ok = dve.mark(nc.vector.scalar_tensor_tensor(out=row[:, 0:NT1], in0=ej[:, :], scalar=float(R1), in1=sj[:, :], op0=ALU.mult, op1=ALU.add))
        a = dve.mark(nc.vector.tensor_scalar(wex[:, :], ej[:, :], float(E1 - 1), None, ALU.min))
        def load_tile(j, n):
            at = sp.eng.value_load(row[0:1, bass.ds(j, 1)], min_val=0, max_val=E1 * R1 + 7 * P)
            s_x[n >= 2].mark(nc.sync.dma_start(xd[:, n, :], dram["xd"][bass.ds(at, P), :]))

        sp.need(row_ok, t_in)
        pe.need(w_ready, *w2_in)
        c.new_epoch()
        for n in range(ND):
            load_tile(n, n)

        with nc.Fori(0, NT1 // ND) as i:
            nc.tensor.wait_ge(s_x[0].sem, (i + 1) * (16 * 2))
            xt_ok, up_ok, gs_ok, g_ok, gt_ok, dn_ok, gt_tr = ([None] * ND for _ in range(7))

            def turn_in(n):
                b = 6
                pe.need(c.bank_read[b])
                for k in range(KD):
                    t = nc.tensor.transpose(c.ps[:, b, P * k:P * k + P], xd[:, n, P * k:P * k + P], con["ident"])
                t = pe.mark(t)
                sp.need(t)
                load_tile((i + 1) * ND + n, n)
                act.need(t, up_ok[n - 2] if n >= 2 else None)
                for k in range(KD):
                    a = act.mark(nc.scalar.activation(xt[:, n % 2, k, :], c.ps[:, b, P * k:P * k + P], ACT.Copy, scale=cols[:, 3, k:k + 1]))
                c.bank_read[b] = a
                xt_ok[n] = a

            def expert(n):
                return pe.eng.value_load(wex[0:1, bass.ds(i * ND + n, 1)], min_val=0, max_val=E1 - 1)

            def up(n, e, halves=range(2)):
                for half in halves:
                    b = 2 * (n % 2) + half
                    pe.need(xt_ok[n], c.bank_read[b])
                    for k in range(KD):
                        ins = nc.tensor.matmul(c.ps[:, b, :], xt[:, n % 2, k, :], w13[:, bass.ds(e * (2 * KD) + 2 * k + half, 1), :],
                                               start=(k == 0), stop=(k == KD - 1))
                    r = pe.mark(ins)
                    if half == 0:
                        act.need(r)
                        gs_ok[n] = act.mark(nc.scalar.activation(gs[:, n % 2, :], c.ps[:, b, :], ACT.Silu))
                        c.bank_read[b] = gs_ok[n]
                    else:
                        dve.need(r, gs_ok[n], gt_tr[n - 2] if n >= 2 else None)
                        g_ok[n] = dve.mark(nc.vector.tensor_tensor(g[:, n % 2, :], gs[:, n % 2, :], c.ps[:, b, :], ALU.mult))
                        c.bank_read[b] = g_ok[n]
                up_ok[n] = r

            def turn_hidden(n):
                t = c.transposes(4, [(P * m, g[:, n % 2, P * m:P * m + P]) for m in range(MF)], con["ident"], g_ok[n])
                gt_tr[n] = t
                dve.need(t, dn_ok[n - 2] if n >= 2 else None)
                gt_ok[n] = dve.mark(nc.vector.tensor_copy(gt[:, n % 2, :, :].rearrange("p m t -> p (m t)"), c.ps[:, 4, :]))
                c.bank_read[4] = gt_ok[n]

            def down(n, e):
                pe.need(gt_ok[n], c.bank_read[5])
                for m in range(MF):
                    ins = nc.tensor.matmul(c.ps[:, 5, 0:D], gt[:, n % 2, m, :], w2[:, bass.ds(e * MF + m, 1), :], start=(m == 0), stop=(m == MF - 1))
                dn_ok[n] = pe.mark(ins)
                dve.need(dn_ok[n])
                nc.vector.wait_ge(s_y[n % 2].sem, i * (16 * ND // 2) + 16 + 16 * (n // 2))
                a = dve.mark(nc.vector.tensor_copy(yd[:, n % 2, :], c.ps[:, 5, 0:D]))
                c.bank_read[5] = a
                sp.need(a)
                s_y[n % 2].mark(nc.sync.dma_start(dram["yd"][bass.ds((i * ND + n) * P, P), :], yd[:, n % 2, :]))

            es = [None] * ND
            turn_in(0)
            es[0] = expert(0)
            up(0, es[0])
            turn_in(1)
            nc.tensor.wait_ge(s_x[1].sem, (i + 1) * (16 * (ND - 2)))
            for n in range(ND):
                if n + 1 < ND:
                    es[n + 1] = expert(n + 1)
                    up(n + 1, es[n + 1], (0,))
                turn_hidden(n)
                if n + 1 < ND:
                    up(n + 1, es[n + 1], (1,))
                if n + 2 < ND:
                    turn_in(n + 2)
                down(n, es[n])
            c.new_epoch()

        rows = w2
        x_all = persist["x"]
        s_g, s_o = [c.stream("d_gather%d" % n) for n in range(NSEQ // 2)], c.stream("out")
        pool.need(*[(s, 16 + 16 * NT1 // 2) for s in s_y])
        for j in range(2 * NSEQ):
            m = s_g[j // 4].mark(nc.gpsimd.indirect_dma_start(out=rows[:, j, :], out_offset=None, in_=dram["yd"],
                                                      in_offset=bass.IndirectOffsetOnAxis(ap=persist["gidx"][:, j // 2, j % 2:j % 2 + 1], axis=0)))
            if j % 4 == 3:
                s = j // 2 - 1
                dve.need(m)
                for k in range(2):
                    for q in (s, s + 1):
                        a = dve.mark(nc.vector.scalar_tensor_tensor(out=x_all[:, q, :], in0=rows[:, 2 * q + k, :], scalar=persist["gwt"][:, q, k:k + 1],
                                                                    in1=x_all[:, q, :], op0=ALU.mult, op1=ALU.add))
                    dve.need(a)
                sp.need(a)
                s_o.mark(nc.sync.dma_start(out.rearrange("s l d -> l s d")[:, s:s + 2, :], x_all[:, s:s + 2, :]))
        sp.need((s_o, s_o.count))
        sp.need((s_x[0], (NT1 // ND + 1) * 16 * 2), (s_x[1], (NT1 // ND + 1) * 16 * (ND - 2)))
        c.new_epoch()


def build(nc, dram, out):
    for name, n in (("xe", E0 * CAP), ("ye", E0 * CAP), ("xd", E1 * R1 + E1 * P), ("yd", NT1 * P)):
        dram[name] = nc.dram_tensor(name, (n, D), F32, kind="Internal").ap()
    with ExitStack() as ctx:
        c = Core(nc, ctx)
        dve, pool, pe, act = c.dve, c.pool, c.pe, c.act

        def sb(name, shape, dt=F32):
            return ctx.enter_context(nc.sbuf_tensor(name, shape, dt))

        cf = sb("cf", [P, dram["cf"].shape[1]])
        cb = sb("cb", [P, dram["cb"].shape[1]], BF16)
        persist = {"x": sb("x_all", [P, NSEQ, D]), "gidx": sb("gidx_all", [P, NSEQ + RS, 2], U32),
                   "gwt": sb("gwt_all", [P, NSEQ, 2]), "total": sb("total1", [P, E1], BF16), "choice": sb("choice", [P, NSEQ, 2]),
                   "place": sb("place", [P, NSEQ, 2])}
        con = {"ident": cf[:, 0:128], "par": cf[:, 128:132], "iota": cf[:, 132:164],
               "ones": cf[:, 164:292], "rope": cf[:, 292:804].rearrange("p (n l) -> p n l", l=P), "ident_bf": cb[:, 0:128], "mask": cb[:, 128:640],
               "before_bf": cb[:, 640:768], "ones_bf": cb[:, 768:896]}
        zero = sb("zero", [P, D])
        s_in, s_xin = c.stream("in", reset=False), c.stream("x_in", reset=False)
        with nc.sbuf_tensor("cb_f32", list(dram["cb"].shape), F32) as cb_f32:
            s_in.mark(nc.sync.dma_start(cf[:, :], dram["cf"]))
            m = s_in.mark(nc.sync.dma_start(cb_f32[:, :], dram["cb"]))
            dve.need(m)
            c.sp.need(dve.mark(nc.vector.tensor_copy(cb[:, :], cb_f32[:, :])))
        for lane in (pe, act):
            lane.need(m)
        x_in = s_xin.mark(nc.scalar.dma_start(persist["x"][:, :, :], dram["x"]))
        zm = dve.mark(nc.vector.memset(zero[:, :], 0.0))
        s_zero = c.stream("zero", reset=False)
        zp = max(n for n in range(1, P + 1) if E0 * CAP % n == 0)
        xd_tail = dram["xd"][E1 * R1:, :].rearrange("(p r) d -> p (r d)", p=P)

        def write_zeros():
            s_zero.mark(nc.sync.dma_start(dram["xe"].rearrange("(p n) d -> p n d", p=zp),
                                          zero[0:zp, None, :].to_broadcast([zp, E0 * CAP // zp, D])))
            s_zero.mark(nc.sync.dma_start(xd_tail.rearrange("p (n e) -> p n e", e=D), zero[:, None, :].to_broadcast([P, E1, D])))

        c.sp.need(zm)
        con["zero"] = zero
        dve.mark(nc.vector.memset(persist["gidx"][:, NSEQ:, :], 0))
        region = sb("weights", [P, REGION])
        with ExitStack() as stack:
            ring = (stack.enter_context(nc.sbuf_tensor("ring1", [P, RING, KD, F0], F32)),
                    stack.enter_context(nc.sbuf_tensor("ring2", [P, RING, F0 // P, D], F32)))
            s_ring = [c.stream("ring%d" % n, reset=False) for n in range(RING)]
            phase_a(c, con, dram, persist, Region(region), x_in, s_zero,
                    lambda: [write_zeros()] + [load_expert(c, dram, ring, s_ring, n, n) for n in range(RING)])
            weights_c = phase_b(c, con, dram, ring, s_ring, lambda: WeightsC(c, dram, Region(region)))
        with ExitStack() as stack:
            w13 = stack.enter_context(nc.sbuf_tensor("w13", [P, E1 * KD * 2, F1], F32))
            s_w = c.stream("w_d", reset=False)
            split = 5 * KD * 2
            first_experts = lambda: s_w.mark(nc.sync.dma_start(w13[:, 0:split, :], dram["w13"][:, 0:split, :]))
            spare = iter([w13[:, r:r + 2, :].rearrange("p r (h k) -> p (r h) k", k=P) for r in range(split, E1 * KD * 2, 2)])
            phase_c(c, con, dram, persist, weights_c, spare, first_experts)
            w_ready = s_w.mark(nc.sync.dma_start(w13[:, split:, :], dram["w13"][:, split:, :]))
            phase_d(c, con, dram, persist, weights_c, w13, w_ready, out)


def constants():
    p = np.arange(P)
    par = np.stack([(p // HD) % 4 == j for j in range(4)], 1).astype(np.float32)
    cf = np.concatenate([np.eye(P), par, np.tile(np.arange(E0), (P, 1)), np.ones((P, P))], 1).astype(np.float32)
    freq = (1.0 / np.float32(10000.0) ** (np.arange(0, HD, 2, dtype=np.float32) / HD)).astype(np.float32)
    ang = (np.arange(P, dtype=np.float32)[:, None] * freq[None, :]).astype(np.float32)
    ang = np.tile(np.concatenate([ang, ang], 1).T, (P // HD, 1))
    sign = np.where(p % HD < HD // 2, -1.0, 1.0)[:, None]
    cos, sin = np.cos(ang), np.sin(ang) * sign
    cf = np.concatenate([cf, cos * HD ** -0.5, sin * HD ** -0.5, cos, sin], 1).astype(np.float32)
    e8, j = np.arange(E1), np.arange(NT1)
    dconst = np.concatenate([p[:, None] + R1 * e8[None, :]] + [np.tile(v.reshape(1, -1), (P, 1)) for v in (
        P * np.arange(16), e8[None, :] <= e8[:, None], j, P * j)], 1).astype(np.float32)
    causal = np.where(p[None, :] > p[:, None], NEG, 0.0)
    cb = np.concatenate([np.eye(P), np.tile(causal, (1, 4)), (p[:, None] < p[None, :]).astype(np.float32), np.ones((P, P))], 1).astype(np.float32)
    return {"cf": cf, "cb": cb, "dconst": dconst}


def layouts(x):
    def chunks(w):
        return np.ascontiguousarray(w.reshape(-1, P, w.shape[1]).transpose(1, 0, 2))

    a = {}
    a["x"] = np.ascontiguousarray(x["x"].transpose(1, 0, 2))
    a["ctx_t"] = chunks(x["ctx_1024"].reshape(NSEQ * P, D).T)
    a["win"] = chunks(x["L0_attn_W_in"].T)
    w = x["L0_attn_W_xproj"].T
    pad = np.zeros((DI, 16), w.dtype)
    a["wx"] = chunks(np.concatenate([w[:, :16], pad, w[:, 16:32], pad, w[:, 32:]], 1))
    a["wo"] = chunks(x["L0_attn_W_out"].T)
    a["conv"] = chunks(np.concatenate([x["L0_attn_conv_w"], x["L0_attn_conv_b"][:, None]], 1))
    a["dvec"] = np.ascontiguousarray(x["L0_attn_D"].reshape(KI, P).T)
    bd = np.zeros((P, 3, P), np.float32)
    for n, name in enumerate(("L0_xattn_Wq", "L0_xattn_Wk", "L0_xattn_Wv")):
        for h in range(P // HD):
            bd[HD * h:HD * h + HD, n, HD * h:HD * h + HD] = x[name].T
    a["bd"] = bd
    a["gw"] = chunks(x["L0_ffn_gate_w"])
    a["gb"] = x["L0_ffn_gate_b"]
    a["w1"], a["w2"] = x["L0_ffn_w1"], x["L0_ffn_w2"]
    a["b1"] = np.ascontiguousarray(x["L0_ffn_b1"].reshape(E0, P, F0 // P).transpose(1, 0, 2))
    a["b2"] = np.ascontiguousarray(x["L0_ffn_b2"].reshape(E0, KD, P).transpose(2, 0, 1))
    stack = lambda ws: np.ascontiguousarray(np.stack([chunks(w) for w in ws], 1))
    a["wa"] = stack([x["L1_attn_W" + n].T for n in "qkvo"])
    a["wc"] = stack([x["L1_xattn_W" + n].T for n in "qkv"])
    qkv = x["L1_ffn_wqkv"]
    swap = np.arange(D).reshape(-1, 2, HD // 2)[:, ::-1].reshape(-1)
    q = qkv[:D]
    kv = HD * (NH // 4)
    k = np.repeat(qkv[D:D + kv].reshape(4, HD, D), 4, axis=0).reshape(D, D)
    a["wf"] = stack([q.T, q[swap].T, k.T, k[swap].T, x["L1_ffn_wo"].T])
    a["wv"] = chunks(qkv[D + kv:].T)
    a["gw1"] = chunks(x["L1_ffn_gate_w"].T)
    col = lambda v: v.reshape(KD, P).T
    a["cols"] = np.ascontiguousarray(np.stack([col(x[n]) for n in ("L1_xattn_bq", "L1_xattn_bk", "L1_ffn_ln1_w", "L1_ffn_ln2_w")], 1))
    a["bo"], a["bv"] = x["L1_attn_bo"], x["L1_xattn_bv"]
    for n, name in enumerate(("risk", "prio", "impl")):
        a["beta%d" % n] = np.asarray(x["L1_xattn_beta_" + name]).reshape(1)
    a["phi"] = np.ascontiguousarray(x["fside_BxSxS2_0"].transpose(1, 0, 2))
    w13 = x["L1_ffn_w13"].reshape(E1, 2, F1, KD, P)
    a["w13"] = np.ascontiguousarray(w13.transpose(4, 0, 3, 1, 2).reshape(P, E1 * KD * 2, F1))
    w2 = x["L1_ffn_w2"].reshape(E1, D, F1 // P, P)
    a["w2d"] = np.ascontiguousarray(w2.transpose(3, 0, 2, 1).reshape(P, E1 * F1 // P, D))
    return a


def kernel(**inputs):
    import concourse.bacc as bacc
    from concourse.bass_utils import run_bass_kernel_spmd

    nc = bacc.Bacc("TRN2", target_bir_lowering=False, num_devices=1)
    arrays = {"in_" + k: v for k, v in {**layouts({k: np.asarray(v) for k, v in inputs.items()}), **constants()}.items()}
    dram = {k[3:]: nc.dram_tensor(k, v.shape, mybir.dt.from_np(v.dtype), kind="ExternalInput").ap() for k, v in arrays.items()}
    out = nc.dram_tensor("out_dram", (NSEQ, P, D), F32, kind="ExternalOutput").ap()
    build(nc, dram, out)
    r = run_bass_kernel_spmd(nc, [arrays], core_ids=[0])
    return r.results[0]["out_dram"]
```
